# Optimizing a Trainium2 kernel written in Bass

```python
import numpy as np
import jax
import jax.numpy as jnp

def _softmax(x, axis=-1):
    return jax.nn.softmax(x, axis=axis)

def _gelu(x):
    return jax.nn.gelu(x, approximate=True)

def _silu(x):
    return jax.nn.silu(x)

def _sigmoid(x):
    return jax.nn.sigmoid(x)

def _layernorm(x, axis=-1, eps=1e-05):
    m = jnp.mean(x, axis=axis, keepdims=True)
    v = jnp.var(x, axis=axis, keepdims=True)
    return (x - m) / jnp.sqrt(v + eps)

def _scatter_add(tgt, idx, src, axis=0):
    return tgt.at[idx].add(src)

def _segment_sum(src, seg, n):
    return jax.ops.segment_sum(src, seg, n)
kernel_name = 'mk_metaformer_d2_conv_nchw128_r4_430bcb'

def setup_inputs(seed: int=0):
    np.random.seed(seed)
    _w = jnp.asarray

    def _rec_inputs():
        import jax
        import jax.numpy as jnp
        _gk = jax.random.key(seed)
        x = -0.0002928 + 1 * jax.random.normal(jax.random.fold_in(_gk, 1), (8, 32, 16, 16), jnp.float32)
        return x
    x = _rec_inputs()

    def _L0_conv_setup():
        import jax, jax.numpy as jnp
        import numpy as np
        B, C, H, W = (8, 32, 16, 16)

        def _conv1x1(t, w, b):
            return jnp.einsum('bchw,oc->bohw', t, w) + b[None, :, None, None]
        key = jax.random.key(seed)
        ks = jax.random.split(key, 6)
        s = 1.0 / np.sqrt(C)
        return {'x': jax.random.normal(ks[0], (B, C, H, W), dtype=jnp.float32), 'freq_weights': jnp.ones((C,), dtype=jnp.float32), 'wq': jax.random.normal(ks[1], (C, C), dtype=jnp.float32) * s, 'bq': jnp.zeros((C,), dtype=jnp.float32), 'wk': jax.random.normal(ks[2], (C, C), dtype=jnp.float32) * s, 'bk': jnp.zeros((C,), dtype=jnp.float32), 'wv': jax.random.normal(ks[3], (C, C), dtype=jnp.float32) * s, 'bv': jnp.zeros((C,), dtype=jnp.float32), 'wo': jax.random.normal(ks[4], (C, C), dtype=jnp.float32) * s, 'bo': jnp.zeros((C,), dtype=jnp.float32)}
    _L0_conv_all = _L0_conv_setup()
    _L0_conv_in = {k: v for k, v in _L0_conv_all.items() if k in ('freq_weights', 'wq', 'bq', 'wk', 'bk', 'wv', 'bv', 'wo', 'bo')}
    del _L0_conv_all

    def _L0_ffn_setup():
        import jax, jax.numpy as jnp
        import numpy as np
        NB, NOPS = (33, 19)
        D, H = (32, 128)
        B, S = (8, 256)
        CARRY_OPS = [0, 1, 2, 10, 11, 12, 13]

        def _build_masks():
            am = np.zeros((NB, NOPS), dtype=bool)
            fm = np.zeros((NB, NOPS), dtype=bool)
            fm[0, :] = True
            for b in range(1, 8):
                am[b, CARRY_OPS] = True
                fm[b, CARRY_OPS] = True
            am[8, [14, 15, 8, 9]] = True
            fm[8, [14, 15, 8, 9]] = True
            for b in range(16, 32):
                fm[b, [3, 4]] = True
            am[32, [10, 11, 12, 13]] = True
            fm[32, [5, 6, 7, 2, 4, 10, 11, 12, 13]] = True
            return (jnp.asarray(am), jnp.asarray(fm))
        key = jax.random.key(seed)
        ks = jax.random.split(key, 9)
        sd = 1.0 / np.sqrt(D)
        sh = 1.0 / np.sqrt(H)
        am, fm = _build_masks()
        return {'x': jax.random.normal(ks[0], (B, S, D), jnp.float32), 'ffn_w1': jax.random.normal(ks[1], (NB, NOPS, D, H), jnp.float32) * sd, 'ffn_b1': jnp.zeros((NB, NOPS, H), jnp.float32), 'ffn_w2': jax.random.normal(ks[2], (NB, NOPS, H, D), jnp.float32) * sh, 'ffn_b2': jnp.zeros((NB, NOPS, D), jnp.float32), 'wq': jax.random.normal(ks[3], (NB, NOPS, D, D), jnp.float32) * sd, 'wk': jax.random.normal(ks[4], (NB, NOPS, D, D), jnp.float32) * sd, 'wv': jax.random.normal(ks[5], (NB, NOPS, D, D), jnp.float32) * sd, 'wo': jax.random.normal(ks[6], (NB, NOPS, D, D), jnp.float32) * sd, 'attn_mask': am, 'ffn_mask': fm}
    _L0_ffn_all = _L0_ffn_setup()
    _L0_ffn_in = {k: v for k, v in _L0_ffn_all.items() if k in ('ffn_w1', 'ffn_b1', 'ffn_w2', 'ffn_b2', 'wq', 'wk', 'wv', 'wo', 'attn_mask', 'ffn_mask')}
    del _L0_ffn_all

    def _L1_conv_setup():
        import jax, jax.numpy as jnp
        import numpy as np
        from jax import lax
        K = 3
        DG = 2
        PAD = K // 2
        EPS = 1e-05

        def _defconv(x, w_off, b_off, w, b, gamma, beta):
            B, C, H, W = x.shape
            C_out = w.shape[0]
            P = K * K
            Cg = C // DG
            xr = jax.nn.relu(x)
            om = lax.conv_general_dilated(xr, w_off, (1, 1), [(PAD, PAD), (PAD, PAD)], dimension_numbers=('NCHW', 'OIHW', 'NCHW')) + b_off[None, :, None, None]
            o1, o2, m = jnp.split(om, 3, axis=1)
            off_y = o1.reshape(B, DG, P, H, W)
            off_x = o2.reshape(B, DG, P, H, W)
            mask = jax.nn.sigmoid(m).reshape(B, DG, P, H, W)
            ki, kj = jnp.meshgrid(jnp.arange(K), jnp.arange(K), indexing='ij')
            ki = ki.reshape(P).astype(jnp.float32)
            kj = kj.reshape(P).astype(jnp.float32)
            base_y = jnp.arange(H, dtype=jnp.float32)[None, :, None] - PAD + ki[:, None, None]
            base_x = jnp.arange(W, dtype=jnp.float32)[None, None, :] - PAD + kj[:, None, None]
            ys = off_y + base_y[None, None]
            xs = off_x + base_x[None, None]
            y0 = jnp.floor(ys)
            x0 = jnp.floor(xs)
            wy = ys - y0
            wx = xs - x0
            y0i = y0.astype(jnp.int32)
            x0i = x0.astype(jnp.int32)
            xg = xr.reshape(B, DG, Cg, H * W)

            def gather(yi, xi):
                valid = (yi >= 0) & (yi < H) & (xi >= 0) & (xi < W)
                yc = jnp.clip(yi, 0, H - 1)
                xc = jnp.clip(xi, 0, W - 1)
                idx = (yc * W + xc).reshape(B, DG, 1, P * H * W)
                vals = jnp.take_along_axis(xg, jnp.broadcast_to(idx, (B, DG, Cg, P * H * W)), axis=3)
                vals = vals.reshape(B, DG, Cg, P, H, W)
                return vals * valid.astype(xr.dtype)[:, :, None]
            v00 = gather(y0i, x0i)
            v01 = gather(y0i, x0i + 1)
            v10 = gather(y0i + 1, x0i)
            v11 = gather(y0i + 1, x0i + 1)
            wy_ = wy[:, :, None]
            wx_ = wx[:, :, None]
            sampled = v00 * (1 - wy_) * (1 - wx_) + v01 * (1 - wy_) * wx_ + v10 * wy_ * (1 - wx_) + v11 * wy_ * wx_
            sampled = sampled * mask[:, :, None]
            wr = w.reshape(C_out, DG, Cg, P)
            out = jnp.einsum('bgcphw,ogcp->bohw', sampled, wr) + b[None, :, None, None]
            mu = out.mean(axis=(0, 2, 3), keepdims=True)
            var = out.var(axis=(0, 2, 3), keepdims=True)
            out = (out - mu) * lax.rsqrt(var + EPS)
            out = out * gamma[None, :, None, None] + beta[None, :, None, None]
            return out
        key = jax.random.key(seed)
        ks = jax.random.split(key, 8)
        B, C_in, C_out, H, W = (8, 32, 32, 56, 56)
        x = jax.random.normal(ks[0], (B, C_in, H, W), jnp.float32)
        och = 3 * DG * K * K
        w_off = jax.random.normal(ks[1], (och, C_in, K, K), jnp.float32) * 0.01
        b_off = jax.random.normal(ks[2], (och,), jnp.float32) * 0.01
        scale = 1.0 / np.sqrt(C_in * K * K)
        w = jax.random.normal(ks[3], (C_out, C_in, K, K), jnp.float32) * scale
        b = jax.random.normal(ks[4], (C_out,), jnp.float32) * scale
        gamma = jnp.ones((C_out,), jnp.float32)
        beta = jnp.zeros((C_out,), jnp.float32)
        return {'x': x, 'w_off': w_off, 'b_off': b_off, 'w': w, 'b': b, 'gamma': gamma, 'beta': beta}
    _L1_conv_all = _L1_conv_setup()
    _L1_conv_in = {k: v for k, v in _L1_conv_all.items() if k in ('w_off', 'b_off', 'w', 'b', 'gamma', 'beta')}
    del _L1_conv_all

    def _L1_ffn_setup():
        import jax, jax.numpy as jnp
        import numpy as np
        B, S, D, E, H, O, K = (128, 512, 32, 16, 128, 32, 8)
        key = jax.random.key(seed)
        k0, k1, k2, k3 = jax.random.split(key, 4)
        x = jax.random.normal(k0, (B, S, D), dtype=jnp.float32)
        gate_w = jax.random.normal(k1, (E, D), dtype=jnp.float32) * (1.0 / np.sqrt(D))
        gate_b = jnp.zeros((E,), dtype=jnp.float32)
        weight1 = jax.random.uniform(k2, (E, D + 1, H), dtype=jnp.float32, minval=-1.0, maxval=1.0) * (1.0 / np.sqrt(D + 1))
        weight2 = jax.random.uniform(k3, (E, H + 1, O), dtype=jnp.float32, minval=-1.0, maxval=1.0) * (1.0 / np.sqrt(H + 1))
        return {'x': x, 'gate_w': gate_w, 'gate_b': gate_b, 'weight1': weight1, 'weight2': weight2}
    _L1_ffn_all = _L1_ffn_setup()
    _L1_ffn_in = {k: v for k, v in _L1_ffn_all.items() if k in ('gate_w', 'gate_b', 'weight1', 'weight2')}
    del _L1_ffn_all
    return {'x': x, 'L0_conv_freq_weights': _L0_conv_in['freq_weights'], 'L0_conv_wq': _L0_conv_in['wq'], 'L0_conv_bq': _L0_conv_in['bq'], 'L0_conv_wk': _L0_conv_in['wk'], 'L0_conv_bk': _L0_conv_in['bk'], 'L0_conv_wv': _L0_conv_in['wv'], 'L0_conv_bv': _L0_conv_in['bv'], 'L0_conv_wo': _L0_conv_in['wo'], 'L0_conv_bo': _L0_conv_in['bo'], 'L0_ffn_ffn_w1': _L0_ffn_in['ffn_w1'], 'L0_ffn_ffn_b1': _L0_ffn_in['ffn_b1'], 'L0_ffn_ffn_w2': _L0_ffn_in['ffn_w2'], 'L0_ffn_ffn_b2': _L0_ffn_in['ffn_b2'], 'L0_ffn_wq': _L0_ffn_in['wq'], 'L0_ffn_wk': _L0_ffn_in['wk'], 'L0_ffn_wv': _L0_ffn_in['wv'], 'L0_ffn_wo': _L0_ffn_in['wo'], 'L0_ffn_attn_mask': _L0_ffn_in['attn_mask'], 'L0_ffn_ffn_mask': _L0_ffn_in['ffn_mask'], 'L1_conv_w_off': _L1_conv_in['w_off'], 'L1_conv_b_off': _L1_conv_in['b_off'], 'L1_conv_w': _L1_conv_in['w'], 'L1_conv_b': _L1_conv_in['b'], 'L1_conv_gamma': _L1_conv_in['gamma'], 'L1_conv_beta': _L1_conv_in['beta'], 'L1_ffn_gate_w': _L1_ffn_in['gate_w'], 'L1_ffn_gate_b': _L1_ffn_in['gate_b'], 'L1_ffn_weight1': _L1_ffn_in['weight1'], 'L1_ffn_weight2': _L1_ffn_in['weight2']}

def reference(x, L0_conv_freq_weights, L0_conv_wq, L0_conv_bq, L0_conv_wk, L0_conv_bk, L0_conv_wv, L0_conv_bv, L0_conv_wo, L0_conv_bo, L0_ffn_ffn_w1, L0_ffn_ffn_b1, L0_ffn_ffn_w2, L0_ffn_ffn_b2, L0_ffn_wq, L0_ffn_wk, L0_ffn_wv, L0_ffn_wo, L0_ffn_attn_mask, L0_ffn_ffn_mask, L1_conv_w_off, L1_conv_b_off, L1_conv_w, L1_conv_b, L1_conv_gamma, L1_conv_beta, L1_ffn_gate_w, L1_ffn_gate_b, L1_ffn_weight1, L1_ffn_weight2):
    import jax
    import jax.numpy as jnp

    def _L0_conv_ref(x, freq_weights, wq, bq, wk, bk, wv, bv, wo, bo):
        import jax, jax.numpy as jnp
        import numpy as np
        B, C, H, W = (8, 32, 16, 16)

        def _conv1x1(t, w, b):
            return jnp.einsum('bchw,oc->bohw', t, w) + b[None, :, None, None]
        b, c, h, w = x.shape
        n = h * w
        fd = jnp.fft.fft2(x, axes=(-2, -1))
        mag = jnp.abs(fd)
        freq_attn = mag * freq_weights[None, :, None, None]
        refined_freq = freq_attn * jnp.exp(1j * jnp.angle(fd))
        refined = jnp.fft.ifft2(refined_freq, axes=(-2, -1)).real.astype(x.dtype)
        q = _conv1x1(refined, wq, bq).reshape(b, c, n)
        k = _conv1x1(refined, wk, bk).reshape(b, c, n)
        v = _conv1x1(refined, wv, bv).reshape(b, c, n)
        scores = jnp.einsum('bcn,bcm->bnm', q, k) / jnp.sqrt(jnp.asarray(c, x.dtype))
        attn = jax.nn.softmax(scores, axis=-1)
        out = jnp.einsum('bnm,bcm->bcn', attn, v).reshape(b, c, h, w)
        return _conv1x1(out, wo, bo)

    def _L0_ffn_ref(x, ffn_w1, ffn_b1, ffn_w2, ffn_b2, wq, wk, wv, wo, attn_mask, ffn_mask):
        import jax, jax.numpy as jnp
        import numpy as np
        NB, NOPS = (33, 19)
        D, H = (32, 128)
        B, S = (8, 256)
        CARRY_OPS = [0, 1, 2, 10, 11, 12, 13]

        def _build_masks():
            am = np.zeros((NB, NOPS), dtype=bool)
            fm = np.zeros((NB, NOPS), dtype=bool)
            fm[0, :] = True
            for b in range(1, 8):
                am[b, CARRY_OPS] = True
                fm[b, CARRY_OPS] = True
            am[8, [14, 15, 8, 9]] = True
            fm[8, [14, 15, 8, 9]] = True
            for b in range(16, 32):
                fm[b, [3, 4]] = True
            am[32, [10, 11, 12, 13]] = True
            fm[32, [5, 6, 7, 2, 4, 10, 11, 12, 13]] = True
            return (jnp.asarray(am), jnp.asarray(fm))
        scale = jnp.asarray(1.0 / np.sqrt(D), x.dtype)

        def step(h, p):
            op = jnp.argmax(h[0, 0, :NOPS])
            q = h @ p['wq'][op]
            k = h @ p['wk'][op]
            v = h @ p['wv'][op]
            attn = jax.nn.softmax(jnp.einsum('bqd,bkd->bqk', q, k) * scale, axis=-1)
            y = jnp.einsum('bqk,bkd->bqd', attn, v) @ p['wo'][op]
            h = jnp.where(p['am'][op], y, h)
            z = jax.nn.relu(h @ p['w1'][op] + p['b1'][op]) @ p['w2'][op] + p['b2'][op]
            h = jnp.where(p['fm'][op], z, h)
            return (h, None)
        xs = {'w1': ffn_w1, 'b1': ffn_b1, 'w2': ffn_w2, 'b2': ffn_b2, 'wq': wq, 'wk': wk, 'wv': wv, 'wo': wo, 'am': attn_mask, 'fm': ffn_mask}
        out, _ = jax.lax.scan(step, x, xs)
        return out

    def _L1_conv_ref(x, w_off, b_off, w, b, gamma, beta):
        import jax, jax.numpy as jnp
        import numpy as np
        from jax import lax
        K = 3
        DG = 2
        PAD = K // 2
        EPS = 1e-05

        def _defconv(x, w_off, b_off, w, b, gamma, beta):
            B, C, H, W = x.shape
            C_out = w.shape[0]
            P = K * K
            Cg = C // DG
            xr = jax.nn.relu(x)
            om = lax.conv_general_dilated(xr, w_off, (1, 1), [(PAD, PAD), (PAD, PAD)], dimension_numbers=('NCHW', 'OIHW', 'NCHW')) + b_off[None, :, None, None]
            o1, o2, m = jnp.split(om, 3, axis=1)
            off_y = o1.reshape(B, DG, P, H, W)
            off_x = o2.reshape(B, DG, P, H, W)
            mask = jax.nn.sigmoid(m).reshape(B, DG, P, H, W)
            ki, kj = jnp.meshgrid(jnp.arange(K), jnp.arange(K), indexing='ij')
            ki = ki.reshape(P).astype(jnp.float32)
            kj = kj.reshape(P).astype(jnp.float32)
            base_y = jnp.arange(H, dtype=jnp.float32)[None, :, None] - PAD + ki[:, None, None]
            base_x = jnp.arange(W, dtype=jnp.float32)[None, None, :] - PAD + kj[:, None, None]
            ys = off_y + base_y[None, None]
            xs = off_x + base_x[None, None]
            y0 = jnp.floor(ys)
            x0 = jnp.floor(xs)
            wy = ys - y0
            wx = xs - x0
            y0i = y0.astype(jnp.int32)
            x0i = x0.astype(jnp.int32)
            xg = xr.reshape(B, DG, Cg, H * W)

            def gather(yi, xi):
                valid = (yi >= 0) & (yi < H) & (xi >= 0) & (xi < W)
                yc = jnp.clip(yi, 0, H - 1)
                xc = jnp.clip(xi, 0, W - 1)
                idx = (yc * W + xc).reshape(B, DG, 1, P * H * W)
                vals = jnp.take_along_axis(xg, jnp.broadcast_to(idx, (B, DG, Cg, P * H * W)), axis=3)
                vals = vals.reshape(B, DG, Cg, P, H, W)
                return vals * valid.astype(xr.dtype)[:, :, None]
            v00 = gather(y0i, x0i)
            v01 = gather(y0i, x0i + 1)
            v10 = gather(y0i + 1, x0i)
            v11 = gather(y0i + 1, x0i + 1)
            wy_ = wy[:, :, None]
            wx_ = wx[:, :, None]
            sampled = v00 * (1 - wy_) * (1 - wx_) + v01 * (1 - wy_) * wx_ + v10 * wy_ * (1 - wx_) + v11 * wy_ * wx_
            sampled = sampled * mask[:, :, None]
            wr = w.reshape(C_out, DG, Cg, P)
            out = jnp.einsum('bgcphw,ogcp->bohw', sampled, wr) + b[None, :, None, None]
            mu = out.mean(axis=(0, 2, 3), keepdims=True)
            var = out.var(axis=(0, 2, 3), keepdims=True)
            out = (out - mu) * lax.rsqrt(var + EPS)
            out = out * gamma[None, :, None, None] + beta[None, :, None, None]
            return out
        return _defconv(x, w_off, b_off, w, b, gamma, beta)

    def _L1_ffn_ref(x, gate_w, gate_b, weight1, weight2):
        import jax, jax.numpy as jnp
        import numpy as np
        B, S, D, E, H, O, K = (128, 512, 32, 16, 128, 32, 8)
        Bn, Sn, Dn = x.shape
        logits = jnp.einsum('bsd,ed->bse', x, gate_w) + gate_b
        probs = jax.nn.softmax(logits, axis=1)
        vals, idx = jax.lax.top_k(probs.transpose(0, 2, 1), K)
        topv = vals.transpose(0, 2, 1)
        topi = idx.transpose(0, 2, 1)
        flat_idx = topi.reshape(Bn, K * E)
        gathered = jnp.take_along_axis(x, flat_idx[:, :, None], axis=1)
        gathered = gathered.reshape(Bn, K, E, Dn)
        pooled = jnp.einsum('bked,bke->bed', gathered, topv)
        ones = jnp.ones((E, Bn, 1), dtype=x.dtype)
        h = jnp.concatenate([pooled.transpose(1, 0, 2), ones], axis=-1)
        h = jax.nn.gelu(jnp.einsum('ebd,edh->ebh', h, weight1), approximate=False)
        h = jnp.concatenate([h, ones], axis=-1)
        out = jnp.einsum('ebh,eho->ebo', h, weight2)
        out = out.transpose(1, 0, 2)
        weighted = jnp.einsum('beo,bke->bkeo', out, topv).reshape(Bn, K * E, O)
        outputs = jnp.zeros((Bn, Sn, O), dtype=x.dtype)
        outputs = outputs.at[jnp.arange(Bn)[:, None], flat_idx].add(weighted)
        return outputs

    def _gn(v, G=32, eps=1e-05):
        B_, C_, H_, W_ = v.shape
        g = v.reshape(B_, G, C_ // G, H_, W_)
        m = jnp.mean(g, axis=(2, 3, 4), keepdims=True)
        s = jnp.var(g, axis=(2, 3, 4), keepdims=True)
        return ((g - m) / jnp.sqrt(s + eps)).reshape(v.shape)

    def _ln_c(v, eps=1e-06):
        m = jnp.mean(v, axis=1, keepdims=True)
        s = jnp.var(v, axis=1, keepdims=True)
        return (v - m) / jnp.sqrt(s + eps)

    def _ln_t(v, eps=1e-05):
        m = jnp.mean(v, axis=-1, keepdims=True)
        s = jnp.var(v, axis=-1, keepdims=True)
        return (v - m) / jnp.sqrt(s + eps)

    def _to_tokens(v):
        B_, C_, H_, W_ = v.shape
        return v.reshape(B_, C_, H_ * W_).transpose(0, 2, 1)

    def _from_tokens(t, like):
        B_, C_, H_, W_ = like.shape
        return t.transpose(0, 2, 1).reshape(B_, C_, H_, W_)
    x = x + _L0_conv_ref(_ln_c(x), L0_conv_freq_weights, L0_conv_wq, L0_conv_bq, L0_conv_wk, L0_conv_bk, L0_conv_wv, L0_conv_bv, L0_conv_wo, L0_conv_bo)
    t = _to_tokens(x)
    t = t + _L0_ffn_ref(_ln_t(t), L0_ffn_ffn_w1, L0_ffn_ffn_b1, L0_ffn_ffn_w2, L0_ffn_ffn_b2, L0_ffn_wq, L0_ffn_wk, L0_ffn_wv, L0_ffn_wo, L0_ffn_attn_mask, L0_ffn_ffn_mask)
    x = _from_tokens(t, x)
    x = x + _L1_conv_ref(_ln_c(x), L1_conv_w_off, L1_conv_b_off, L1_conv_w, L1_conv_b, L1_conv_gamma, L1_conv_beta)
    t = _to_tokens(x)
    t = t + _L1_ffn_ref(_ln_t(t), L1_ffn_gate_w, L1_ffn_gate_b, L1_ffn_weight1, L1_ffn_weight2)
    x = _from_tokens(t, x)
    return x

_drawn_inputs = setup_inputs


def setup_inputs(seed=0):
    import zlib

    import numpy as np

    out = dict(_drawn_inputs(seed))
    spreads = {'L0_conv_freq_weights': (1.0, 0.2),
     'L0_conv_bq': (0.0, 0.1),
     'L0_conv_bk': (0.0, 0.8),
     'L0_conv_bv': (0.0, 0.1),
     'L0_conv_bo': (0.0, 0.1),
     'L0_ffn_ffn_b1': (0.0, 0.1),
     'L0_ffn_ffn_b2': (0.0, 0.1),
     'L1_conv_gamma': (1.0, 0.2),
     'L1_conv_beta': (0.0, 0.1),
     'L1_ffn_gate_b': (0.0, 0.8)}
    factors = {'L1_conv_b_off': 4.77,
     'L1_conv_b': 8.0,
     'L1_ffn_gate_w': 8.0,
     'L1_ffn_weight1': 8.0,
     'L1_ffn_weight2': 8.0}
    for name, (base, spread) in spreads.items():
        noise = np.random.default_rng([zlib.crc32(name.encode()), seed]).standard_normal(out[name].shape)
        drawn = base * np.exp(spread * noise) if base else spread * noise
        out[name] = jnp.asarray(drawn.astype(out[name].dtype))
    for name, factor in factors.items():
        out[name] = (out[name] * factor).astype(out[name].dtype)
    return out
```

```python
import concourse.bass as bass
from concourse import mybir
from contextlib import ExitStack
import numpy as np

B, C, H, W = 8, 32, 16, 16
N = H * W
P = 128
BP = P // C
J = B // BP
F = J * N
NH = N // P
STEPS, OPS = 33, 19
HID = 128
DG, K = 2, 3
TAPS = K * K
CG = C // DG
GK = DG * TAPS
OCH = 3 * GK
E, TOPK = 16, 8
QSCALE = float(C) ** -0.5
NONE = 4 * STEPS
TPAD = 32 * OPS
WROWS = 8
NWIN = 4
BLK = 64
XROWS = H + 4
K3 = 3

f32 = mybir.dt.float32
i32 = mybir.dt.int32
u32 = mybir.dt.uint32
ALU = mybir.AluOpType
ACT = mybir.ActivationFunctionType
AX = mybir.AxisListType


def constants():
    p = np.arange(P)
    cols = {}
    cols["ident"] = np.eye(P)
    cols["mean"] = (p[:, None] // C == p[None, :] // C) / C
    cols["fold"] = (p[:, None] % C == p[None, :] % C) / BP
    k = np.arange(TAPS)
    row, col = p // W, p % W
    by = (row % 4)[:, None] + 1 + (k // K)[None, :]
    bx = col[:, None] - 1 + (k % K)[None, :]
    cols["base"] = np.concatenate([by, by, bx, bx, np.zeros((P, GK))], 1)
    cols["grid"] = np.broadcast_to(np.arange(W), (P, W))
    lead = [[(4 * ((8 * h + row) // 4) - 2)[:, None] for _ in range(2)] for h in range(NH)]
    cols["wide"] = np.concatenate(
        [np.arange(WROWS)[None, :] + WROWS * w - lead[h][w] for h in range(NH) for w in range(2)], 1)
    be = np.arange(P) // E
    cols["own"] = np.concatenate([(be[:, None] == J * np.arange(BP)[None, :] + j) for j in range(J)], 1)
    cols["eps"] = np.broadcast_to(np.array([1e-6, 1e-5]), (P, 2))
    at, off = {}, 0
    for name, a in cols.items():
        at[name] = (off, off + a.shape[1])
        off += a.shape[1]
    return np.concatenate([np.asarray(a, np.float32) for a in cols.values()], 1), at


def step_codes():
    return (4 * np.repeat(np.arange(STEPS), OPS)[None, :] - NONE).astype(np.float32)


class Chain:

    def __init__(self, eng, sem):
        self.eng, self.sem, self.n = eng, sem, 0

    def __call__(self, ins):
        self.n += 1
        ins.then_inc(self.sem, 1)
        self.eng.wait_ge(self.sem, self.n)


def metaformer_kernel(nc, a, out, upto="all"):
    _, CA = constants()
    NCST = max(e for _, e in CA.values())
    ctx = ExitStack()

    def sb(name, shape, dt=f32):
        return ctx.enter_context(nc.sbuf_tensor(name, shape, dt))

    sems = {}

    def sem(name):
        if name not in sems:
            sems[name] = ctx.enter_context(nc.semaphore(name))
        return sems[name]

    with ctx:
        cst = sb("cst", [P, NCST])

        def const(name):
            return cst[:, CA[name][0]:CA[name][1]]

        ident, meanm, fold = const("ident"), const("mean"), const("fold")
        eps6, eps5 = cst[:, CA["eps"][0]:CA["eps"][0] + 1], cst[:, CA["eps"][0] + 1:CA["eps"][1]]
        x = sb("x", [P, F])
        u = sb("u", [P, F])
        xc = sb("xc", [P, F])
        sq = sb("sq", [P, F])
        rstd = sb("rstd", [P, F])
        a4 = sb("a4", [P, 4, P])
        a4t = sb("a4t", [P, 4, P])
        r4 = sb("r4", [P, 4, P])
        acol = sb("acol", [P, 4])
        bvrow = sb("bvrow", [P, C])
        q_sb = sb("q_sb", [P, F])
        k_sb = sb("k_sb", [P, F])
        v_sb = sb("v_sb", [P, J * NH, P])
        negmax = sb("negmax", [P, B, NH])
        rowsum = sb("rowsum", [P, B, NH])
        rinv = sb("rinv", [P, B, NH])
        att = sb("att", [P, F])
        masks = sb("masks", [1, 2, STEPS * OPS], i32)
        codes = sb("codes", [1, STEPS * OPS])
        table = sb("table", [1, 2, STEPS * OPS + TPAD])
        nexts = sb("nexts", [1, STEPS * OPS], i32)
        top = sb("top", [1, 8])
        topi = sb("topi", [1, 8], u32)
        w1 = sb("w1", [P, HID])
        w2 = sb("w2", [HID, C])
        b1 = sb("b1", [HID, 1])
        b2 = sb("b2", [P, 1])
        woff_n = sb("woff_n", [OCH, C * TAPS])
        wc_n = sb("wc_n", [C, C * TAPS])
        woff = sb("woff", [P, TAPS, BP, OCH])
        wc = sb("wc", [P, TAPS, BP, C])
        ccol = sb("ccol", [P, 3])
        boff = sb("boff", [P, OCH])
        offb = sb("offb", [P, OCH])
        xcol = sb("xcol", [P, K, J, XROWS, W])
        xwin = xcol[:, 1, :, :, :]
        xt = sb("xt", [P, J, DG, NWIN, BP, C])
        om = sb("om", [P, J * NH * BP, OCH])
        msk = sb("msk", [P, J * NH * BP, GK])
        fit = sb("fit", [P, J * NH * BP, GK])
        fitm = sb("fitm", [P, 4])
        fiti = sb("fiti", [1, 1], i32)
        ty = sb("ty", [P, 2, J * NH, GK, BP, WROWS])
        tx = sb("tx", [P, J * NH, GK, BP, W])
        disty = sb("disty", [P, 2, BP, GK, WROWS])
        distx = sb("distx", [P, 2, BP, GK, W])
        smat = sb("smat", [P, 3, K3 * BP, P])
        smatT = sb("smatT", [P, 2, K3, BP, P])
        early = smat[:, :, :, :].rearrange("p r u n -> p (r u n)")
        probs = early[:, 0:2 * F].rearrange("p (r h m) -> p r h m", r=2, h=NH)
        probsT = early[:, 2 * F:4 * F].rearrange("p (r h m) -> p r h m", r=2, h=NH)
        relu = smatT[:, :, :, :, :].rearrange("p r k g n -> p (r k g n)")[:, 0:BP * F].rearrange(
            "p (g n) -> p g n", g=BP)
        samp = sb("samp", [P, 2, K3, P])
        y = sb("y", [P, F])
        stats = sb("stats", [P, 6])
        agg = sb("agg", [P, 2])
        bn = sb("bn", [P, 6])
        gw_n = sb("gw_n", [E, C])
        gwt = sb("gwt", [P, J, BP, J, E])
        gb = sb("gb", [P, 1])
        ew1 = sb("ew1", [C + 1, E, HID])
        ew2 = sb("ew2", [HID, E, C])
        eb2 = sb("eb2", [P, C])
        lg = sb("lg", [P, N])
        pr = sb("pr", [P, N])
        ltop = sb("ltop", [P, 8])
        lnm = sb("lnm", [P, 4])
        ptop = sb("ptop", [P, 8])
        rest = sb("rest", [P, N])
        pm = sb("pm", [P, N])
        pmT = sb("pmT", [P, NH, P])
        ut = sb("ut", [P, J * NH, P])
        pooled = sb("pooled", [C + 1, E, B])
        hid = sb("hid", [HID, E, B])
        eo = sb("eo", [C, B, E])
        eoT = sb("eoT", [P, C])
        eol = sb("eol", [P, J, BP, C])
        fin = sb("fin", [P, F])
        ps = ctx.enter_context(nc.psum_tensor("ps", [P, 8, 512], f32))

        loads = sem("loads_x")

        LOOP = ["l_w", "l_attn_w", "l_col", "l_done", "l_hid", "l_relu_act", "l_relu_dve", "l_ffn", "l_h",
                "l_dve", "l_act"]
        ATT = ["proj", "q", "k", "v", "sc", "mx", "ex", "nrm", "pt", "pts", "av", "att", "wo", "fin", "dchain",
               "achain"]
        for n in LOOP:
            sem(n)
        for n in ATT:
            sem("r_" + n)
        for n in ("go_pe", "go_act", "go_sp"):
            sem(n)

        block = ctx.enter_context(nc.Block())

        def dr(name):
            return a[name]

        def fm(ap):
            v = ap.rearrange("(g j) c h w -> g c j (h w)", j=J)
            return [v[g] for g in range(BP)]

        def att_pe(pe, px, weights, between=None):
            S = lambda n: sem(px + n)
            wq_, wk_, wv_, wo_ = weights
            nc.tensor.matmul(ps[:, 0, :], wq_, u[:, :], start=True, stop=True).then_inc(S("proj"), 1)
            nc.tensor.matmul(ps[:, 1, :], wk_, u[:, :], start=True, stop=True).then_inc(S("proj"), 1)
            for i in range(J * NH):
                last = nc.tensor.matmul(ps[:, 2, i * P:(i + 1) * P], u[:, i * P:(i + 1) * P], wv_,
                                        start=True, stop=True)
            last.then_inc(S("proj"), 1)
            pe.wait_ge(S("q"), 1)
            pe.wait_ge(S("k"), 1)

            def scores(t):
                bp, j = t % BP, t // BP
                if t >= 2:
                    pe.wait_ge(S("ex"), 2 * (t - 1))
                rows = slice(C * bp, C * bp + C)
                for h in range(NH):
                    q0 = j * N + h * P
                    last = nc.tensor.matmul(ps[:, 3 + t % 2, h * N:(h + 1) * N], q_sb[rows, q0:q0 + P],
                                            k_sb[rows, j * N:(j + 1) * N], start=True, stop=True)
                last.then_inc(S("sc"), 1)

            def transposes(t):
                pe.wait_ge(S("nrm"), t + 1)
                if t >= 2:
                    pe.wait_ge(S("pts"), t - 1)
                for mh in range(NH):
                    for h in range(NH):
                        last = nc.tensor.transpose(ps[:, 5 + t % 2, mh * N + h * P:mh * N + (h + 1) * P],
                                                   probs[:, t % 2, h, mh * P:(mh + 1) * P], ident)
                last.then_inc(S("pt"), 1)

            def values(t):
                bp, j = t % BP, t // BP
                pe.wait_ge(S("pts"), t + 1)
                if t == 0:
                    pe.wait_ge(S("v"), 1)
                for mh in range(NH):
                    last = nc.tensor.matmul(ps[C * bp:C * bp + C, 7, j * N:(j + 1) * N],
                                            v_sb[:, j * NH + mh, C * bp:C * bp + C], probsT[:, t % 2, mh, :],
                                            start=(mh == 0), stop=(mh == NH - 1))
                last.then_inc(S("av"), 1)

            scores(0)
            scores(1)
            if between:
                between()
            for t in range(B + 1):
                if t < B:
                    transposes(t)
                if t + 2 < B:
                    scores(t + 2)
                if t >= 1:
                    values(t - 1)
            pe.wait_ge(S("att"), 1)
            if between:
                pe.wait_ge(sem("c_wa"), 2 * BP)
            nc.tensor.matmul(ps[:, 0, :], wo_, att[:, :], start=True, stop=True).then_inc(S("wo"), 1)

        def att_act(act, px, bk, between=None):
            S = lambda n: sem(px + n)
            act.wait_ge(S("proj"), 2)
            nc.scalar.activation(k_sb[:, :], ps[:, 1, :], ACT.Identity, bias=bk).then_inc(S("k"), 1)
            for t in range(B):
                act.wait_ge(S("mx"), t + 1)
                if t >= 2:
                    act.wait_ge(S("pt"), t - 1)
                for h in range(NH):
                    nc.scalar.activation(probs[:, t % 2, h, :], ps[:, 3 + t % 2, h * N:(h + 1) * N], ACT.Exp,
                                         bias=negmax[:, t, h:h + 1],
                                         accum_out=rowsum[:, t, h:h + 1]).then_inc(S("ex"), 1)
                if t >= 1:
                    copy_probs(act, S, t - 1)
                if between:
                    between(t)
            copy_probs(act, S, B - 1)

        def copy_probs(act, S, t):
            act.wait_ge(S("pt"), t + 1)
            if t >= 2:
                act.wait_ge(S("av"), t - 1)
            nc.scalar.activation(probsT[:, t % 2, :, :], ps[:, 5 + t % 2, :], ACT.Copy).then_inc(S("pts"), 1)

        def table_step(link, t):
            size = STEPS * OPS
            am, fm_ = masks[:, 0, :], masks[:, 1, :]
            t0, t1 = table[:, 0, :], table[:, 1, :]
            if t == 0:
                link.eng.wait_ge(sem("ld_m"), 48)
                link(nc.vector.memset(table[:, :, size:], 0.0))
                link(nc.vector.tensor_tensor(t1[:, 0:size], am, fm_, ALU.max))
            elif t == 1:
                link(nc.vector.scalar_tensor_tensor(out=t0[:, 0:size], in0=am, scalar=2.0, in1=codes[:, :],
                                                    op0=ALU.mult, op1=ALU.add))
                link(nc.vector.tensor_tensor(t0[:, 0:size], t0[:, 0:size], fm_, ALU.add))
            elif t == 2:
                link(nc.vector.tensor_tensor(t0[:, 0:size], t0[:, 0:size], t1[:, 0:size], ALU.mult))
            elif t < 6:
                for n in (2 * (t - 3), 2 * (t - 3) + 1):
                    d, (src_, dst) = OPS << n, ((t0, t1) if n % 2 == 0 else (t1, t0))
                    link(nc.vector.tensor_tensor(dst[:, 0:size], src_[:, 0:size], src_[:, d:d + size], ALU.min))
            elif t == 6:
                nc.vector.tensor_scalar(nexts[:, :], t0[:, 0:size], float(NONE), None,
                                        ALU.add).then_inc(sem("table"), 1)

        def att_dve(dve, px, bq, bv, between=None):
            S = lambda n: sem(px + n)
            link = Chain(dve, S("dchain"))
            dve.wait_ge(S("proj"), 1)
            nc.vector.tensor_scalar(q_sb[:, :], ps[:, 0, :], bq, QSCALE, ALU.add, ALU.mult).then_inc(S("q"), 1)
            dve.wait_ge(S("proj"), 3)
            if bv is None:
                nc.vector.tensor_copy(v_sb[:, :, :], ps[:, 2, :]).then_inc(S("v"), 1)
            else:
                nc.vector.tensor_tensor(v_sb[:, :, :].rearrange("p i (g c) -> p (i g) c", c=C),
                                        ps[:, 2, :].rearrange("p (i c) -> p i c", c=C),
                                        bv.unsqueeze(1).broadcast_to([P, J * NH * BP, C]),
                                        ALU.add).then_inc(S("v"), 1)

            def maxima(t):
                dve.wait_ge(S("sc"), t + 1)
                nc.vector.tensor_reduce(negmax[:, t, :], ps[:, 3 + t % 2, :].rearrange("p (h m) -> p h m", h=NH),
                                        AX.X, ALU.max, negate=True).then_inc(S("mx"), 1)

            maxima(0)
            for t in range(B):
                if t + 1 < B:
                    maxima(t + 1)
                dve.wait_ge(S("ex"), 2 * (t + 1))
                link(nc.vector.reciprocal(rinv[:, t, :], rowsum[:, t, :]))
                for h in range(NH):
                    ins = nc.vector.tensor_scalar(probs[:, t % 2, h, :], probs[:, t % 2, h, :],
                                                  rinv[:, t, h:h + 1], None, ALU.mult)
                ins.then_inc(S("nrm"), 1)
                if between:
                    between(link, t)
            dve.wait_ge(S("av"), B)
            nc.vector.tensor_copy(att[:, :], ps[:, 7, :]).then_inc(S("att"), 1)
            dve.wait_ge(S("wo"), 1)

        def norm_pe(pe, i):
            nc.tensor.matmul(ps[:, 5, :], meanm, x[:, :], start=True, stop=True).then_inc(sem("norm_mean"), 1)
            pe.wait_ge(sem("norm_sq"), i)
            nc.tensor.matmul(ps[:, 6, :], meanm, sq[:, :], start=True, stop=True).then_inc(sem("norm_var"), 1)

        def norm_act(act, i, eps):
            act.wait_ge(sem("norm_xc"), i)
            nc.scalar.activation(sq[:, :], xc[:, :], ACT.Square).then_inc(sem("norm_sq"), 1)
            act.wait_ge(sem("norm_var"), i)
            nc.scalar.activation(rstd[:, :], ps[:, 6, :], ACT.Ln, bias=eps).then_inc(sem("norm_ln"), 1)
            act.wait_ge(sem("norm_ln"), i)
            nc.scalar.activation(rstd[:, :], rstd[:, :], ACT.Exp, scale=-0.5).then_inc(sem("norm_rstd"), 1)

        def norm_dve(dve, i):
            dve.wait_ge(sem("norm_mean"), i)
            nc.vector.tensor_tensor(xc[:, :], x[:, :], ps[:, 5, :], ALU.subtract).then_inc(sem("norm_xc"), 1)
            dve.wait_ge(sem("norm_rstd"), i)

        def recurrent(eng, body):
            cur = eng.alloc_register("cur")
            op = eng.alloc_register("op")
            code = eng.alloc_register("code")
            at = eng.alloc_register("at")
            wi = eng.alloc_register("wi")
            has_att = eng.alloc_register("has_att")
            has_ffn = eng.alloc_register("has_ffn")
            eng.reg_mov(cur, 0)
            with eng.Fori(0, STEPS):
                with eng.If_cmp(cur, STEPS, "IS_LT"):
                    body.start(eng)
                    eng.load(op, topi[0:1, 0:1])
                    eng.reg_mul(at, cur, OPS)
                    eng.reg_add(at, at, op)
                    ati = eng.snap(at, min_val=0, max_val=STEPS * OPS - 1)
                    eng.load(code, nexts[0:1, bass.ds(ati, 1)])
                    eng.reg_alu(cur, code, 2, ALU.logical_shift_right)
                    eng.reg_mul(wi, cur, OPS)
                    eng.reg_add(wi, wi, op)
                    eng.reg_add(cur, cur, 1)
                    eng.reg_alu(has_ffn, code, 1, ALU.bitwise_and)
                    eng.reg_alu(has_att, code, 2, ALU.bitwise_and)
                    with eng.If_cmp(code, NONE, "IS_LT"):
                        with eng.If_cmp(has_att, 0, "IS_NE"):
                            body.attention(eng, wi)
                        with eng.If_cmp(has_ffn, 0, "IS_NE"):
                            body.ffn(eng, wi)
                        body.end(eng)

        class SPBody:
            def start(self, sp):
                sp.wait_ge(sem("go_sp"), 1)
                sp.sem_clear(sem("go_sp"))

            def attention(self, sp, wi):
                i = sp.snap(wi, min_val=0, max_val=STEPS * OPS - 1)
                for n, name in enumerate(("wq", "wk", "wv", "wo")):
                    w = dr("L0_ffn_" + name)
                    for g in range(BP):
                        sp.dma_start(r4[C * g:C * g + C, n, C * g:C * g + C],
                                     w[bass.ds(i, 1), :, :].rearrange("o c d -> (o c) d")).then_inc(sem("l_attn_w"), 16)

            def ffn(self, sp, wi):
                i = sp.snap(wi, min_val=0, max_val=STEPS * OPS - 1)
                for g in range(BP):
                    sp.dma_start(w1[C * g:C * g + C, :],
                                 dr("L0_ffn_ffn_w1")[bass.ds(i, 1), :, :].rearrange("o c d -> (o c) d")).then_inc(sem("l_w"), 16)
                sp.dma_start(b1[:, :], dr("L0_ffn_ffn_b1")[bass.ds(i, 1), :].rearrange("o (c k) -> (o c) k", k=1)).then_inc(sem("l_w"), 16)
                sp.dma_start(w2[:, :], dr("L0_ffn_ffn_w2")[bass.ds(i, 1), :, :].rearrange("o c d -> (o c) d")).then_inc(sem("l_w"), 16)
                for g in range(BP):
                    sp.dma_start(b2[C * g:C * g + C, :],
                                 dr("L0_ffn_ffn_b2")[bass.ds(i, 1), :].rearrange("o (c k) -> (o c) k", k=1)).then_inc(sem("l_w"), 16)

            def end(self, sp):
                sp.sem_inc(sem("l_done"), 1)

        FFN_LOADS = 16 * (2 * BP + 2)
        ATT_LOADS = 16 * 4 * BP

        class PEBody:
            def start(self, pe):
                pe.wait_ge(sem("go_pe"), 1)
                pe.sem_clear(sem("go_pe"))

            def attention(self, pe, wi):
                pe.wait_ge(sem("l_attn_w"), ATT_LOADS)
                att_pe(pe, "r_", [r4[:, n, :] for n in range(4)])
                pe.wait_ge(sem("r_fin"), 1)

            def ffn(self, pe, wi):
                pe.wait_ge(sem("l_w"), FFN_LOADS)
                for g in range(BP):
                    nc.tensor.matmul(ps[:, g, :], w1[C * g:C * g + C, :], u[C * g:C * g + C, :],
                                     start=True, stop=True).then_inc(sem("l_hid"), 1)
                for g in range(BP):
                    pe.wait_ge(sem("l_relu_dve" if g % 2 else "l_relu_act"), g // 2 + 1)
                    last = nc.tensor.matmul(ps[C * g:C * g + C, 4, :], w2[:, :], relu[:, g, :],
                                            start=True, stop=True)
                last.then_inc(sem("l_ffn"), 1)
                pe.wait_ge(sem("l_h"), 1)

            def end(self, pe):
                nc.tensor.matmul(ps[0:1, 5, 0:C], u[0:C, 0:1], ident[0:C, 0:C],
                                 start=True, stop=True).then_inc(sem("l_col"), 1)

        class ACTBody:
            def start(self, act):
                act.wait_ge(sem("go_act"), 1)
                act.sem_clear(sem("go_act"))

            def attention(self, act, wi):
                att_act(act, "r_", 0.0)

            def ffn(self, act, wi):
                act.wait_ge(sem("l_w"), FFN_LOADS)
                for g in (0, 2):
                    act.wait_ge(sem("l_hid"), g + 1)
                    nc.scalar.activation(relu[:, g, :], ps[:, g, :], ACT.Relu,
                                         bias=b1[:, 0:1]).then_inc(sem("l_relu_act"), 1)

            def end(self, act):
                act.sem_inc(sem("l_done"), 1)

        class DVEBody:
            def start(self, dve):
                pass

            def attention(self, dve, wi):
                att_dve(dve, "r_", 0.0, None)
                nc.vector.tensor_copy(u[:, :], ps[:, 0, :]).then_inc(sem("r_fin"), 1)
                dve.wait_ge(sem("r_fin"), 1)

            def ffn(self, dve, wi):
                dve.wait_ge(sem("l_w"), FFN_LOADS)
                for g in (1, 3):
                    dve.wait_ge(sem("l_hid"), g + 1)
                    nc.vector.tensor_scalar(relu[:, g, :], ps[:, g, :], b1[:, 0:1], 0.0,
                                            ALU.add, ALU.max).then_inc(sem("l_relu_dve"), 1)
                dve.wait_ge(sem("l_ffn"), 1)
                nc.vector.tensor_scalar(u[:, :], ps[:, 4, :], b2[:, 0:1], None, ALU.add).then_inc(sem("l_h"), 1)

            def end(self, dve):
                dve.wait_ge(sem("l_col"), 1)
                dve.wait_ge(sem("l_done"), 2)
                for n in LOOP:
                    if n != "l_dve":
                        dve.sem_clear(sem(n))
                for n in ATT:
                    dve.sem_clear(sem("r_" + n))
                pick_op(dve, "l_dve")
                dve.sem_clear(sem("l_dve"))

        def pick_op(dve, name):
            link = Chain(dve, sem(name))
            link(nc.vector.max(top[:, :], ps[0:1, 5, 0:OPS]))
            link(nc.vector.max_index(topi[:, :], top[:, :], ps[0:1, 5, 0:OPS]))
            dve.sem_inc(sem("go_pe"), 1)
            dve.sem_inc(sem("go_act"), 1)
            dve.sem_inc(sem("go_sp"), 1)

        def sample_steps(wins):
            return [(jh, k3, g, w) for jh in range(J * NH) for k3 in range(TAPS // K3)
                    for g in range(DG) for w in range(len(wins))]

        def by_fit(eng, run):
            eng.wait_ge(sem("c_fit"), 1)
            fits = eng.alloc_register("fits")
            eng.load(fits, fiti[0:1, 0:1])
            with eng.If_cmp(fits, 0, "IS_NE"):
                run((None,))
            with eng.If_cmp(fits, 0, "IS_EQ"):
                run((0, 1))

        def on_pool(n):
            return n % 4 == 3

        def weigh(eng, wins, n, step):
            jh, k3, g, w = step
            if n >= 3:
                eng.wait_ge(sem("s_tr"), n - 2)
            ks = slice(g * TAPS + K3 * k3, g * TAPS + K3 * k3 + K3)
            rows = ty[:, w, jh, ks, :, :].rearrange("p k g r -> p (k g) r")
            colw = tx[:, jh, ks, :, :].rearrange("p k g r -> p (k g) r")
            shape = [P, K3 * BP, WROWS, W]
            return eng.tensor_tensor(smat[:, n % 3, :, :].rearrange("p u (r c) -> p u r c", c=W),
                                     rows.unsqueeze(3).broadcast_to(shape), colw.unsqueeze(2).broadcast_to(shape),
                                     ALU.mult)

        def sample_pool(pool, wins):
            nw = len(wins)
            for n, step in enumerate(sample_steps(wins)):
                if on_pool(n):
                    pool.wait_ge(sem("s_ty"), nw * (step[0] + 1))
                    pool.wait_ge(sem("s_tx"), step[0] + 1)
                    weigh(nc.gpsimd, wins, n, step).then_inc(sem("s_wp"), 1)

        def sample_dve(dve, wins):
            nw = len(wins)
            steps = sample_steps(wins)
            per_group = DG * nw

            def distances(jh):
                lead = slice(BP * jh, BP * jh + BP)
                for w in range(nw):
                    i = jh * nw + w
                    shape = [P, BP, GK, WROWS]
                    lo = CA["grid"][0] if wins[0] is None else CA["wide"][0] + ((jh % NH) * 2 + w) * WROWS
                    nc.vector.tensor_tensor(disty[:, i % 2, :, :, :],
                                            om[:, lead, 0:GK].unsqueeze(3).broadcast_to(shape),
                                            cst[:, lo:lo + WROWS].unsqueeze(1).unsqueeze(1).broadcast_to(shape),
                                            ALU.subtract).then_inc(sem("s_dy"), 1)
                    if nw > 1:
                        row_weights(jh, w)
                if jh >= 2:
                    dve.wait_ge(sem("s_tx"), jh - 1)
                shape = [P, BP, GK, W]
                nc.vector.tensor_tensor(distx[:, jh % 2, :, :, :],
                                        om[:, lead, GK:2 * GK].unsqueeze(3).broadcast_to(shape),
                                        const("grid").unsqueeze(1).unsqueeze(1).broadcast_to(shape),
                                        ALU.subtract).then_inc(sem("s_dx"), 1)

            def row_weights(jh, w):
                i = jh * nw + w
                dve.wait_ge(sem("s_ay"), i + 1)
                nc.vector.tensor_tensor(ty[:, w, jh, :, :, :].rearrange("p k g r -> p g k r"),
                                        disty[:, i % 2, :, :, :],
                                        msk[:, BP * jh:BP * jh + BP, :].unsqueeze(3).broadcast_to(
                                            [P, BP, GK, WROWS]), ALU.mult).then_inc(sem("s_ty"), 1)

            def keep(q):
                dve.wait_ge(sem("s_grp"), q + 1)
                if q >= 2:
                    dve.wait_ge(sem("s_cv"), q - 1)
                nc.vector.tensor_copy(samp[:, q % 2, :, :], ps[:, 6, 0:K3 * P]).then_inc(sem("s_samp"), 1)

            distances(0)
            if nw == 1:
                distances(1)
                row_weights(0, 0)
            for n, step in enumerate(steps):
                jh = step[0]
                if n and steps[n - 1][0] != jh:
                    if nw == 1:
                        if jh + 1 < J * NH:
                            distances(jh + 1)
                        row_weights(jh, 0)
                    else:
                        distances(jh)
                if not on_pool(n):
                    dve.wait_ge(sem("s_ty"), nw * (jh + 1))
                    dve.wait_ge(sem("s_tx"), jh + 1)
                    weigh(nc.vector, wins, n, step).then_inc(sem("s_wd"), 1)
                if n >= 2 and (n - 1) % per_group == 0:
                    keep((n - 1) // per_group - 1)
            keep(len(steps) // per_group - 1)

        def sample_act(act, wins):
            nw = len(wins)
            steps = sample_steps(wins)
            link = Chain(act, sem("s_achain"))

            def weights(jh):
                for w in range(nw):
                    i = jh * nw + w
                    act.wait_ge(sem("s_dy"), i + 1)
                    link(nc.scalar.activation(disty[:, i % 2, :, :, :], disty[:, i % 2, :, :, :], ACT.Abs))
                    nc.scalar.activation(disty[:, i % 2, :, :, :], disty[:, i % 2, :, :, :], ACT.Relu,
                                         bias=1.0, scale=-1.0).then_inc(sem("s_ay"), 1)
                act.wait_ge(sem("s_dx"), jh + 1)
                link(nc.scalar.activation(distx[:, jh % 2, :, :, :], distx[:, jh % 2, :, :, :], ACT.Abs))
                nc.scalar.activation(tx[:, jh, :, :, :].rearrange("p k g r -> p g k r"), distx[:, jh % 2, :, :, :],
                                     ACT.Relu, bias=1.0, scale=-1.0).then_inc(sem("s_tx"), 1)

            weights(0)
            if nw == 1:
                weights(1)
            for n, step in enumerate(steps):
                jh = step[0]
                if n and steps[n - 1][0] != jh:
                    if nw > 1:
                        weights(jh)
                    elif jh + 1 < J * NH:
                        weights(jh + 1)
                act.wait_ge(sem("s_tr"), n + 1)
                if n >= 2:
                    act.wait_ge(sem("s_mm"), n - 1)
                nc.scalar.activation(smatT[:, n % 2, :, :, :].rearrange("p k g n -> p (k g n)"),
                                     ps[:, 3 * (n % 2):3 * (n % 2) + 3, :].rearrange("p b n -> p (b n)"),
                                     ACT.Copy).then_inc(sem("s_smt"), 1)

        def sample_pe(pe, wins):
            nw = len(wins)
            steps = sample_steps(wins)
            per_group = DG * nw
            pe.wait_ge(sem("c_xts"), J * DG)
            if nw > 1:
                for j in range(J):
                    for w in range(2):
                        last = nc.tensor.transpose(
                            ps[:, 2 + j, w * P:(w + 1) * P],
                            xwin[:, j, 2 + WROWS * w:2 + WROWS * w + WROWS, :].rearrange("p r c -> p (r c)"), ident)
                last.then_inc(sem("s_xt"), 1)
                pe.wait_ge(sem("s_xts"), J * DG)

            def transposes(n):
                if on_pool(n):
                    pe.wait_ge(sem("s_wp"), n // 4 + 1)
                else:
                    pe.wait_ge(sem("s_wd"), n - (n + 1) // 4 + 1)
                if n >= 2:
                    pe.wait_ge(sem("s_smt"), n - 1)
                for kk in range(K3):
                    for bp in range(BP):
                        last = nc.tensor.transpose(ps[:, 3 * (n % 2) + kk, bp * P:(bp + 1) * P],
                                                   smat[:, n % 3, kk * BP + bp, :], ident)
                last.then_inc(sem("s_tr"), 1)

            def products(n):
                jh, k3, g, w = steps[n]
                j, h = jh // NH, jh % NH
                pe.wait_ge(sem("s_smt"), n + 1)
                first, final = n % per_group == 0, n % per_group == per_group - 1
                if nw == 1:
                    for blk in range(2):
                        for bp in range(BP):
                            o = ps[C * bp:C * bp + C, 6, 0:K3 * P].rearrange("c (k n) -> c k n", k=K3)
                            last = nc.tensor.matmul(o[:, :, blk * BLK:(blk + 1) * BLK],
                                                    xt[:, j, g, 2 * h + blk, bp, :],
                                                    smatT[:, n % 2, :, bp, blk * BLK:(blk + 1) * BLK],
                                                    start=(first and blk == 0), stop=final, skip_group_check=True)
                else:
                    for bp in range(BP):
                        o = ps[C * bp:C * bp + C, 6, 0:K3 * P].rearrange("c (k n) -> c k n", k=K3)
                        last = nc.tensor.matmul(o, xt[:, j, g, w, bp, :], smatT[:, n % 2, :, bp, :],
                                                start=first, stop=final, skip_group_check=True)
                last.then_inc(sem("s_mm"), 1)
                if final:
                    pe.wait_ge(sem("s_mm"), n + 1)
                    pe.sem_inc(sem("s_grp"), 1)

            def convolve(q):
                jh, k3 = q // (TAPS // K3), q % (TAPS // K3)
                pe.wait_ge(sem("s_samp"), q + 1)
                for kk in range(K3):
                    tap = K3 * k3 + kk
                    last = nc.tensor.matmul(ps[:, 7, jh * P:(jh + 1) * P], wc[:, tap, :, :].rearrange("p g o -> p (g o)"),
                                            samp[:, q % 2, kk, :], start=(tap == 0), stop=(tap == TAPS - 1))
                last.then_inc(sem("s_cv"), 1)
                return last

            transposes(0)
            for n in range(len(steps)):
                if n + 1 < len(steps):
                    transposes(n + 1)
                if n and n % per_group == 0:
                    convolve(n // per_group - 1)
                products(n)
            convolve(len(steps) // per_group - 1)
            pe.wait_ge(sem("s_cv"), len(steps) // per_group)
            pe.sem_inc(sem("c_out"), 1)

        def windows(eng_copy, eng, name, nwin, done):
            eng.wait_ge(sem(name), 1)
            for j in range(J):
                for g in range(DG):
                    src_ = ps[:, 2 + j, 0:nwin * P].rearrange("p (w g c) -> p w g c", w=nwin, g=BP)
                    eng_copy(xt[:, j, g, 0:nwin, :, CG * g:CG * g + CG],
                             src_[:, :, :, CG * g:CG * g + CG]).then_inc(sem(done), 1)

        @block.sync
        def _(sp):
            for g, v in enumerate(fm(dr("x"))):
                sp.dma_start(x[C * g:C * g + C, :].rearrange("c (j n) -> c j n", j=J), v).then_inc(sem("ld_x"), 16)
            sp.dma_start(cst[:, :], dr("cst")).then_inc(sem("ld_cst"), 16)
            sp.wait_ge(sem("zero_a4"), 1)
            for n, name in enumerate(("wq", "wk", "wv", "wo")):
                for g in range(BP):
                    sp.dma_start(a4[C * g:C * g + C, n, C * g:C * g + C], dr("L0_conv_" + name)).then_inc(sem("ld_a"), 16)
            for n, name in enumerate(("freq_weights", "bq", "bk", "bo")):
                for g in range(BP):
                    sp.dma_start(acol[C * g:C * g + C, n:n + 1],
                                 dr("L0_conv_" + name).rearrange("(c k) -> c k", k=1)).then_inc(sem("ld_a"), 16)
            sp.dma_start(bvrow[:, :], dr("L0_conv_bv").partition_broadcast(P)).then_inc(sem("ld_a"), 16)
            sp.dma_start(masks[:, 0, :], dr("L0_ffn_attn_mask")).then_inc(sem("ld_m"), 16)
            sp.dma_start(masks[:, 1, :], dr("L0_ffn_ffn_mask")).then_inc(sem("ld_m"), 16)
            sp.dma_start(codes[:, :], dr("codes")).then_inc(sem("ld_m"), 16)
            recurrent(sp, SPBody())
            sp.wait_ge(sem("out_ready"), 1)
            src = {"a": x, "b": x, "c": x}.get(upto, fin)
            for g, v in enumerate(fm(out)):
                sp.dma_start(v, src[C * g:C * g + C, :].rearrange("c (j n) -> c j n", j=J)).then_inc(sem("stored"), 16)
            sp.wait_ge(sem("stored"), 16 * BP)

        @block.gpsimd
        def _(pool):
            nc.gpsimd.memset(a4[:, :, :], 0.0).then_inc(sem("zero_a4"), 1)
            nc.gpsimd.memset(r4[:, :, :], 0.0).then_inc(sem("zero_r4"), 1)
            pool.dma_start(woff_n[:, :], dr("L1_conv_w_off").rearrange("o c a b -> o (c a b)")).then_inc(sem("ld_c"), 16)
            pool.dma_start(wc_n[:, :], dr("L1_conv_w").rearrange("o c a b -> o (c a b)")).then_inc(sem("ld_c"), 16)
            pool.dma_start(gw_n[:, :], dr("L1_ffn_gate_w")).then_inc(sem("ld_c"), 16)
            pool.dma_start(boff[:, :], dr("L1_conv_b_off").partition_broadcast(P)).then_inc(sem("ld_c"), 16)
            nc.gpsimd.memset(woff[:, :, :, :], 0.0).then_inc(sem("zero_c"), 1)
            nc.gpsimd.memset(wc[:, :, :, :], 0.0).then_inc(sem("zero_c"), 1)
            nc.gpsimd.memset(gwt[:, :, :, :, :], 0.0).then_inc(sem("zero_c"), 1)
            nc.gpsimd.memset(xcol[:, :, :, :, :], 0.0).then_inc(sem("zero_c"), 1)
            nc.gpsimd.memset(xt[:, :, :, :, :, :], 0.0).then_inc(sem("zero_c"), 1)
            pool.wait_ge(sem("zero_c"), 5)
            nc.gpsimd.memset(pooled[C:C + 1, :, :], 1.0).then_inc(sem("zero_c"), 1)
            for n, name in enumerate(("b", "gamma", "beta")):
                col = dr("L1_conv_" + name).rearrange("(c k) -> c k", k=1)
                for g in range(BP):
                    pool.dma_start(ccol[C * g:C * g + C, n:n + 1], col).then_inc(sem("ld_d"), 16)
            for b in range(B):
                pool.dma_start(gb[E * b:E * b + E, :],
                               dr("L1_ffn_gate_b").rearrange("(e k) -> e k", k=1)).then_inc(sem("ld_d"), 16)
            pool.dma_start(ew1[:, :, :], dr("L1_ffn_weight1").rearrange("e d h -> d e h")).then_inc(sem("ld_d"), 16)
            w2_ = dr("L1_ffn_weight2").rearrange("e h o -> h e o")
            pool.dma_start(ew2[:, :, :], w2_[0:HID, :, :]).then_inc(sem("ld_d"), 16)
            for b in range(B):
                pool.dma_start(eb2[E * b:E * b + E, :], dr("L1_ffn_weight2")[:, HID, :]).then_inc(sem("ld_d"), 16)
            by_fit(pool, lambda wins: sample_pool(pool, wins))

        @block.scalar
        def _(act):
            act.wait_ge(sem("ld_cst"), 16)
            norm_act(act, 1, eps6)

            def weights_of_3(t):
                if t == 2:
                    act.wait_ge(sem("c_w"), 1)
                    act.wait_ge(sem("zero_c"), 6)
                if 2 <= t < 2 + BP:
                    g = t - 2
                    rows = slice(C * g, C * g + C)
                    nc.scalar.activation(woff[rows, :, g, :], ps[0:C, 0, 0:TAPS * OCH].rearrange("c (t o) -> c t o", o=OCH),
                                         ACT.Copy).then_inc(sem("c_wa"), 1)
                    nc.scalar.activation(wc[rows, :, g, :], ps[0:C, 1, 0:TAPS * C].rearrange("c (t o) -> c t o", o=C),
                                         ACT.Copy).then_inc(sem("c_wa"), 1)

            att_act(act, "a_", acol[:, 2:3], weights_of_3)
            norm_act(act, 2, eps5)
            act.wait_ge(sem("table"), 1)
            recurrent(act, ACTBody())
            norm_act(act, 3, eps6)
            act.wait_ge(sem("c_u"), 1)
            nc.scalar.activation(xcol[:, 0, :, 2:2 + H, 1:W], xwin[:, :, 2:2 + H, 0:W - 1],
                                 ACT.Copy).then_inc(sem("c_right"), 1)
            act.wait_ge(sem("c_oms"), 2)
            nc.scalar.activation(msk[:, :, :], om[:, :, 2 * GK:], ACT.Exp, scale=-1.0).then_inc(sem("c_me"), 1)
            windows(lambda o, i: nc.scalar.activation(o, i, ACT.Copy), act, "c_xt", NWIN, "c_xts")

            def run(wins):
                if len(wins) > 1:
                    windows(lambda o, i: nc.scalar.activation(o, i, ACT.Copy), act, "s_xt", 2, "s_xts")
                sample_act(act, wins)
            by_fit(act, run)
            act.wait_ge(sem("c_var"), 1)
            link = Chain(act, sem("a_main"))
            link(nc.scalar.activation(bn[:, 2:3], ps[:, 1, 0:1], ACT.Ln, bias=eps5))
            nc.scalar.activation(bn[:, 3:4], bn[:, 2:3], ACT.Exp, scale=-0.5).then_inc(sem("c_rs"), 1)
            norm_act(act, 4, eps5)
            act.wait_ge(sem("e_ut"), 1)
            nc.scalar.activation(ut[:, :, :].rearrange("p i c -> p (i c)"), ps[:, 1, :], ACT.Copy).then_inc(sem("e_uts"), 1)
            act.wait_ge(sem("e_max"), 1)
            nc.scalar.activation(pr[:, :], lg[:, :], ACT.Exp, bias=lnm[:, 0:1], accum_out=lnm[:, 1:2]).then_inc(sem("e_ex"), 1)
            act.wait_ge(sem("e_h"), 1)
            nc.scalar.activation(hid[:, :, :].rearrange("p e b -> p (e b)"), ps[:, 4, 0:E * B], ACT.Gelu).then_inc(sem("e_hid"), 1)

        @block.tensor
        def _(pe):
            pe.wait_ge(sem("ld_x"), 16 * BP)
            pe.wait_ge(sem("ld_cst"), 16)
            norm_pe(pe, 1)
            pe.wait_ge(sem("a_u"), 1)
            pe.wait_ge(sem("a_w"), 1)

            def weights_of_3():
                pe.wait_ge(sem("ld_c"), 64)
                for tap in range(TAPS):
                    nc.tensor.transpose(ps[0:C, 0, tap * OCH:(tap + 1) * OCH], woff_n[:, tap::TAPS], ident[0:OCH, 0:OCH])
                for tap in range(TAPS):
                    nc.tensor.transpose(ps[0:C, 1, tap * C:(tap + 1) * C], wc_n[:, tap::TAPS], ident[0:C, 0:C])
                nc.tensor.transpose(ps[0:C, 1, TAPS * C:TAPS * C + E], gw_n[:, :], ident[0:E, 0:E]).then_inc(sem("c_w"), 1)

            att_pe(pe, "a_", [a4t[:, n, :] for n in range(4)], weights_of_3)
            pe.wait_ge(sem("a_x"), 1)
            norm_pe(pe, 2)
            pe.wait_ge(sem("b_u"), 1)
            pe.wait_ge(sem("zero_r4"), 1)
            nc.tensor.matmul(ps[0:1, 5, 0:C], u[0:C, 0:1], ident[0:C, 0:C], start=True, stop=True).then_inc(sem("b_col"), 1)
            pe.wait_ge(sem("table"), 1)
            recurrent(pe, PEBody())
            pe.wait_ge(sem("b_x"), 1)
            norm_pe(pe, 3)
            pe.wait_ge(sem("c_u"), 1)
            pe.wait_ge(sem("c_wd"), 1)
            for jh in range(J * NH):
                j, h = jh // NH, jh % NH
                for n, tap in enumerate((1, 4, 7, 0, 3, 6, 2, 5, 8)):
                    if n == 3:
                        pe.wait_ge(sem("c_right"), 1)
                    if n == 6:
                        pe.wait_ge(sem("c_left"), 1)
                    r0 = H // NH * h + tap // K + 1
                    last = nc.tensor.matmul(ps[:, jh // 2, (jh % 2) * BP * OCH:(jh % 2 + 1) * BP * OCH],
                                            xcol[:, tap % K, j, r0:r0 + H // NH, :].rearrange("p r c -> p (r c)"),
                                            woff[:, tap, :, :].rearrange("p g o -> p (g o)"),
                                            start=(n == 0), stop=(n == TAPS - 1))
                last.then_inc(sem("c_om"), 1)
            for j in range(J):
                for w in range(NWIN):
                    last = nc.tensor.transpose(ps[:, 2 + j, w * P:(w + 1) * P],
                                               xwin[:, j, 4 * w:4 * w + WROWS, :].rearrange("p r c -> p (r c)"), ident)
            last.then_inc(sem("c_xt"), 1)
            pe.wait_ge(sem("c_fitp"), 1)
            nc.tensor.transpose(ps[0:1, 4, 0:P], fitm[:, 0:1], ident).then_inc(sem("c_fitt"), 1)
            by_fit(pe, lambda wins: sample_pe(pe, wins))
            pe.wait_ge(sem("c_agg"), 1)
            nc.tensor.matmul(ps[:, 0, 0:1], fold, agg[:, 0:1], start=True, stop=True).then_inc(sem("c_mu"), 1)
            pe.wait_ge(sem("c_dev"), 1)
            nc.tensor.matmul(ps[:, 1, 0:1], fold, bn[:, 1:2], start=True, stop=True).then_inc(sem("c_var"), 1)
            pe.wait_ge(sem("c_xn"), 1)
            norm_pe(pe, 4)
            pe.wait_ge(sem("e_u"), 1)
            for j in range(J):
                last = nc.tensor.matmul(ps[:, 0, 0:N], gwt[:, j, :, :, :].rearrange("p g j e -> p (g j e)"),
                                        u[:, j * N:(j + 1) * N], start=(j == 0), stop=(j == J - 1))
            last.then_inc(sem("e_lg"), 1)
            for i in range(J * NH):
                last = nc.tensor.transpose(ps[:, 1, i * P:(i + 1) * P], u[:, i * P:(i + 1) * P], ident)
            last.then_inc(sem("e_ut"), 1)
            pe.wait_ge(sem("e_pm"), 1)
            for h in range(NH):
                last = nc.tensor.transpose(ps[:, 2, h * P:(h + 1) * P], pm[:, h * P:(h + 1) * P], ident)
            last.then_inc(sem("e_pmt"), 1)
            pe.wait_ge(sem("e_uts"), 1)
            pe.wait_ge(sem("e_pmts"), 1)
            for j in range(J):
                for h in range(NH):
                    last = nc.tensor.matmul(ps[:, 3, j * P:(j + 1) * P], ut[:, j * NH + h, :], pmT[:, h, :],
                                            start=(h == 0), stop=(h == NH - 1))
            last.then_inc(sem("e_pool"), 1)
            pe.wait_ge(sem("ld_d"), 16 * (3 * BP + 2 * B + 2))
            pe.wait_ge(sem("e_pools"), BP)
            for e in range(E):
                last = nc.tensor.matmul(ps[:, 4, e * B:(e + 1) * B], ew1[:, e, :], pooled[:, e, :], start=True, stop=True)
            last.then_inc(sem("e_h"), 1)
            pe.wait_ge(sem("e_hid"), 1)
            for e in range(E):
                last = nc.tensor.matmul(ps[0:C, 5, e * B:(e + 1) * B], ew2[:, e, :], hid[:, e, :], start=True, stop=True)
            last.then_inc(sem("e_o"), 1)
            pe.wait_ge(sem("e_os"), 1)
            nc.tensor.transpose(ps[:, 6, 0:C], eo[:, :, :].rearrange("o b e -> o (b e)"), ident[0:C, 0:C]).then_inc(sem("e_ot"), 1)
            pe.wait_ge(sem("e_ol"), 1)
            for j in range(J):
                last = nc.tensor.matmul(ps[:, 7, j * N:(j + 1) * N], eol[:, j, :, :].rearrange("p g o -> p (g o)"),
                                        pm[:, :], start=True, stop=True)
            last.then_inc(sem("e_y"), 1)

        @block.vector
        def _(dve):
            dve.wait_ge(sem("ld_x"), 16 * BP)
            norm_dve(dve, 1)
            link = Chain(dve, sem("d_main"))
            link(nc.vector.tensor_tensor(xc[:, :], xc[:, :], rstd[:, :], ALU.mult))
            dve.wait_ge(sem("ld_a"), 16 * (8 * BP + 1))
            nc.vector.tensor_scalar(u[:, :], xc[:, :], acol[:, 0:1], None, ALU.mult).then_inc(sem("a_u"), 1)
            nc.vector.transpose(a4t[:, :, :].rearrange("p a b -> p (a b)"),
                                a4[:, :, :].rearrange("p a b -> p (a b)")).then_inc(sem("a_w"), 1)
            att_dve(dve, "a_", acol[:, 1:2], bvrow[:, :], table_step)
            dve.wait_ge(sem("c_w"), 1)
            for g in range(BP):
                for j in range(J):
                    last = nc.vector.tensor_copy(gwt[C * g:C * g + C, j, g, j, :], ps[0:C, 1, TAPS * C:TAPS * C + E])
            last.then_inc(sem("c_wd"), 1)
            nc.vector.scalar_tensor_tensor(out=x[:, :], in0=ps[:, 0, :], scalar=acol[:, 3:4], in1=x[:, :],
                                           op0=ALU.add, op1=ALU.add).then_inc(sem("a_x"), 1)
            dve.wait_ge(sem("a_x"), 1)
            if upto == "a":
                dve.sem_inc(sem("out_ready"), 1)
            norm_dve(dve, 2)
            nc.vector.tensor_tensor(u[:, :], xc[:, :], rstd[:, :], ALU.mult).then_inc(sem("b_u"), 1)
            dve.wait_ge(sem("b_u"), 1)
            dve.wait_ge(sem("b_col"), 1)
            pick_op(dve, "d_pick")
            dve.wait_ge(sem("table"), 1)
            recurrent(dve, DVEBody())
            nc.vector.tensor_tensor(x[:, :], x[:, :], u[:, :], ALU.add).then_inc(sem("b_x"), 1)
            dve.wait_ge(sem("b_x"), 1)
            if upto == "b":
                dve.sem_inc(sem("out_ready"), 1)
            dve.wait_ge(sem("zero_c"), 6)
            dve.wait_ge(sem("ld_c"), 64)
            link(nc.vector.tensor_tensor(offb[:, :], boff[:, :], const("base"), ALU.add))
            norm_dve(dve, 3)
            nc.vector.scalar_tensor_tensor(out=xwin[:, :, 2:2 + H, :],
                                           in0=xc[:, :].rearrange("p (j r c) -> p j r c", j=J, r=H), scalar=0.0,
                                           in1=rstd[:, :].rearrange("p (j r c) -> p j r c", j=J, r=H),
                                           op0=ALU.max, op1=ALU.mult).then_inc(sem("c_u"), 1)
            dve.wait_ge(sem("c_u"), 1)
            nc.vector.tensor_copy(xcol[:, 2, :, 2:2 + H, 0:W - 1], xwin[:, :, 2:2 + H, 1:W]).then_inc(sem("c_left"), 1)
            for half in range(2):
                dve.wait_ge(sem("c_om"), 2 * (half + 1))
                nb = NH * BP
                nc.vector.tensor_tensor(om[:, nb * half:nb * half + nb, :],
                                        ps[:, half, 0:nb * OCH].rearrange("p (i o) -> p i o", o=OCH),
                                        offb[:, :].unsqueeze(1).broadcast_to([P, nb, OCH]),
                                        ALU.add).then_inc(sem("c_oms"), 1)
            dve.wait_ge(sem("c_oms"), 2)
            mid = (WROWS - 1) / 2
            link(nc.vector.tensor_scalar(fit[:, :, :], om[:, :, 0:GK], -mid, None, ALU.add))
            nc.vector.tensor_reduce(fitm[:, 0:1], fit[:, :, :], AX.XY, ALU.max,
                                    apply_absolute_value=True).then_inc(sem("c_fitp"), 1)
            dve.wait_ge(sem("c_me"), 1)
            link(nc.vector.tensor_scalar(msk[:, :, :], msk[:, :, :], 1.0, None, ALU.add))
            link(nc.vector.reciprocal(msk[:, :, :], msk[:, :, :]))
            dve.wait_ge(sem("c_fitt"), 1)
            link(nc.vector.tensor_reduce(fitm[0:1, 1:2], ps[0:1, 4, 0:P], AX.X, ALU.max))
            nc.vector.tensor_scalar(fiti[:, :], fitm[0:1, 1:2], mid, None, ALU.is_le).then_inc(sem("c_fit"), 1)
            by_fit(dve, lambda wins: sample_dve(dve, wins))
            dve.wait_ge(sem("ld_d"), 16 * (3 * BP + 2 * B + 2))
            dve.wait_ge(sem("c_out"), 1)
            link(nc.vector.tensor_scalar(y[:, :], ps[:, 7, :], ccol[:, 0:1], None, ALU.add))
            link(nc.vector.bn_stats(stats[:, :], y[:, :]))
            nc.vector.bn_aggr(agg[:, :], stats[:, :]).then_inc(sem("c_agg"), 1)
            dve.wait_ge(sem("c_mu"), 1)
            link(nc.vector.tensor_tensor(bn[:, 0:1], agg[:, 0:1], ps[:, 0, 0:1], ALU.subtract))
            nc.vector.scalar_tensor_tensor(out=bn[:, 1:2], in0=bn[:, 0:1], scalar=bn[:, 0:1], in1=agg[:, 1:2],
                                           op0=ALU.mult, op1=ALU.add).then_inc(sem("c_dev"), 1)
            link(nc.vector.tensor_copy(bn[:, 5:6], ps[:, 0, 0:1]))
            dve.wait_ge(sem("c_rs"), 1)
            link(nc.vector.tensor_tensor(bn[:, 4:5], bn[:, 3:4], ccol[:, 1:2], ALU.mult))
            link(nc.vector.tensor_scalar(y[:, :], y[:, :], bn[:, 5:6], bn[:, 4:5], ALU.subtract, ALU.mult))
            nc.vector.scalar_tensor_tensor(out=x[:, :], in0=y[:, :], scalar=ccol[:, 2:3], in1=x[:, :],
                                           op0=ALU.add, op1=ALU.add).then_inc(sem("c_xn"), 1)
            dve.wait_ge(sem("c_xn"), 1)
            if upto == "c":
                dve.sem_inc(sem("out_ready"), 1)
            norm_dve(dve, 4)
            nc.vector.tensor_tensor(u[:, :], xc[:, :], rstd[:, :], ALU.mult).then_inc(sem("e_u"), 1)
            dve.wait_ge(sem("e_lg"), 1)
            link(nc.vector.tensor_scalar(lg[:, :], ps[:, 0, 0:N], gb[:, 0:1], None, ALU.add))
            link(nc.vector.reduce_max(lnm[:, 2:3], lg[:, :], AX.X))
            nc.vector.tensor_scalar(lnm[:, 0:1], lnm[:, 2:3], -1.0, None, ALU.mult).then_inc(sem("e_max"), 1)
            dve.wait_ge(sem("e_ex"), 1)
            link(nc.vector.reciprocal(lnm[:, 3:4], lnm[:, 1:2]))
            link(nc.vector.tensor_scalar(pr[:, :], pr[:, :], lnm[:, 3:4], None, ALU.mult))
            link(nc.vector.max(ptop[:, :], pr[:, :]))
            link(nc.vector.match_replace(rest[:, :], ptop[:, :], pr[:, :], -1.0))
            nc.vector.scalar_tensor_tensor(out=pm[:, :], in0=rest[:, :], scalar=0.0, in1=pr[:, :],
                                           op0=ALU.is_lt, op1=ALU.mult).then_inc(sem("e_pm"), 1)
            dve.wait_ge(sem("e_pmt"), 1)
            nc.vector.tensor_copy(pmT[:, :, :].rearrange("p h n -> p (h n)"), ps[:, 2, 0:NH * P]).then_inc(sem("e_pmts"), 1)
            dve.wait_ge(sem("e_pool"), 1)
            for g in range(BP):
                span = J * (P + E)
                own = ps[C * g:C * g + C, 3, J * E * g:J * E * g + span].rearrange("c (j n) -> c j n", j=J)[:, :, 0:E]
                nc.vector.tensor_copy(pooled[0:C, :, J * g:J * g + J].rearrange("c e j -> c j e"),
                                      own).then_inc(sem("e_pools"), 1)
            dve.wait_ge(sem("e_o"), 1)
            nc.vector.tensor_copy(eo[:, :, :], ps[0:C, 5, 0:E * B].rearrange("o (e b) -> o b e", b=B)).then_inc(sem("e_os"), 1)
            dve.wait_ge(sem("e_ot"), 1)
            link(nc.vector.tensor_tensor(eoT[:, :], ps[:, 6, 0:C], eb2[:, :], ALU.add))
            nc.vector.tensor_tensor(eol[:, :, :, :].rearrange("p j g o -> p (j g) o"),
                                    eoT[:, :].unsqueeze(1).broadcast_to([P, J * BP, C]),
                                    const("own").unsqueeze(2).broadcast_to([P, J * BP, C]),
                                    ALU.mult).then_inc(sem("e_ol"), 1)
            dve.wait_ge(sem("e_y"), 1)
            nc.vector.tensor_tensor(fin[:, :], ps[:, 7, :], x[:, :], ALU.add).then_inc(sem("fin"), 1)
            dve.wait_ge(sem("fin"), 1)
            if upto == "all":
                dve.sem_inc(sem("out_ready"), 1)


def kernel(**inputs):
    import concourse.bacc as _bacc
    from concourse.bass_utils import run_bass_kernel_spmd as _run

    nc = _bacc.Bacc("TRN2", target_bir_lowering=False, num_devices=1)
    inputs = dict(inputs)
    cst, _ = constants()
    arrays, aps = {}, {}
    inputs["cst"], inputs["codes"] = cst, step_codes()
    for name, v in inputs.items():
        v = np.ascontiguousarray(v)
        if v.dtype == np.bool_:
            v = v.astype(np.int32).reshape(1, -1)
        elif name.startswith("L0_ffn_"):
            v = v.reshape((STEPS * OPS,) + v.shape[2:])
        arrays[f"in_{name}"] = v
        aps[name] = nc.dram_tensor(f"in_{name}", v.shape, mybir.dt.from_np(v.dtype), kind="ExternalInput").ap()
    out = nc.dram_tensor("out", (B, C, H, W), f32, kind="ExternalOutput").ap()
    metaformer_kernel(nc, aps, out, UPTO)
    return _run(nc, [arrays], core_ids=[0]).results[0]["out"]


UPTO = "all"
```

```python
import concourse.bass as bass
from concourse import mybir
from contextlib import ExitStack
import numpy as np

B, C, H, W = 8, 32, 16, 16
N = H * W
P = 128
BP = P // C
J = B // BP
F = J * N
NH = N // P
STEPS, OPS = 33, 19
HID = 128
DG, K = 2, 3
TAPS = K * K
CG = C // DG
GK = DG * TAPS
OCH = 3 * GK
E, TOPK = 16, 8
QSCALE = float(C) ** -0.5
NEST = (4, 3, 3)
assert NEST[0] * NEST[1] * NEST[2] >= STEPS + 1
NONE = 4 * STEPS
TPAD = 32
OMBANK = (4, 7)
WROWS = 8
NWIN = 4
BLK = 64
FIRST, REST = slice(0, 1), slice(1, F)
FILL = 5
OPAD = 64
XROWS = H + 4
K3 = 3

f32 = mybir.dt.float32
i32 = mybir.dt.int32
u32 = mybir.dt.uint32
ALU = mybir.AluOpType
ACT = mybir.ActivationFunctionType
AX = mybir.AxisListType


def constants():
    p = np.arange(P)
    cols = {}
    cols["ident"] = np.eye(P)
    cols["mean"] = (p[:, None] // C == p[None, :] // C) / C
    cols["fold"] = (p[:, None] % C == p[None, :] % C) / BP
    k = np.arange(TAPS)
    row, col = p // W, p % W
    by = (row % 4)[:, None] + 1 + (k // K)[None, :]
    bx = col[:, None] - 1 + (k % K)[None, :]
    cols["base"] = np.concatenate([by, by, bx, bx, np.zeros((P, GK))], 1)
    cols["grid"] = np.broadcast_to(np.arange(W), (P, W))
    lead = [[(4 * ((8 * h + row) // 4) - 2)[:, None] for _ in range(2)] for h in range(NH)]
    cols["wide"] = np.concatenate(
        [np.arange(WROWS)[None, :] + WROWS * w - lead[h][w] for h in range(NH) for w in range(2)], 1)
    be = np.arange(P) // E
    cols["own"] = np.concatenate([(be[:, None] == J * np.arange(BP)[None, :] + j) for j in range(J)], 1)
    cols["eps"] = np.broadcast_to(np.array([1e-6, 1e-5]), (P, 2))
    at, off = {}, 0
    for name, a in cols.items():
        at[name] = (off, off + a.shape[1])
        off += a.shape[1]
    return np.concatenate([np.asarray(a, np.float32) for a in cols.values()], 1), at


def step_codes():
    return np.broadcast_to(4 * np.arange(STEPS)[None, :] - NONE, (OPS, STEPS)).astype(np.float32)


class Chain:

    def __init__(self, eng, sem):
        self.eng, self.sem, self.n = eng, sem, 0

    def __call__(self, ins):
        self.n += 1
        ins.then_inc(self.sem, 1)
        self.eng.wait_ge(self.sem, self.n)


def metaformer_kernel(nc, a, out, upto="all"):
    _, CA = constants()
    NCST = max(e for _, e in CA.values())
    ctx = ExitStack()

    def sb(name, shape, dt=f32):
        return ctx.enter_context(nc.sbuf_tensor(name, shape, dt))

    sems = {}

    def sem(name):
        if name not in sems:
            sems[name] = ctx.enter_context(nc.semaphore(name))
        return sems[name]

    with ctx:
        cst = sb("cst", [P, NCST])

        def const(name):
            return cst[:, CA[name][0]:CA[name][1]]

        ident, meanm, fold = const("ident"), const("mean"), const("fold")
        zero = cst[:, CA["base"][1] - 1:CA["base"][1]]
        eps6, eps5 = cst[:, CA["eps"][0]:CA["eps"][0] + 1], cst[:, CA["eps"][0] + 1:CA["eps"][1]]
        x = sb("x", [P, F])
        u = sb("u", [P, F])
        xc = sb("xc", [P, F])
        sq = sb("sq", [P, F])
        rstd = sb("rstd", [P, F])
        a4 = sb("a4", [P, 4, C])
        a4s = sb("a4s", [P, 4, C])
        a4t = sb("a4t", [P, 4, P])
        r4 = sb("r4", [P, 4, P])
        acol = sb("acol", [P, 4])
        bqs = sb("bqs", [P, 1])
        bvrow = sb("bvrow", [P, C])
        q_sb = sb("q_sb", [P, BP, F])
        k_sb = sb("k_sb", [P, F])
        v_sb = sb("v_sb", [P, J * NH, P])
        negmax = sb("negmax", [P, B, NH])
        rowsum = sb("rowsum", [P, B, NH])
        rinv = sb("rinv", [P, B, NH])
        att = sb("att", [P, F])
        masks = sb("masks", [OPS, 2, STEPS], i32)
        codes = sb("codes", [OPS, STEPS])
        table = sb("table", [OPS, 2, STEPS + TPAD])
        nexts_op = sb("nexts_op", [OPS, STEPS + 1], i32)
        nexts = sb("nexts", [1, OPS * (STEPS + 1)], i32)
        top = sb("top", [1, 8])
        topi = sb("topi", [1, 8], u32)
        rs4 = sb("rs4", [P, 4, C])
        w1 = sb("w1", [P, HID])
        w2b1 = sb("w2b1", [HID, C + 1])
        w2, b1 = w2b1[:, 0:C], w2b1[:, C:C + 1]
        b2 = sb("b2", [P, 1])
        woff_n = sb("woff_n", [OCH, C * TAPS])
        wc_n = sb("wc_n", [C, C * TAPS])
        woff = sb("woff", [P, K, OPAD])
        omc = sb("omc", [P, J, F])
        wc = sb("wc", [P, TAPS, BP, C])
        ccol = sb("ccol", [P, 3])
        boff = sb("boff", [P, OCH])
        offb = sb("offb", [P, OCH])
        xwin = sb("xwin", [P, J, XROWS, W])
        xs = sb("xs", [P, J, BP, XROWS, W])
        xt = sb("xt", [P, J, DG, NWIN, BP, C])
        om = sb("om", [P, J * NH * BP, OCH])
        msk = sb("msk", [P, J * NH * BP, GK])
        fit = sb("fit", [P, J * NH * BP, GK])
        fitm = sb("fitm", [P, 4])
        fiti = sb("fiti", [1, 1], i32)
        ty = sb("ty", [P, 2, J * NH, GK, BP, WROWS])
        tx = sb("tx", [P, J * NH, GK, BP, W])
        disty = sb("disty", [P, 2, BP, GK, WROWS])
        distx = sb("distx", [P, 2, BP, GK, W])
        smat = sb("smat", [P, 3, K3 * BP, P])
        smatT = sb("smatT", [P, 2, K3, BP, P])
        early = smat[:, :, :, :].rearrange("p r u n -> p (r u n)")
        probs = early[:, 0:2 * F].rearrange("p (r h m) -> p r h m", r=2, h=NH)
        probsT = early[:, 2 * F:4 * F].rearrange("p (r h m) -> p r h m", r=2, h=NH)
        relu = smatT[:, :, :, :, :].rearrange("p r k g n -> p (r k g n)")[:, 0:BP * F].rearrange(
            "p (g n) -> p g n", g=BP)
        samp = sb("samp", [P, 2, K3, P])
        y = sb("y", [P, F])
        stats = sb("stats", [P, 6])
        agg = sb("agg", [P, 2])
        bn = sb("bn", [P, 6])
        gw_n = sb("gw_n", [E, C])
        gwt = sb("gwt", [P, J, BP, J, E])
        gb = sb("gb", [P, 1])
        ew1 = sb("ew1", [C + 1, E, HID])
        ew2 = sb("ew2", [HID, E, C])
        eb2 = sb("eb2", [P, C])
        lg = sb("lg", [P, N])
        pr = sb("pr", [P, N])
        ltop = sb("ltop", [P, 8])
        lnm = sb("lnm", [P, 4])
        ptop = sb("ptop", [P, 8])
        rest = sb("rest", [P, N])
        pm = sb("pm", [P, N])
        pmT = sb("pmT", [P, NH, P])
        ut = sb("ut", [P, J * NH, P])
        pooled = sb("pooled", [C + 1, E, B])
        hid = sb("hid", [HID, E, B])
        eo = sb("eo", [C, B, E])
        eoT = sb("eoT", [P, C])
        eol = sb("eol", [P, J, BP, C])
        fin = sb("fin", [P, F])
        ps = ctx.enter_context(nc.psum_tensor("ps", [P, 8, 512], f32))

        LOOP = ["l_w1", "l_w2", "l_attn_w", "l_col", "l_done", "l_hid", "l_relu_act", "l_relu_dve", "l_ffn", "l_h"]
        ATT = ["w", "proj", "q", "q1", "k", "v", "sc", "mx", "ex", "nrm", "pt", "pts", "av", "att", "wo", "fin", "dchain",
               "achain"]
        for n in LOOP:
            sem(n)
        for n in ATT:
            sem("r_" + n)
        loop_sems = range(sem(LOOP[0]).num, sem("r_" + ATT[-1]).num + 1)
        assert len(loop_sems) == len(LOOP) + len(ATT)
        for n in ("l_pick", "go_pe", "go_act", "go_sp"):
            sem(n)

        block = ctx.enter_context(nc.Block())

        def dr(name):
            return a[name]

        def every_pair(ap):
            return ap.unsqueeze(0).broadcast_to([BP, *ap.shape])

        def att_pe(pe, px, weights, between=None):
            S = lambda n: sem(px + n)
            wq_, wk_, wv_, wo_ = weights
            nc.tensor.matmul(ps[:, 0, :], wq_, u[:, :], start=True, stop=True).then_inc(S("proj"), 1)
            nc.tensor.matmul(ps[:, 1, :], wk_, u[:, :], start=True, stop=True).then_inc(S("proj"), 1)
            for i in range(J * NH):
                last = nc.tensor.matmul(ps[:, 2, i * P:(i + 1) * P], u[:, i * P:(i + 1) * P], wv_,
                                        start=True, stop=True)
            last.then_inc(S("proj"), 1)

            def scores(t):
                bp, j = t % BP, t // BP
                if t >= 2:
                    pe.wait_ge(S("ex"), 2 * (t - 1))
                pe.wait_ge(S("q1") if j else S("q"), bp + 1)
                pe.wait_ge(S("k"), j + 1)
                for h in range(NH):
                    q0 = j * N + h * P
                    last = nc.tensor.matmul(ps[:, 3 + t % 2, h * N:(h + 1) * N], q_sb[:, bp, q0:q0 + P],
                                            k_sb[:, j * N:(j + 1) * N], start=True, stop=True)
                last.then_inc(S("sc"), 1)

            def transposes(t):
                pe.wait_ge(S("nrm"), t + 1)
                if t >= 2:
                    pe.wait_ge(S("pts"), t - 1)
                for mh in range(NH):
                    for h in range(NH):
                        last = nc.tensor.transpose(ps[:, 5 + t % 2, mh * N + h * P:mh * N + (h + 1) * P],
                                                   probs[:, t % 2, h, mh * P:(mh + 1) * P], ident)
                last.then_inc(S("pt"), 1)

            def values(t):
                bp, j = t % BP, t // BP
                pe.wait_ge(S("pts"), t + 1)
                if t == 0:
                    pe.wait_ge(S("v"), 1)
                for mh in range(NH):
                    last = nc.tensor.matmul(ps[C * bp:C * bp + C, 7, j * N:(j + 1) * N],
                                            v_sb[:, j * NH + mh, C * bp:C * bp + C], probsT[:, t % 2, mh, :],
                                            start=(mh == 0), stop=(mh == NH - 1))
                last.then_inc(S("av"), 1)

            scores(0)
            scores(1)
            for t in range(B + 1):
                if between and t == BP - 1:
                    pe.wait_ge(S("q1"), BP)
                    between()
                if t + 2 < B:
                    scores(t + 2)
                if t < B:
                    transposes(t)
                if t >= 1:
                    values(t - 1)
            keep_clock(2, 3)
            pe.wait_ge(S("att"), 1)
            if between:
                pe.wait_ge(sem("c_wa"), BP + K)
            nc.tensor.matmul(ps[:, 0, :], wo_, att[:, :], start=True, stop=True).then_inc(S("wo"), 1)
            keep_clock(3, 7)

        def att_act(act, px, bq, bk, between=None):
            S = lambda n: sem(px + n)
            act.wait_ge(S("proj"), 2)
            for j in range(J):
                nc.scalar.activation(k_sb[:, j * N:j * N + N], ps[:, 1, j * N:j * N + N], ACT.Identity,
                                     bias=bk).then_inc(S("k"), 1)
            for t in range(B):
                if t < BP:
                    rows = slice(C * t, C * t + C)
                    act.wait_ge(S("q"), t + 1)
                    nc.scalar.activation(q_sb[rows, t, N:], ps[rows, 0, N:], ACT.Identity, scale=QSCALE,
                                         bias=bq if isinstance(bq, float) else bq[rows, :]).then_inc(S("q1"), 1)
                act.wait_ge(S("mx"), t + 1)
                if t >= 2:
                    act.wait_ge(S("pt"), t - 1)
                for h in range(NH):
                    nc.scalar.activation(probs[:, t % 2, h, :], ps[:, 3 + t % 2, h * N:(h + 1) * N], ACT.Exp,
                                         bias=negmax[:, t, h:h + 1],
                                         accum_out=rowsum[:, t, h:h + 1]).then_inc(S("ex"), 1)
                if t >= 1:
                    copy_probs(act, S, t - 1)
                if between:
                    between(t)
            copy_probs(act, S, B - 1)

        def copy_probs(act, S, t):
            act.wait_ge(S("pt"), t + 1)
            if t >= 2:
                act.wait_ge(S("av"), t - 1)
            nc.scalar.activation(probsT[:, t % 2, :, :], ps[:, 5 + t % 2, :], ACT.Copy).then_inc(S("pts"), 1)

        def table_of_steps(link):
            am, fm_ = masks[:, 0, :], masks[:, 1, :]
            t0, t1 = table[:, 0, :], table[:, 1, :]
            link.eng.wait_ge(sem("ld_m"), 48)
            link(nc.vector.memset(table[:, :, STEPS:], 0.0))
            link(nc.vector.tensor_tensor(t1[:, 0:STEPS], am, fm_, ALU.max))
            link(nc.vector.scalar_tensor_tensor(out=t0[:, 0:STEPS], in0=am, scalar=2.0, in1=codes[:, :],
                                                op0=ALU.mult, op1=ALU.add))
            link(nc.vector.tensor_tensor(t0[:, 0:STEPS], t0[:, 0:STEPS], fm_, ALU.add))
            link(nc.vector.tensor_tensor(t0[:, 0:STEPS], t0[:, 0:STEPS], t1[:, 0:STEPS], ALU.mult))
            for n in range(6):
                d, (src_, dst) = 1 << n, ((t0, t1) if n % 2 == 0 else (t1, t0))
                link(nc.vector.tensor_tensor(dst[:, 0:STEPS], src_[:, 0:STEPS], src_[:, d:d + STEPS], ALU.min))
            nc.vector.tensor_scalar(nexts_op[:, :], t0[:, 0:STEPS + 1], float(NONE), None,
                                    ALU.add).then_inc(sem("table_op"), 1)

        def att_dve(dve, px, bq, bv):
            S = lambda n: sem(px + n)
            link = Chain(dve, S("dchain"))
            dve.wait_ge(sem("ld_cst"), 16)
            dve.wait_ge(S("proj"), 1)
            for g in range(BP):
                rows = slice(C * g, C * g + C)
                nc.vector.tensor_scalar(q_sb[rows, g, 0:N], ps[rows, 0, 0:N], bq[rows, :], QSCALE,
                                        ALU.add, ALU.mult).then_inc(S("q"), 1)
            dve.wait_ge(S("proj"), 3)
            if bv is None:
                nc.vector.tensor_copy(v_sb[:, :, :], ps[:, 2, :]).then_inc(S("v"), 1)
            else:
                nc.vector.tensor_tensor(v_sb[:, :, :].rearrange("p i (g c) -> p (i g) c", c=C),
                                        ps[:, 2, :].rearrange("p (i c) -> p i c", c=C),
                                        bv.unsqueeze(1).broadcast_to([P, J * NH * BP, C]),
                                        ALU.add).then_inc(S("v"), 1)

            def maxima(t):
                dve.wait_ge(S("sc"), t + 1)
                nc.vector.tensor_reduce(negmax[:, t, :], ps[:, 3 + t % 2, :].rearrange("p (h m) -> p h m", h=NH),
                                        AX.X, ALU.max, negate=True).then_inc(S("mx"), 1)

            maxima(0)
            maxima(1)
            for t in range(B):
                dve.wait_ge(S("ex"), 2 * (t + 1))
                link(nc.vector.reciprocal(rinv[:, t, :], rowsum[:, t, :]))
                for h in range(NH):
                    ins = nc.vector.tensor_scalar(probs[:, t % 2, h, :], probs[:, t % 2, h, :],
                                                  rinv[:, t, h:h + 1], None, ALU.mult)
                ins.then_inc(S("nrm"), 1)
                if t + 2 < B:
                    maxima(t + 2)
            dve.wait_ge(S("av"), B)
            nc.vector.tensor_copy(att[:, :], ps[:, 7, :]).then_inc(S("att"), 1)
            dve.wait_ge(S("wo"), 1)

        def keep_clock(n, bank, weights=ident, data=cst[:, 0:N]):
            for _ in range(n):
                nc.tensor.matmul(ps[:, bank, 0:N], weights, data, start=True, stop=True)

        def norm_pe(pe, i, bank):
            nc.tensor.matmul(ps[:, 5, :], meanm, x[:, :], start=True, stop=True).then_inc(sem("norm_mean"), 1)
            keep_clock(4, bank)
            pe.wait_ge(sem("norm_sq"), i)
            nc.tensor.matmul(ps[:, 6, :], meanm, sq[:, :], start=True, stop=True).then_inc(sem("norm_var"), 1)
            keep_clock(5, bank)

        def norm_act(act, i, eps):
            act.wait_ge(sem("norm_xc"), i)
            nc.scalar.activation(sq[:, :], xc[:, :], ACT.Square).then_inc(sem("norm_sq"), 1)
            act.wait_ge(sem("norm_var"), i)
            nc.scalar.activation(rstd[:, :], ps[:, 6, :], ACT.Ln, bias=eps).then_inc(sem("norm_ln"), 1)
            act.wait_ge(sem("norm_ln"), i)
            nc.scalar.activation(rstd[:, :], rstd[:, :], ACT.Exp, scale=-0.5).then_inc(sem("norm_rstd"), 1)

        def deviations(dve, i):
            dve.wait_ge(sem("norm_mean"), i)
            nc.vector.tensor_tensor(xc[:, :], x[:, :], ps[:, 5, :], ALU.subtract).then_inc(sem("norm_xc"), 1)

        def norm_dve(dve, i):
            deviations(dve, i)
            dve.wait_ge(sem("norm_rstd"), i)

        def recurrent(eng, body):
            cur = eng.alloc_register("cur")
            op = eng.alloc_register("op")
            code = eng.alloc_register("code")
            at = eng.alloc_register("at")
            wi = eng.alloc_register("wi")
            has_att = eng.alloc_register("has_att")
            has_ffn = eng.alloc_register("has_ffn")
            eng.reg_mov(cur, 0)
            with eng.Fori(0, NEST[0]), eng.If_cmp(cur, STEPS + 1, "IS_LT"), \
                    eng.Fori(0, NEST[1]), eng.If_cmp(cur, STEPS + 1, "IS_LT"), eng.Fori(0, NEST[2]):
                with eng.If_cmp(cur, STEPS + 1, "IS_LT"):
                    body.start(eng)
                    eng.load(op, topi[0:1, 0:1])
                    eng.reg_mul(at, op, STEPS + 1)
                    eng.reg_add(at, at, cur)
                    ati = eng.snap(at, min_val=0, max_val=OPS * (STEPS + 1) - 1)
                    eng.load(code, nexts[0:1, bass.ds(ati, 1)])
                    eng.reg_alu(cur, code, 2, ALU.logical_shift_right)
                    eng.reg_mul(wi, cur, OPS)
                    eng.reg_add(wi, wi, op)
                    eng.reg_add(cur, cur, 1)
                    eng.reg_alu(has_ffn, code, 1, ALU.bitwise_and)
                    eng.reg_alu(has_att, code, 2, ALU.bitwise_and)
                    with eng.If_cmp(code, NONE, "IS_LT"):
                        with eng.If_cmp(has_att, 0, "IS_NE"):
                            body.attention(eng, wi)
                        with eng.If_cmp(has_ffn, 0, "IS_NE"):
                            body.ffn(eng, wi)
                        body.end(eng)
                    with eng.If_cmp(code, NONE, "IS_GE"):
                        body.finish(eng)

        class SPBody:
            def start(self, sp):
                sp.wait_ge(sem("go_sp"), 1)
                sp.sem_clear(sem("go_sp"))

            def attention(self, sp, wi):
                i = sp.snap(wi, min_val=0, max_val=STEPS * OPS - 1)
                w4 = dr("L0_ffn_w4")[bass.ds(i, 1), :, :].rearrange("o c d -> (o c) d")
                sp.dma_start(rs4[:, :, :].rearrange("p a c -> p (a c)"), every_pair(w4)).then_inc(sem("l_attn_w"), 16)

            def ffn(self, sp, wi):
                i = sp.snap(wi, min_val=0, max_val=STEPS * OPS - 1)
                step = lambda name: dr("L0_ffn_ffn_" + name)[bass.ds(i, 1)]
                sp.dma_start(w1[:, :], every_pair(step("w1").rearrange("o c d -> (o c) d"))).then_inc(sem("l_w1"), 16)
                sp.dma_start(w2b1[:, :], step("w2b1").rearrange("o c d -> (o c) d")).then_inc(sem("l_w2"), 16)
                sp.dma_start(b2[:, :], every_pair(step("b2").rearrange("o (c k) -> (o c) k", k=1))).then_inc(sem("l_w2"), 16)

            def end(self, sp):
                sp.sem_inc(sem("l_done"), 1)

            def finish(self, sp):
                pass

        class PEBody:
            def start(self, pe):
                keep_clock(3, 7)
                pe.wait_ge(sem("go_pe"), 1)
                pe.sem_clear(sem("go_pe"))

            def attention(self, pe, wi):
                keep_clock(4, 7)
                pe.wait_ge(sem("r_w"), 1)
                att_pe(pe, "r_", [r4[:, n, :] for n in range(4)])
                pe.wait_ge(sem("r_fin"), 1)

            def ffn(self, pe, wi):
                keep_clock(FILL, 7)
                pe.wait_ge(sem("l_w1"), 16)
                for g in range(BP):
                    rows = slice(C * g, C * g + C)
                    nc.tensor.matmul(ps[:, g, :], w1[rows, :], u[rows, :],
                                     start=True, stop=True).then_inc(sem("l_hid"), 1)
                pe.wait_ge(sem("l_w2"), 32)
                for g in range(BP):
                    pe.wait_ge(sem("l_relu_dve" if g % 2 else "l_relu_act"), g // 2 + 1)
                    last = nc.tensor.matmul(ps[C * g:C * g + C, 4, :], w2, relu[:, g, :],
                                            start=True, stop=True)
                last.then_inc(sem("l_ffn"), 1)
                pe.wait_ge(sem("l_h"), 1)

            def end(self, pe):
                nc.tensor.matmul(ps[0:1, 5, 0:C], u[0:C, 0:1], ident[0:C, 0:C],
                                 start=True, stop=True).then_inc(sem("l_col"), 1)

            def finish(self, pe):
                keep_clock(1, 7)
                pe.wait_ge(sem("b_x"), 1)
                norm_pe(pe, 3, 7)

        class ACTBody:
            def start(self, act):
                act.wait_ge(sem("go_act"), 1)
                act.sem_clear(sem("go_act"))

            def attention(self, act, wi):
                att_act(act, "r_", 0.0, 0.0)

            def ffn(self, act, wi):
                act.wait_ge(sem("l_w2"), 32)
                for g in (0, 2):
                    act.wait_ge(sem("l_hid"), g + 1)
                    nc.scalar.activation(relu[:, g, :], ps[:, g, :], ACT.Relu,
                                         bias=b1).then_inc(sem("l_relu_act"), 1)

            def end(self, act):
                act.sem_inc(sem("l_done"), 1)

            def finish(self, act):
                norm_act(act, 3, eps6)

        class DVEBody:
            def start(self, dve):
                pass

            def attention(self, dve, wi):
                dve.wait_ge(sem("l_attn_w"), 16)
                dve.wait_ge(sem("zero_r4"), 1)
                for g in range(BP):
                    rows = slice(C * g, C * g + C)
                    last = nc.vector.tensor_copy(r4[rows, :, rows], rs4[rows, :, :])
                last.then_inc(sem("r_w"), 1)
                att_dve(dve, "r_", zero, None)
                nc.vector.tensor_copy(u[:, :], ps[:, 0, :]).then_inc(sem("r_fin"), 1)
                dve.wait_ge(sem("r_fin"), 1)

            def ffn(self, dve, wi):
                dve.wait_ge(sem("l_w2"), 32)
                for g in (1, 3):
                    dve.wait_ge(sem("l_hid"), g + 1)
                    nc.vector.tensor_scalar(relu[:, g, :], ps[:, g, :], b1, 0.0,
                                            ALU.add, ALU.max).then_inc(sem("l_relu_dve"), 1)
                dve.wait_ge(sem("l_ffn"), 1)
                for cols in (FIRST, REST):
                    nc.vector.tensor_scalar(u[:, cols], ps[:, 4, cols], b2[:, 0:1], None,
                                            ALU.add).then_inc(sem("l_h"), 1)
                dve.wait_ge(sem("l_h"), 2)

            def end(self, dve):
                dve.wait_ge(sem("l_col"), 1)
                dve.wait_ge(sem("l_done"), 2)
                dve.sem_clear(loop_sems)
                pick_op(dve, "l_pick")
                dve.sem_clear(sem("l_pick"))

            def finish(self, dve):
                nc.vector.tensor_tensor(x[:, :], x[:, :], u[:, :], ALU.add).then_inc(sem("b_x"), 1)
                deviations(dve, 3)

        def pick_op(dve, name):
            link = Chain(dve, sem(name))
            link(nc.vector.max(top[:, :], ps[0:1, 5, 0:OPS]))
            link(nc.vector.max_index(topi[:, :], top[:, :], ps[0:1, 5, 0:OPS]))
            dve.sem_inc(sem("go_pe"), 1)
            dve.sem_inc(sem("go_act"), 1)
            dve.sem_inc(sem("go_sp"), 1)

        def sample_steps(wins):
            return [(jh, k3, g, w) for jh in range(J * NH) for k3 in range(TAPS // K3)
                    for g in range(DG) for w in range(len(wins))]

        def by_act(bp, k):
            return (bp * K + k) % 2 == 0

        def copies(j, eng):
            return (j + 1) * sum(by_act(g, k) == (eng == 0) for g in range(BP) for k in range(K))

        def spread(eng_copy, j, eng, done):
            for bp in range(BP):
                for k in range(K):
                    if by_act(bp, k) == (eng == 0):
                        to, frm, n = max(0, 1 - k), max(0, k - 1), W - abs(k - 1)
                        eng_copy(xs[C * k:C * k + C, j, bp, 2:2 + H, to:to + n],
                                 xwin[C * bp:C * bp + C, j, 2:2 + H, frm:frm + n]).then_inc(sem(done), 1)

        def by_fit(eng, run):
            eng.wait_ge(sem("c_fit"), 1)
            fits = eng.alloc_register("fits")
            eng.load(fits, fiti[0:1, 0:1])
            with eng.If_cmp(fits, 0, "IS_NE"):
                run((None,))
            with eng.If_cmp(fits, 0, "IS_EQ"):
                run((0, 1))

        def on_pool(n):
            return n % 4 == 3

        def weigh(eng, wins, n, step):
            jh, k3, g, w = step
            if n >= 3:
                eng.wait_ge(sem("s_tr"), n - 2)
            ks = slice(g * TAPS + K3 * k3, g * TAPS + K3 * k3 + K3)
            rows = ty[:, w, jh, ks, :, :].rearrange("p k g r -> p (k g) r")
            colw = tx[:, jh, ks, :, :].rearrange("p k g r -> p (k g) r")
            shape = [P, K3 * BP, WROWS, W]
            return eng.tensor_tensor(smat[:, n % 3, :, :].rearrange("p u (r c) -> p u r c", c=W),
                                     rows.unsqueeze(3).broadcast_to(shape), colw.unsqueeze(2).broadcast_to(shape),
                                     ALU.mult)

        def sample_pool(pool, wins):
            nw = len(wins)
            for n, step in enumerate(sample_steps(wins)):
                if on_pool(n):
                    pool.wait_ge(sem("s_ty"), y_count(nw, step[0], nw - 1) + 1)
                    pool.wait_ge(sem("s_tx"), step[0] + 1)
                    weigh(nc.gpsimd, wins, n, step).then_inc(sem("s_wp"), 1)

        def y_count(nw, jh, w):
            return jh * nw + w + nw - 1

        def distance_y(jh, i, lo):
            shape = [P, BP, GK, WROWS]
            nc.vector.tensor_tensor(disty[:, i % 2, :, :, :],
                                    om[:, BP * jh:BP * jh + BP, 0:GK].unsqueeze(3).broadcast_to(shape),
                                    cst[:, lo:lo + WROWS].unsqueeze(1).unsqueeze(1).broadcast_to(shape),
                                    ALU.subtract).then_inc(sem("s_dy"), 1)

        def distance_x(dve, jh):
            if jh >= 2:
                dve.wait_ge(sem("s_tx"), jh - 1)
            shape = [P, BP, GK, W]
            nc.vector.tensor_tensor(distx[:, jh % 2, :, :, :],
                                    om[:, BP * jh:BP * jh + BP, GK:2 * GK].unsqueeze(3).broadcast_to(shape),
                                    const("grid").unsqueeze(1).unsqueeze(1).broadcast_to(shape),
                                    ALU.subtract).then_inc(sem("s_dx"), 1)

        def sigmoid_mask(dve, link, jh):
            dve.wait_ge(sem("c_me"), jh // NH + 1)
            m = msk[:, BP * jh:BP * jh + BP, :]
            link(nc.vector.tensor_scalar(m, m, 1.0, None, ALU.add))
            link(nc.vector.reciprocal(m, m))

        def row_weights(dve, nw, jh, w):
            i = y_count(nw, jh, w)
            dve.wait_ge(sem("s_ay"), i + 1)
            nc.vector.tensor_tensor(ty[:, w, jh, :, :, :].rearrange("p k g r -> p g k r"),
                                    disty[:, i % 2, :, :, :],
                                    msk[:, BP * jh:BP * jh + BP, :].unsqueeze(3).broadcast_to([P, BP, GK, WROWS]),
                                    ALU.mult).then_inc(sem("s_ty"), 1)

        def sample_dve(dve, wins, link):
            nw = len(wins)
            steps = sample_steps(wins)
            per_group = DG * nw
            per_jh = len(steps) // (J * NH)

            def keep(q):
                dve.wait_ge(sem("s_mm"), per_group * (q + 1))
                if q >= 2:
                    dve.wait_ge(sem("s_cv"), q - 1)
                nc.vector.tensor_copy(samp[:, q % 2, :, :], ps[:, 6, 0:K3 * P]).then_inc(sem("s_samp"), 1)

            for n, step in enumerate(steps):
                jh = step[0]
                at_ = n % per_jh
                if nw > 1 and at_ == 0:
                    if jh:
                        sigmoid_mask(dve, link, jh)
                    for w in range(nw):
                        distance_y(jh, y_count(nw, jh, w), CA["wide"][0] + ((jh % NH) * 2 + w) * WROWS)
                        row_weights(dve, nw, jh, w)
                    if jh:
                        distance_x(dve, jh)
                if not on_pool(n):
                    dve.wait_ge(sem("s_ty"), y_count(nw, jh, nw - 1) + 1)
                    dve.wait_ge(sem("s_tx"), jh + 1)
                    weigh(nc.vector, wins, n, step).then_inc(sem("s_wd"), 1)
                if nw == 1 and jh + 1 < J * NH:
                    if at_ == 1:
                        distance_y(jh + 1, y_count(nw, jh + 1, 0), CA["grid"][0])
                    elif at_ == 2:
                        distance_x(dve, jh + 1)
                    elif at_ == 3:
                        sigmoid_mask(dve, link, jh + 1)
                    elif at_ == 4:
                        row_weights(dve, nw, jh + 1, 0)
                if n >= 2 and (n - 1) % per_group == 0:
                    keep((n - 1) // per_group - 1)
            keep(len(steps) // per_group - 1)

        def tent_y(act, i):
            act.wait_ge(sem("s_dy"), i + 1)
            d = disty[:, i % 2, :, :, :]
            nc.scalar.activation(d, d, ACT.Abs).then_inc(sem("s_achain"), 1)
            act.wait_ge(sem("s_achain"), i + 1)
            nc.scalar.activation(d, d, ACT.Relu, bias=1.0, scale=-1.0).then_inc(sem("s_ay"), 1)

        def abs_x(act, jh):
            act.wait_ge(sem("s_dx"), jh + 1)
            d = distx[:, jh % 2, :, :, :]
            nc.scalar.activation(d, d, ACT.Abs).then_inc(sem("s_ax"), 1)

        def relu_x(act, jh):
            act.wait_ge(sem("s_ax"), jh + 1)
            nc.scalar.activation(tx[:, jh, :, :, :].rearrange("p k g r -> p g k r"), distx[:, jh % 2, :, :, :],
                                 ACT.Relu, bias=1.0, scale=-1.0).then_inc(sem("s_tx"), 1)

        def tent_x(act, jh):
            abs_x(act, jh)
            relu_x(act, jh)

        def sample_act(act, wins):
            nw = len(wins)
            steps = sample_steps(wins)
            per_jh = len(steps) // (J * NH)
            for n, step in enumerate(steps):
                jh = step[0]
                if nw > 1 and n % per_jh == 0:
                    for w in range(nw):
                        tent_y(act, y_count(nw, jh, w))
                    if jh:
                        tent_x(act, jh)
                act.wait_ge(sem("s_tr"), n + 1)
                if n >= 2:
                    act.wait_ge(sem("s_mm"), n - 1)
                nc.scalar.activation(smatT[:, n % 2, :, :, :].rearrange("p k g n -> p (k g n)"),
                                     ps[:, 3 * (n % 2):3 * (n % 2) + 3, :].rearrange("p b n -> p (b n)"),
                                     ACT.Copy).then_inc(sem("s_smt"), 1)
                if nw == 1 and jh + 1 < J * NH:
                    if n % per_jh == 1:
                        tent_y(act, y_count(nw, jh + 1, 0))
                    elif n % per_jh == 2:
                        abs_x(act, jh + 1)
                    elif n % per_jh == 3:
                        relu_x(act, jh + 1)

        def sample_pe(pe, wins):
            nw = len(wins)
            steps = sample_steps(wins)
            per_group = DG * nw
            pe.wait_ge(sem("c_xts"), J * DG)
            if nw > 1:
                for j in range(J):
                    for w in range(2):
                        last = nc.tensor.transpose(
                            ps[:, 2 + j, w * P:(w + 1) * P],
                            xwin[:, j, 2 + WROWS * w:2 + WROWS * w + WROWS, :].rearrange("p r c -> p (r c)"), ident)
                last.then_inc(sem("s_xt"), 1)
                pe.wait_ge(sem("s_xts"), J * DG)

            def transposes(n):
                if on_pool(n):
                    pe.wait_ge(sem("s_wp"), n // 4 + 1)
                else:
                    pe.wait_ge(sem("s_wd"), n - (n + 1) // 4 + 1)
                if n >= 2:
                    pe.wait_ge(sem("s_smt"), n - 1)
                for kk in range(K3):
                    for bp in range(BP):
                        last = nc.tensor.transpose(ps[:, 3 * (n % 2) + kk, bp * P:(bp + 1) * P],
                                                   smat[:, n % 3, kk * BP + bp, :], ident)
                last.then_inc(sem("s_tr"), 1)

            def products(n):
                jh, k3, g, w = steps[n]
                j, h = jh // NH, jh % NH
                pe.wait_ge(sem("s_smt"), n + 1)
                first, final = n % per_group == 0, n % per_group == per_group - 1
                if nw == 1:
                    for blk in range(2):
                        for bp in range(BP):
                            o = ps[C * bp:C * bp + C, 6, 0:K3 * P].rearrange("c (k n) -> c k n", k=K3)
                            last = nc.tensor.matmul(o[:, :, blk * BLK:(blk + 1) * BLK],
                                                    xt[:, j, g, 2 * h + blk, bp, :],
                                                    smatT[:, n % 2, :, bp, blk * BLK:(blk + 1) * BLK],
                                                    start=(first and blk == 0), stop=final, skip_group_check=True)
                else:
                    for bp in range(BP):
                        o = ps[C * bp:C * bp + C, 6, 0:K3 * P].rearrange("c (k n) -> c k n", k=K3)
                        last = nc.tensor.matmul(o, xt[:, j, g, w, bp, :], smatT[:, n % 2, :, bp, :],
                                                start=first, stop=final, skip_group_check=True)
                last.then_inc(sem("s_mm"), 1)

            def convolve(q):
                jh, k3 = q // (TAPS // K3), q % (TAPS // K3)
                pe.wait_ge(sem("s_samp"), q + 1)
                for kk in range(K3):
                    tap = K3 * k3 + kk
                    last = nc.tensor.matmul(ps[:, 7, jh * P:(jh + 1) * P], wc[:, tap, :, :].rearrange("p g o -> p (g o)"),
                                            samp[:, q % 2, kk, :], start=(tap == 0), stop=(tap == TAPS - 1))
                last.then_inc(sem("s_cv"), 1)
                return last

            keep_clock(2, 6)
            transposes(0)
            for n in range(len(steps)):
                if n + 1 < len(steps):
                    transposes(n + 1)
                if n and n % per_group == 0:
                    convolve(n // per_group - 1)
                products(n)
            convolve(len(steps) // per_group - 1)
            pe.wait_ge(sem("s_cv"), len(steps) // per_group)
            pe.sem_inc(sem("c_out"), 1)

        def windows(eng_copy, eng, name, nwin, done):
            eng.wait_ge(sem(name), 1)
            for j in range(J):
                for g in range(DG):
                    src_ = ps[:, 2 + j, 0:nwin * P].rearrange("p (w g c) -> p w g c", w=nwin, g=BP)
                    eng_copy(xt[:, j, g, 0:nwin, :, CG * g:CG * g + CG],
                             src_[:, :, :, CG * g:CG * g + CG]).then_inc(sem(done), 1)

        @block.sync
        def _(sp):
            sp.dma_start(x[:, :], dr("x")).then_inc(sem("ld_x"), 16)
            sp.dma_start(cst[:, :], dr("cst")).then_inc(sem("ld_cst"), 16)
            sp.dma_start(a4[:, :, :], every_pair(dr("L0_conv_w4"))).then_inc(sem("ld_a"), 16)
            sp.dma_start(acol[:, :], every_pair(dr("L0_conv_col"))).then_inc(sem("ld_a"), 16)
            sp.dma_start(bvrow[:, :], dr("L0_conv_bv").partition_broadcast(P)).then_inc(sem("ld_a"), 16)
            sp.dma_start(masks[:, 0, :], dr("L0_ffn_attn_mask")).then_inc(sem("ld_m"), 16)
            sp.dma_start(masks[:, 1, :], dr("L0_ffn_ffn_mask")).then_inc(sem("ld_m"), 16)
            sp.dma_start(codes[:, :], dr("codes")).then_inc(sem("ld_m"), 16)
            sp.wait_ge(sem("table_op"), 1)
            sp.dma_start(nexts[0:1, :].rearrange("a (o s) -> a o s", o=OPS), nexts_op[:, :]).then_inc(sem("table"), 16)
            sp.wait_ge(sem("table"), 16)
            recurrent(sp, SPBody())
            sp.wait_ge(sem("out_ready"), 1)
            src = {"a": x, "b": x, "c": x}.get(upto, fin)
            sp.dma_start(out, src[:, :]).then_inc(sem("stored"), 16)
            sp.wait_ge(sem("stored"), 16)

        @block.gpsimd
        def _(pool):
            nc.gpsimd.memset(a4t[:, :, :], 0.0).then_inc(sem("zero_a4"), 1)
            nc.gpsimd.memset(q_sb[:, :, :], 0.0).then_inc(sem("zero_a4"), 1)
            nc.gpsimd.memset(r4[:, :, :], 0.0).then_inc(sem("zero_r4"), 1)
            pool.dma_start(woff_n[:, :], dr("L1_conv_w_off").rearrange("o c a b -> o (c a b)")).then_inc(sem("ld_c"), 16)
            pool.dma_start(wc_n[:, :], dr("L1_conv_w").rearrange("o c a b -> o (c a b)")).then_inc(sem("ld_c"), 16)
            pool.dma_start(gw_n[:, :], dr("L1_ffn_gate_w")).then_inc(sem("ld_c"), 16)
            pool.dma_start(boff[:, :], dr("L1_conv_b_off").partition_broadcast(P)).then_inc(sem("ld_c"), 16)
            nc.gpsimd.memset(xwin[:, :, :, :], 0.0).then_inc(sem("zero_c"), 1)
            nc.gpsimd.memset(woff[:, :, :], 0.0).then_inc(sem("zero_c"), 1)
            nc.gpsimd.memset(wc[:, :, :, :], 0.0).then_inc(sem("zero_c"), 1)
            nc.gpsimd.memset(gwt[:, :, :, :, :], 0.0).then_inc(sem("zero_c"), 1)
            nc.gpsimd.memset(xs[:, :, :, :, :], 0.0).then_inc(sem("zero_c"), 1)
            nc.gpsimd.memset(xt[:, :, :, :, :, :], 0.0).then_inc(sem("zero_c"), 1)
            pool.wait_ge(sem("zero_c"), 6)
            nc.gpsimd.memset(pooled[C:C + 1, :, :], 1.0).then_inc(sem("zero_c"), 1)
            pool.dma_start(ccol[:, :], every_pair(dr("L1_conv_col"))).then_inc(sem("ld_d"), 16)
            pool.dma_start(gb[:, :], dr("L1_ffn_gate_b").rearrange("(e k) -> e k", k=1).unsqueeze(0).broadcast_to(
                [B, E, 1])).then_inc(sem("ld_d"), 16)
            pool.dma_start(ew1[:, :, :], dr("L1_ffn_weight1").rearrange("e d h -> d e h")).then_inc(sem("ld_d"), 16)
            w2_ = dr("L1_ffn_weight2").rearrange("e h o -> h e o")
            pool.dma_start(ew2[:, :, :], w2_[0:HID, :, :]).then_inc(sem("ld_d"), 16)
            pool.dma_start(eb2[:, :], dr("L1_ffn_weight2")[:, HID, :].unsqueeze(0).broadcast_to(
                [B, E, C])).then_inc(sem("ld_d"), 16)
            by_fit(pool, lambda wins: sample_pool(pool, wins))

        @block.scalar
        def _(act):
            nc.scalar.preload_act_table_set("natural_log_exp_and_others")
            act.wait_ge(sem("ld_cst"), 16)
            norm_act(act, 1, eps6)

            def weights_of_3(t):
                if t == BP:
                    act.wait_ge(sem("c_w"), 1)
                    act.wait_ge(sem("zero_c"), 7)
                if t >= BP:
                    g = t - BP
                    rows = slice(C * g, C * g + C)
                    if g < K:
                        taps = ps[0:C, 0, 0:TAPS * OCH].rearrange("c (i k o) -> c k i o", k=K, o=OCH)
                        nc.scalar.activation(woff[rows, :, 0:OCH], taps[:, g, :, :], ACT.Copy).then_inc(sem("c_wa"), 1)
                    nc.scalar.activation(wc[rows, :, g, :], ps[0:C, 1, 0:TAPS * C].rearrange("c (t o) -> c t o", o=C),
                                         ACT.Copy).then_inc(sem("c_wa"), 1)

            act.wait_ge(sem("a_bqs"), 1)
            att_act(act, "a_", bqs, acol[:, 2:3], weights_of_3)
            norm_act(act, 2, eps5)
            act.wait_ge(sem("table"), 16)
            recurrent(act, ACTBody())
            for j in range(J):
                act.wait_ge(sem("c_u"), j + 1)
                spread(lambda o, i: nc.scalar.activation(o, i, ACT.Copy), j, 0, "c_xsa")

            def channels_first(j):
                act.wait_ge(sem("c_omc"), j + 1)
                nc.scalar.activation(omc[:, j, :], ps[:, j, :], ACT.Copy).then_inc(sem("c_omcs"), 1)

            def exp_mask(j):
                act.wait_ge(sem("c_oms"), j + 1)
                i = slice(NH * BP * j, NH * BP * j + NH * BP)
                nc.scalar.activation(msk[:, i, :], om[:, i, 2 * GK:], ACT.Exp, scale=-1.0).then_inc(sem("c_me"), 1)

            channels_first(0)
            exp_mask(0)
            channels_first(1)
            tent_y(act, 0)
            tent_x(act, 0)
            exp_mask(1)
            windows(lambda o, i: nc.scalar.activation(o, i, ACT.Copy), act, "c_xt", NWIN, "c_xts")

            def run(wins):
                if len(wins) > 1:
                    windows(lambda o, i: nc.scalar.activation(o, i, ACT.Copy), act, "s_xt", 2, "s_xts")
                sample_act(act, wins)
            by_fit(act, run)
            act.wait_ge(sem("c_var"), 1)
            link = Chain(act, sem("a_main"))
            link(nc.scalar.activation(bn[:, 2:3], ps[:, 1, 0:1], ACT.Ln, bias=eps5))
            nc.scalar.activation(bn[:, 3:4], bn[:, 2:3], ACT.Exp, scale=-0.5).then_inc(sem("c_rs"), 1)
            norm_act(act, 4, eps5)
            act.wait_ge(sem("e_ut"), 1)
            nc.scalar.activation(ut[:, :, :].rearrange("p i c -> p (i c)"), ps[:, 1, :], ACT.Copy).then_inc(sem("e_uts"), 1)
            act.wait_ge(sem("e_max"), 1)
            nc.scalar.activation(pr[:, :], lg[:, :], ACT.Exp, bias=lnm[:, 0:1], accum_out=lnm[:, 1:2]).then_inc(sem("e_ex"), 1)
            act.wait_ge(sem("e_h"), 1)
            nc.scalar.activation(hid[:, :, :].rearrange("p e b -> p (e b)"), ps[:, 4, 0:E * B], ACT.Gelu).then_inc(sem("e_hid"), 1)

        @block.tensor
        def _(pe):
            pe.wait_ge(sem("zero_a4"), 1)
            keep_clock(4, 7, a4t[:, 0, :], a4t[:, 0:2, :].rearrange("p a n -> p (a n)"))
            pe.wait_ge(sem("ld_x"), 16)
            pe.wait_ge(sem("ld_cst"), 16)
            norm_pe(pe, 1, 7)
            pe.wait_ge(sem("a_u"), 1)
            pe.wait_ge(sem("a_w"), 1)

            def weights_of_3():
                pe.wait_ge(sem("ld_c"), 64)
                for tap in range(TAPS):
                    nc.tensor.transpose(ps[0:C, 0, tap * OCH:(tap + 1) * OCH], woff_n[:, tap::TAPS], ident[0:OCH, 0:OCH])
                for tap in range(TAPS):
                    nc.tensor.transpose(ps[0:C, 1, tap * C:(tap + 1) * C], wc_n[:, tap::TAPS], ident[0:C, 0:C])
                nc.tensor.transpose(ps[0:C, 1, TAPS * C:TAPS * C + E], gw_n[:, :], ident[0:E, 0:E]).then_inc(sem("c_w"), 1)

            att_pe(pe, "a_", [a4t[:, n, :] for n in range(4)], weights_of_3)
            pe.wait_ge(sem("a_x"), 1)
            norm_pe(pe, 2, 7)
            pe.wait_ge(sem("b_u"), 1)
            nc.tensor.matmul(ps[0:1, 5, 0:C], u[0:C, 0:1], ident[0:C, 0:C], start=True, stop=True).then_inc(sem("b_col"), 1)
            pe.wait_ge(sem("table"), 16)
            recurrent(pe, PEBody())
            pe.wait_ge(sem("c_wd"), 1)

            def positions_first(j):
                pe.wait_ge(sem("c_omcs"), j + 1)
                for h in range(NH):
                    for i in range(2):
                        c0 = i * N + h * P
                        last = nc.tensor.transpose(ps[:, OMBANK[j], (2 * h + i) * P:(2 * h + i + 1) * P],
                                                   omc[:, j, c0:c0 + P], ident)
                last.then_inc(sem("c_om"), 1)

            keep_clock(3, 7)
            for j in range(J):
                pe.wait_ge(sem("c_xsa"), copies(j, 0))
                pe.wait_ge(sem("c_xsd"), copies(j, 1))
                for ki in range(K):
                    for s in range(2):
                        last = nc.tensor.matmul(ps[OPAD * s:OPAD * s + OPAD, j, :], woff[:, ki, :],
                                                xs[:, j, s::2, ki + 1:ki + 1 + H, :].rearrange("p g r c -> p g (r c)"),
                                                start=(ki == 0), stop=(ki == K - 1))
                    if j == 1 and ki == 0:
                        positions_first(0)
                last.then_inc(sem("c_omc"), 1)
            pe.wait_ge(sem("c_u"), J)
            for j in range(J):
                for w in range(NWIN):
                    last = nc.tensor.transpose(ps[:, 2 + j, w * P:(w + 1) * P],
                                               xwin[:, j, 4 * w:4 * w + WROWS, :].rearrange("p r c -> p (r c)"), ident)
            last.then_inc(sem("c_xt"), 1)
            positions_first(1)
            keep_clock(3, 6)
            pe.wait_ge(sem("c_fitp"), 1)
            nc.tensor.transpose(ps[0:1, 5, 0:P], fitm[:, 0:1], ident).then_inc(sem("c_fitt"), 1)
            keep_clock(7, 6)
            by_fit(pe, lambda wins: sample_pe(pe, wins))
            keep_clock(4, 4)
            pe.wait_ge(sem("c_agg"), 1)
            nc.tensor.matmul(ps[:, 0, 0:1], fold, agg[:, 0:1], start=True, stop=True).then_inc(sem("c_mu"), 1)
            pe.wait_ge(sem("c_dev"), 1)
            nc.tensor.matmul(ps[:, 1, 0:1], fold, bn[:, 1:2], start=True, stop=True).then_inc(sem("c_var"), 1)
            keep_clock(5, 4)
            pe.wait_ge(sem("c_xn"), 1)
            norm_pe(pe, 4, 4)
            pe.wait_ge(sem("e_u"), 1)
            for j in range(J):
                last = nc.tensor.matmul(ps[:, 0, 0:N], gwt[:, j, :, :, :].rearrange("p g j e -> p (g j e)"),
                                        u[:, j * N:(j + 1) * N], start=(j == 0), stop=(j == J - 1))
            last.then_inc(sem("e_lg"), 1)
            for i in range(J * NH):
                last = nc.tensor.transpose(ps[:, 1, i * P:(i + 1) * P], u[:, i * P:(i + 1) * P], ident)
            last.then_inc(sem("e_ut"), 1)
            keep_clock(6, 4)
            pe.wait_ge(sem("e_pm"), 1)
            for h in range(NH):
                last = nc.tensor.transpose(ps[:, 2, h * P:(h + 1) * P], pm[:, h * P:(h + 1) * P], ident)
            last.then_inc(sem("e_pmt"), 1)
            keep_clock(1, 4)
            pe.wait_ge(sem("e_uts"), 1)
            pe.wait_ge(sem("e_pmts"), 1)
            for j in range(J):
                for h in range(NH):
                    last = nc.tensor.matmul(ps[:, 3, j * P:(j + 1) * P], ut[:, j * NH + h, :], pmT[:, h, :],
                                            start=(h == 0), stop=(h == NH - 1))
            last.then_inc(sem("e_pool"), 1)
            pe.wait_ge(sem("ld_d"), 16 * 5)
            pe.wait_ge(sem("e_pools"), BP)
            for e in range(E):
                last = nc.tensor.matmul(ps[:, 4, e * B:(e + 1) * B], ew1[:, e, :], pooled[:, e, :], start=True, stop=True)
            last.then_inc(sem("e_h"), 1)
            pe.wait_ge(sem("e_hid"), 1)
            for e in range(E):
                last = nc.tensor.matmul(ps[0:C, 5, e * B:(e + 1) * B], ew2[:, e, :], hid[:, e, :], start=True, stop=True)
            last.then_inc(sem("e_o"), 1)
            pe.wait_ge(sem("e_os"), 1)
            nc.tensor.transpose(ps[:, 6, 0:C], eo[:, :, :].rearrange("o b e -> o (b e)"), ident[0:C, 0:C]).then_inc(sem("e_ot"), 1)
            keep_clock(2, 1)
            pe.wait_ge(sem("e_ol"), 1)
            for j in range(J):
                last = nc.tensor.matmul(ps[:, 7, j * N:(j + 1) * N], eol[:, j, :, :].rearrange("p g o -> p (g o)"),
                                        pm[:, :], start=True, stop=True)
            last.then_inc(sem("e_y"), 1)

        @block.vector
        def _(dve):
            dve.wait_ge(sem("ld_x"), 16)
            link = Chain(dve, sem("d_main"))

            def weights_of_1():
                dve.wait_ge(sem("ld_a"), 16 * 3)
                nc.vector.tensor_scalar(bqs[:, :], acol[:, 1:2], QSCALE, None, ALU.mult).then_inc(sem("a_bqs"), 1)
                link(nc.vector.transpose(a4s[:, :, :].rearrange("p a b -> p (a b)"),
                                         a4[:, :, :].rearrange("p a b -> p (a b)")))
                dve.wait_ge(sem("zero_a4"), 2)
                for g in range(BP):
                    rows = slice(C * g, C * g + C)
                    last = nc.vector.tensor_copy(a4t[rows, :, rows], a4s[rows, :, :])
                last.then_inc(sem("a_w"), 1)

            deviations(dve, 1)
            weights_of_1()
            dve.wait_ge(sem("norm_rstd"), 1)
            link(nc.vector.tensor_tensor(xc[:, :], xc[:, :], rstd[:, :], ALU.mult))
            nc.vector.tensor_scalar(u[:, :], xc[:, :], acol[:, 0:1], None, ALU.mult).then_inc(sem("a_u"), 1)
            table_of_steps(link)
            att_dve(dve, "a_", acol[:, 1:2], bvrow[:, :])
            dve.wait_ge(sem("c_w"), 1)
            for g in range(BP):
                for j in range(J):
                    last = nc.vector.tensor_copy(gwt[C * g:C * g + C, j, g, j, :], ps[0:C, 1, TAPS * C:TAPS * C + E])
            last.then_inc(sem("c_wd"), 1)
            nc.vector.scalar_tensor_tensor(out=x[:, :], in0=ps[:, 0, :], scalar=acol[:, 3:4], in1=x[:, :],
                                           op0=ALU.add, op1=ALU.add).then_inc(sem("a_x"), 1)
            dve.wait_ge(sem("a_x"), 1)
            if upto == "a":
                dve.sem_inc(sem("out_ready"), 1)
            norm_dve(dve, 2)
            for cols in (FIRST, REST):
                nc.vector.tensor_tensor(u[:, cols], xc[:, cols], rstd[:, cols], ALU.mult).then_inc(sem("b_u"), 1)
            dve.wait_ge(sem("b_u"), 2)
            dve.wait_ge(sem("b_col"), 1)
            pick_op(dve, "d_pick")
            dve.wait_ge(sem("table"), 16)
            recurrent(dve, DVEBody())
            dve.wait_ge(sem("b_x"), 1)
            if upto == "b":
                dve.sem_inc(sem("out_ready"), 1)
            dve.wait_ge(sem("zero_c"), 7)
            dve.wait_ge(sem("ld_c"), 64)
            link(nc.vector.tensor_tensor(offb[:, :], boff[:, :], const("base"), ALU.add))
            dve.wait_ge(sem("norm_rstd"), 3)
            for j in range(J):
                half = slice(j * N, j * N + N)
                nc.vector.scalar_tensor_tensor(out=xwin[:, j, 2:2 + H, :],
                                               in0=xc[:, half].rearrange("p (r c) -> p r c", r=H), scalar=0.0,
                                               in1=rstd[:, half].rearrange("p (r c) -> p r c", r=H),
                                               op0=ALU.max, op1=ALU.mult).then_inc(sem("c_u"), 1)
                dve.wait_ge(sem("c_u"), j + 1)
                spread(nc.vector.tensor_copy, j, 1, "c_xsd")

            def offsets(j):
                dve.wait_ge(sem("c_om"), j + 1)
                nb = NH * BP
                nc.vector.tensor_tensor(om[:, nb * j:nb * j + nb, :],
                                        ps[:, OMBANK[j], :].rearrange("p (i o) -> p i o", o=OPAD)[:, :, 0:OCH],
                                        offb[:, :].unsqueeze(1).broadcast_to([P, nb, OCH]),
                                        ALU.add).then_inc(sem("c_oms"), 1)
                dve.wait_ge(sem("c_oms"), j + 1)

            offsets(0)
            distance_y(0, 0, CA["grid"][0])
            distance_x(dve, 0)
            sigmoid_mask(dve, link, 0)
            offsets(1)
            mid = (WROWS - 1) / 2
            link(nc.vector.tensor_scalar(fit[:, :, :], om[:, :, 0:GK], -mid, None, ALU.add))
            nc.vector.tensor_reduce(fitm[:, 0:1], fit[:, :, :], AX.XY, ALU.max,
                                    apply_absolute_value=True).then_inc(sem("c_fitp"), 1)
            row_weights(dve, 1, 0, 0)
            dve.wait_ge(sem("c_fitt"), 1)
            link(nc.vector.tensor_reduce(fitm[0:1, 1:2], ps[0:1, 5, 0:P], AX.X, ALU.max))
            nc.vector.tensor_scalar(fiti[:, :], fitm[0:1, 1:2], mid, None, ALU.is_le).then_inc(sem("c_fit"), 1)
            by_fit(dve, lambda wins: sample_dve(dve, wins, Chain(dve, sem("s_dchain"))))
            dve.wait_ge(sem("ld_d"), 16 * 5)
            dve.wait_ge(sem("c_out"), 1)
            link(nc.vector.tensor_scalar(y[:, :], ps[:, 7, :], ccol[:, 0:1], None, ALU.add))
            link(nc.vector.bn_stats(stats[:, :], y[:, :]))
            nc.vector.bn_aggr(agg[:, :], stats[:, :]).then_inc(sem("c_agg"), 1)
            dve.wait_ge(sem("c_mu"), 1)
            link(nc.vector.tensor_tensor(bn[:, 0:1], agg[:, 0:1], ps[:, 0, 0:1], ALU.subtract))
            nc.vector.scalar_tensor_tensor(out=bn[:, 1:2], in0=bn[:, 0:1], scalar=bn[:, 0:1], in1=agg[:, 1:2],
                                           op0=ALU.mult, op1=ALU.add).then_inc(sem("c_dev"), 1)
            link(nc.vector.tensor_copy(bn[:, 5:6], ps[:, 0, 0:1]))
            dve.wait_ge(sem("c_rs"), 1)
            link(nc.vector.tensor_tensor(bn[:, 4:5], bn[:, 3:4], ccol[:, 1:2], ALU.mult))
            link(nc.vector.tensor_scalar(y[:, :], y[:, :], bn[:, 5:6], bn[:, 4:5], ALU.subtract, ALU.mult))
            nc.vector.scalar_tensor_tensor(out=x[:, :], in0=y[:, :], scalar=ccol[:, 2:3], in1=x[:, :],
                                           op0=ALU.add, op1=ALU.add).then_inc(sem("c_xn"), 1)
            dve.wait_ge(sem("c_xn"), 1)
            if upto == "c":
                dve.sem_inc(sem("out_ready"), 1)
            norm_dve(dve, 4)
            nc.vector.tensor_tensor(u[:, :], xc[:, :], rstd[:, :], ALU.mult).then_inc(sem("e_u"), 1)
            dve.wait_ge(sem("e_lg"), 1)
            link(nc.vector.tensor_scalar(lg[:, :], ps[:, 0, 0:N], gb[:, 0:1], None, ALU.add))
            link(nc.vector.reduce_max(lnm[:, 2:3], lg[:, :], AX.X))
            nc.vector.tensor_scalar(lnm[:, 0:1], lnm[:, 2:3], -1.0, None, ALU.mult).then_inc(sem("e_max"), 1)
            dve.wait_ge(sem("e_ex"), 1)
            link(nc.vector.reciprocal(lnm[:, 3:4], lnm[:, 1:2]))
            link(nc.vector.tensor_scalar(pr[:, :], pr[:, :], lnm[:, 3:4], None, ALU.mult))
            link(nc.vector.max(ptop[:, :], pr[:, :]))
            link(nc.vector.match_replace(rest[:, :], ptop[:, :], pr[:, :], -1.0))
            nc.vector.scalar_tensor_tensor(out=pm[:, :], in0=rest[:, :], scalar=0.0, in1=pr[:, :],
                                           op0=ALU.is_lt, op1=ALU.mult).then_inc(sem("e_pm"), 1)
            dve.wait_ge(sem("e_pmt"), 1)
            nc.vector.tensor_copy(pmT[:, :, :].rearrange("p h n -> p (h n)"), ps[:, 2, 0:NH * P]).then_inc(sem("e_pmts"), 1)
            dve.wait_ge(sem("e_pool"), 1)
            for g in range(BP):
                span = J * (P + E)
                own = ps[C * g:C * g + C, 3, J * E * g:J * E * g + span].rearrange("c (j n) -> c j n", j=J)[:, :, 0:E]
                nc.vector.tensor_copy(pooled[0:C, :, J * g:J * g + J].rearrange("c e j -> c j e"),
                                      own).then_inc(sem("e_pools"), 1)
            dve.wait_ge(sem("e_o"), 1)
            nc.vector.tensor_copy(eo[:, :, :], ps[0:C, 5, 0:E * B].rearrange("o (e b) -> o b e", b=B)).then_inc(sem("e_os"), 1)
            dve.wait_ge(sem("e_ot"), 1)
            link(nc.vector.tensor_tensor(eoT[:, :], ps[:, 6, 0:C], eb2[:, :], ALU.add))
            nc.vector.tensor_tensor(eol[:, :, :, :].rearrange("p j g o -> p (j g) o"),
                                    eoT[:, :].unsqueeze(1).broadcast_to([P, J * BP, C]),
                                    const("own").unsqueeze(2).broadcast_to([P, J * BP, C]),
                                    ALU.mult).then_inc(sem("e_ol"), 1)
            dve.wait_ge(sem("e_y"), 1)
            nc.vector.tensor_tensor(fin[:, :], ps[:, 7, :], x[:, :], ALU.add).then_inc(sem("fin"), 1)
            dve.wait_ge(sem("fin"), 1)
            if upto == "all":
                dve.sem_inc(sem("out_ready"), 1)


def pair_major(v):
    return np.asarray(v).reshape(BP, J, C, N).transpose(0, 2, 1, 3).reshape(P, F)


def kernel(**inputs):
    import concourse.bacc as _bacc
    from concourse.bass_utils import run_bass_kernel_spmd as _run

    nc = _bacc.Bacc("TRN2", target_bir_lowering=False, num_devices=1)
    inputs = dict(inputs)
    cst, _ = constants()
    arrays, aps = {}, {}
    inputs["cst"], inputs["codes"] = cst, step_codes()
    inputs["x"] = pair_major(inputs["x"])
    inputs["L0_conv_w4"] = np.stack([inputs.pop("L0_conv_" + n) for n in ("wq", "wk", "wv", "wo")], 1)
    inputs["L0_conv_col"] = np.stack([inputs.pop("L0_conv_" + n) for n in ("freq_weights", "bq", "bk", "bo")], 1)
    inputs["L1_conv_col"] = np.stack([inputs.pop("L1_conv_" + n) for n in ("b", "gamma", "beta")], 1)
    inputs["L0_ffn_w4"] = np.concatenate([inputs.pop("L0_ffn_" + n) for n in ("wq", "wk", "wv", "wo")], -1)
    b1 = np.asarray(inputs.pop("L0_ffn_ffn_b1"))
    inputs["L0_ffn_ffn_w2b1"] = np.concatenate([inputs.pop("L0_ffn_ffn_w2"), b1[..., None]], -1)
    for name, v in inputs.items():
        v = np.ascontiguousarray(v)
        if v.dtype == np.bool_:
            v = np.ascontiguousarray(v.T).astype(np.int32)
        elif name in ("L0_ffn_w4", "L0_ffn_ffn_w1", "L0_ffn_ffn_w2b1", "L0_ffn_ffn_b2"):
            v = v.reshape((-1,) + v.shape[2:])
        arrays[f"in_{name}"] = v
        aps[name] = nc.dram_tensor(f"in_{name}", v.shape, mybir.dt.from_np(v.dtype), kind="ExternalInput").ap()
    out = nc.dram_tensor("out", (P, F), f32, kind="ExternalOutput").ap()
    metaformer_kernel(nc, aps, out, UPTO)
    res = _run(nc, [arrays], core_ids=[0]).results[0]["out"]
    return np.ascontiguousarray(res.reshape(BP, C, J, H, W).transpose(0, 2, 1, 3, 4)).reshape(B, C, H, W)


UPTO = "all"
```

```python
import concourse.bass as bass
from concourse import mybir
from contextlib import ExitStack
import numpy as np

B, C, H, W = 8, 32, 16, 16
N = H * W
P = 128
BP = P // C
J = B // BP
F = J * N
NH = N // P
STEPS, OPS = 33, 19
HID = 128
DG, K = 2, 3
TAPS = K * K
CG = C // DG
GK = DG * TAPS
OCH = 3 * GK
E, TOPK = 16, 8
QSCALE = float(C) ** -0.5
NEST = (3, 3, 2)
assert 2 * NEST[0] * NEST[1] * NEST[2] >= STEPS + 1
NONE = 4 * STEPS
TPAD = 32
OMBANK = (4, 7)
WROWS = 8
NWIN = 4
BLK = 64
FIRST, REST = slice(0, 1), slice(1, F)
FILL = (6, 4)
OPAD = 64
XROWS = H + 4
K3 = 3

f32 = mybir.dt.float32
i32 = mybir.dt.int32
u32 = mybir.dt.uint32
ALU = mybir.AluOpType
ACT = mybir.ActivationFunctionType
AX = mybir.AxisListType


def constants():
    p = np.arange(P)
    cols = {}
    cols["ident"] = np.eye(P)
    cols["mean"] = (p[:, None] // C == p[None, :] // C) / C
    cols["fold"] = (p[:, None] % C == p[None, :] % C) / BP
    k = np.arange(TAPS)
    row, col = p // W, p % W
    by = (row % 4)[:, None] + 1 + (k // K)[None, :]
    bx = col[:, None] - 1 + (k % K)[None, :]
    cols["base"] = np.concatenate([by, by, bx, bx, np.zeros((P, GK))], 1)
    cols["grid"] = np.broadcast_to(np.arange(W), (P, W))
    lead = [[(4 * ((8 * h + row) // 4) - 2)[:, None] for _ in range(2)] for h in range(NH)]
    cols["wide"] = np.concatenate(
        [np.arange(WROWS)[None, :] + WROWS * w - lead[h][w] for h in range(NH) for w in range(2)], 1)
    be = np.arange(P) // E
    cols["own"] = np.concatenate([(be[:, None] == J * np.arange(BP)[None, :] + j) for j in range(J)], 1)
    cols["eps"] = np.broadcast_to(np.array([1e-6, 1e-5]), (P, 2))
    at, off = {}, 0
    for name, a in cols.items():
        at[name] = (off, off + a.shape[1])
        off += a.shape[1]
    return np.concatenate([np.asarray(a, np.float32) for a in cols.values()], 1), at


def step_codes():
    return np.broadcast_to(4 * np.arange(STEPS)[None, :] - NONE, (OPS, STEPS)).astype(np.float32)


class Chain:

    def __init__(self, eng, sem):
        self.eng, self.sem, self.n = eng, sem, 0

    def __call__(self, ins):
        self.n += 1
        ins.then_inc(self.sem, 1)
        self.eng.wait_ge(self.sem, self.n)


def metaformer_kernel(nc, a, out):
    _, CA = constants()
    NCST = max(e for _, e in CA.values())
    ctx = ExitStack()

    def sb(name, shape, dt=f32):
        return ctx.enter_context(nc.sbuf_tensor(name, shape, dt))

    sems = {}

    def sem(name):
        if name not in sems:
            sems[name] = ctx.enter_context(nc.semaphore(name))
        return sems[name]

    with ctx:
        cst = sb("cst", [P, NCST])

        def const(name):
            return cst[:, CA[name][0]:CA[name][1]]

        ident, meanm, fold = const("ident"), const("mean"), const("fold")
        zero = cst[:, CA["base"][1] - 1:CA["base"][1]]
        eps6, eps5 = cst[:, CA["eps"][0]:CA["eps"][0] + 1], cst[:, CA["eps"][0] + 1:CA["eps"][1]]
        x = sb("x", [P, F])
        u = sb("u", [P, F])
        xc = sb("xc", [P, F])
        sq = sb("sq", [P, F])
        rstd = sb("rstd", [P, F])
        a4 = sb("a4", [P, 4, C])
        a4s = sb("a4s", [P, 4, C])
        a4t = sb("a4t", [P, 4, P])
        r4 = sb("r4", [P, 4, P])
        acol = sb("acol", [P, 4])
        bqs = sb("bqs", [P, 1])
        bvrow = sb("bvrow", [P, C])
        q_sb = sb("q_sb", [P, BP, F])
        k_sb = sb("k_sb", [P, F])
        v_sb = sb("v_sb", [P, J * NH, P])
        negmax = sb("negmax", [P, B, NH])
        rowsum = sb("rowsum", [P, B, NH])
        rinv = sb("rinv", [P, B, NH])
        att = sb("att", [P, F])
        masks = sb("masks", [OPS, 2, STEPS], i32)
        codes = sb("codes", [OPS, STEPS])
        table = sb("table", [OPS, 2, STEPS + TPAD])
        nexts_op = sb("nexts_op", [OPS, STEPS + 1], i32)
        nexts = sb("nexts", [1, OPS * (STEPS + 1)], i32)
        top = sb("top", [1, 8])
        topi = sb("topi", [1, 8], u32)
        rs4 = sb("rs4", [P, 4, C])
        w1 = sb("w1", [P, 2, HID])
        w1z = sb("w1z", [P, 2, HID])
        w2b1 = sb("w2b1", [HID, 2, C + 1])
        b2 = sb("b2", [P, 2])
        hcol = sb("hcol", [C, 1])
        woff_n = sb("woff_n", [OCH, C * TAPS])
        wc_n = sb("wc_n", [C, C * TAPS])
        woff = sb("woff", [P, K, OPAD])
        omc = sb("omc", [P, J, F])
        wc = sb("wc", [P, TAPS, BP, C])
        ccol = sb("ccol", [P, 3])
        boff = sb("boff", [P, OCH])
        offb = sb("offb", [P, OCH])
        xwin = sb("xwin", [P, J, XROWS, W])
        xs = sb("xs", [P, J, BP, XROWS, W])
        xt = sb("xt", [P, J, DG, NWIN, BP, C])
        om = sb("om", [P, J * NH * BP, OCH])
        msk = sb("msk", [P, J * NH * BP, GK])
        fit = sb("fit", [P, J * NH * BP, GK])
        fitm = sb("fitm", [P, 4])
        fiti = sb("fiti", [1, 1], i32)
        ty = sb("ty", [P, 2, J * NH, GK, BP, WROWS])
        tx = sb("tx", [P, J * NH, GK, BP, W])
        disty = sb("disty", [P, 2, BP, GK, WROWS])
        distx = sb("distx", [P, 2, BP, GK, W])
        smat = sb("smat", [P, 3, K3 * BP, P])
        smatT = sb("smatT", [P, 2, K3, BP, P])
        early = smat[:, :, :, :].rearrange("p r u n -> p (r u n)")
        probs = early[:, 0:2 * F].rearrange("p (r h m) -> p r h m", r=2, h=NH)
        probsT = early[:, 2 * F:4 * F].rearrange("p (r h m) -> p r h m", r=2, h=NH)
        relu = smatT[:, :, :, :, :].rearrange("p r k g n -> p (r k g n)")[:, 0:BP * F].rearrange(
            "p (g n) -> p g n", g=BP)
        samp = sb("samp", [P, 2, K3, P])
        y = sb("y", [P, F])
        stats = sb("stats", [P, 6])
        agg = sb("agg", [P, 2])
        bn = sb("bn", [P, 6])
        gw_n = sb("gw_n", [E, C])
        gwt = sb("gwt", [P, J, BP, J, E])
        gb = sb("gb", [P, 1])
        ew1 = sb("ew1", [C + 1, E, HID])
        ew2 = sb("ew2", [HID, E, C])
        eb2 = sb("eb2", [P, C])
        lg = sb("lg", [P, N])
        pr = sb("pr", [P, N])
        lnm = sb("lnm", [P, 4])
        ptop = sb("ptop", [P, TOPK])
        rest = sb("rest", [P, N])
        pm = sb("pm", [P, N])
        pmT = sb("pmT", [P, NH, P])
        ut = sb("ut", [P, J * NH, P])
        pooled = sb("pooled", [C + 1, E, B])
        hid = sb("hid", [HID, E, B])
        eo = sb("eo", [C, B, E])
        eoT = sb("eoT", [P, C])
        eol = sb("eol", [P, J, BP, C])
        fin = sb("fin", [P, F])
        ps = ctx.enter_context(nc.psum_tensor("ps", [P, 8, 512], f32))

        LOOP = ["l_col", "l_done", "l_first", "l_hcol", "l_z_act", "l_z_dve", "l_hid", "l_relu_act", "l_relu_dve", "l_ffn", "l_h"]
        ATT = ["w", "proj", "q", "q1", "k", "v", "sc", "mx", "ex", "nrm", "pt", "pts", "av", "att", "wo", "fin", "dchain",
               "achain"]
        for n in LOOP:
            sem(n)
        for n in ATT:
            sem("r_" + n)
        loop_sems = range(sem(LOOP[0]).num, sem("r_" + ATT[-1]).num + 1)
        assert len(loop_sems) == len(LOOP) + len(ATT)
        for n in ("l_pick", "go_pe", "go_act", "go_sp", "clear_pe"):
            sem(n)
        load_sems = []
        for p in range(2):
            first = sem("l_w1_%d" % p).num
            sem("l_w2_%d" % p)
            load_sems.append(range(first, sem("l_attn_w_%d" % p).num + 1))
            assert len(load_sems[p]) == 3

        block = ctx.enter_context(nc.Block())

        def dr(name):
            return a[name]

        def every_pair(ap):
            return ap.unsqueeze(0).broadcast_to([BP, *ap.shape])

        def att_pe(pe, px, weights, between=None):
            S = lambda n: sem(px + n)
            wq_, wk_, wv_, wo_ = weights
            nc.tensor.matmul(ps[:, 0, :], wq_, u[:, :], start=True, stop=True).then_inc(S("proj"), 1)
            nc.tensor.matmul(ps[:, 1, :], wk_, u[:, :], start=True, stop=True).then_inc(S("proj"), 1)
            for i in range(J * NH):
                last = nc.tensor.matmul(ps[:, 2, i * P:(i + 1) * P], u[:, i * P:(i + 1) * P], wv_,
                                        start=True, stop=True)
            last.then_inc(S("proj"), 1)

            def scores(t):
                bp, j = t % BP, t // BP
                if t >= 2:
                    pe.wait_ge(S("ex"), 2 * (t - 1))
                pe.wait_ge(S("q1") if j else S("q"), bp + 1)
                pe.wait_ge(S("k"), j + 1)
                for h in range(NH):
                    q0 = j * N + h * P
                    last = nc.tensor.matmul(ps[:, 3 + t % 2, h * N:(h + 1) * N], q_sb[:, bp, q0:q0 + P],
                                            k_sb[:, j * N:(j + 1) * N], start=True, stop=True)
                last.then_inc(S("sc"), 1)

            def transposes(t):
                pe.wait_ge(S("nrm"), t + 1)
                if t >= 2:
                    pe.wait_ge(S("pts"), t - 1)
                for mh in range(NH):
                    for h in range(NH):
                        last = nc.tensor.transpose(ps[:, 5 + t % 2, mh * N + h * P:mh * N + (h + 1) * P],
                                                   probs[:, t % 2, h, mh * P:(mh + 1) * P], ident)
                last.then_inc(S("pt"), 1)

            def values(t):
                bp, j = t % BP, t // BP
                pe.wait_ge(S("pts"), t + 1)
                if t == 0:
                    pe.wait_ge(S("v"), 1)
                for mh in range(NH):
                    last = nc.tensor.matmul(ps[C * bp:C * bp + C, 7, j * N:(j + 1) * N],
                                            v_sb[:, j * NH + mh, C * bp:C * bp + C], probsT[:, t % 2, mh, :],
                                            start=(mh == 0), stop=(mh == NH - 1))
                last.then_inc(S("av"), 1)

            scores(0)
            scores(1)
            for t in range(B + 1):
                if between and t == BP - 1:
                    pe.wait_ge(S("q1"), BP)
                    between()
                if t + 2 < B:
                    scores(t + 2)
                if t == B - 1:
                    keep_clock(3, 3)
                if t < B:
                    transposes(t)
                else:
                    keep_clock(2, 3)
                if t >= 1:
                    values(t - 1)
            keep_clock(2, 3)
            pe.wait_ge(S("att"), 1)
            if between:
                pe.wait_ge(sem("c_wa"), BP + K)
            nc.tensor.matmul(ps[:, 0, :], wo_, att[:, :], start=True, stop=True).then_inc(S("wo"), 1)
            keep_clock(3, 7)

        def att_act(act, px, bq, bk, between=None):
            S = lambda n: sem(px + n)
            act.wait_ge(S("proj"), 2)
            for j in range(J):
                nc.scalar.activation(k_sb[:, j * N:j * N + N], ps[:, 1, j * N:j * N + N], ACT.Identity,
                                     bias=bk).then_inc(S("k"), 1)
            for t in range(B):
                if t < BP:
                    rows = slice(C * t, C * t + C)
                    act.wait_ge(S("q"), t + 1)
                    nc.scalar.activation(q_sb[rows, t, N:], ps[rows, 0, N:], ACT.Identity, scale=QSCALE,
                                         bias=bq if isinstance(bq, float) else bq[rows, :]).then_inc(S("q1"), 1)
                act.wait_ge(S("mx"), t + 1)
                if t >= 2:
                    act.wait_ge(S("pt"), t - 1)
                for h in range(NH):
                    nc.scalar.activation(probs[:, t % 2, h, :], ps[:, 3 + t % 2, h * N:(h + 1) * N], ACT.Exp,
                                         bias=negmax[:, t, h:h + 1],
                                         accum_out=rowsum[:, t, h:h + 1]).then_inc(S("ex"), 1)
                if t >= 1:
                    copy_probs(act, S, t - 1)
                if between:
                    between(t)
            copy_probs(act, S, B - 1)

        def copy_probs(act, S, t):
            act.wait_ge(S("pt"), t + 1)
            if t >= 2:
                act.wait_ge(S("av"), t - 1)
            nc.scalar.activation(probsT[:, t % 2, :, :], ps[:, 5 + t % 2, :], ACT.Copy).then_inc(S("pts"), 1)

        def table_step(link, t):
            am, fm_ = masks[:, 0, :], masks[:, 1, :]
            t0, t1 = table[:, 0, :], table[:, 1, :]
            if t == 0:
                link.eng.wait_ge(sem("ld_m"), 48)
                link(nc.vector.memset(table[:, :, STEPS:], 0.0))
                link(nc.vector.tensor_tensor(t1[:, 0:STEPS], am, fm_, ALU.max))
                link(nc.vector.scalar_tensor_tensor(out=t0[:, 0:STEPS], in0=am, scalar=2.0, in1=codes[:, :],
                                                    op0=ALU.mult, op1=ALU.add))
            elif t == 1:
                link(nc.vector.tensor_tensor(t0[:, 0:STEPS], t0[:, 0:STEPS], fm_, ALU.add))
                link(nc.vector.tensor_tensor(t0[:, 0:STEPS], t0[:, 0:STEPS], t1[:, 0:STEPS], ALU.mult))
            elif t < 5:
                for n in (2 * (t - 2), 2 * (t - 2) + 1):
                    d, (src_, dst) = 1 << n, ((t0, t1) if n % 2 == 0 else (t1, t0))
                    link(nc.vector.tensor_tensor(dst[:, 0:STEPS], src_[:, 0:STEPS], src_[:, d:d + STEPS], ALU.min))
            elif t == 5:
                nc.vector.tensor_scalar(nexts_op[:, :], t0[:, 0:STEPS + 1], float(NONE), None,
                                        ALU.add).then_inc(sem("table_op"), 1)

        def att_dve(dve, px, bq, bv, between=None):
            S = lambda n: sem(px + n)
            link = Chain(dve, S("dchain"))
            dve.wait_ge(sem("ld_cst"), 16)
            dve.wait_ge(S("proj"), 1)
            for g in range(BP):
                rows = slice(C * g, C * g + C)
                nc.vector.tensor_scalar(q_sb[rows, g, 0:N], ps[rows, 0, 0:N], bq[rows, :], QSCALE,
                                        ALU.add, ALU.mult).then_inc(S("q"), 1)
            dve.wait_ge(S("proj"), 3)
            if bv is None:
                nc.vector.tensor_copy(v_sb[:, :, :], ps[:, 2, :]).then_inc(S("v"), 1)
            else:
                nc.vector.tensor_tensor(v_sb[:, :, :].rearrange("p i (g c) -> p (i g) c", c=C),
                                        ps[:, 2, :].rearrange("p (i c) -> p i c", c=C),
                                        bv.unsqueeze(1).broadcast_to([P, J * NH * BP, C]),
                                        ALU.add).then_inc(S("v"), 1)

            def maxima(t):
                dve.wait_ge(S("sc"), t + 1)
                nc.vector.tensor_reduce(negmax[:, t, :], ps[:, 3 + t % 2, :].rearrange("p (h m) -> p h m", h=NH),
                                        AX.X, ALU.max, negate=True).then_inc(S("mx"), 1)

            maxima(0)
            maxima(1)
            for t in range(B):
                dve.wait_ge(S("ex"), 2 * (t + 1))
                link(nc.vector.reciprocal(rinv[:, t, :], rowsum[:, t, :]))
                for h in range(NH):
                    ins = nc.vector.tensor_scalar(probs[:, t % 2, h, :], probs[:, t % 2, h, :],
                                                  rinv[:, t, h:h + 1], None, ALU.mult)
                ins.then_inc(S("nrm"), 1)
                if t + 2 < B:
                    maxima(t + 2)
                if between:
                    between(link, t)
            dve.wait_ge(S("av"), B)
            nc.vector.tensor_copy(att[:, :], ps[:, 7, :]).then_inc(S("att"), 1)
            dve.wait_ge(S("wo"), 1)

        def keep_clock(n, bank, weights=ident, data=cst[:, 0:N]):
            for _ in range(n):
                nc.tensor.matmul(ps[:, bank, 0:N], weights, data, start=True, stop=True)

        def norm_pe(pe, i, bank, fills=(4, 4)):
            nc.tensor.matmul(ps[:, 5, :], meanm, x[:, :], start=True, stop=True).then_inc(sem("norm_mean"), 1)
            keep_clock(fills[0], bank)
            pe.wait_ge(sem("norm_sq"), i)
            nc.tensor.matmul(ps[:, 6, :], meanm, sq[:, :], start=True, stop=True).then_inc(sem("norm_var"), 1)
            keep_clock(fills[1], bank)

        def norm_act(act, i, eps):
            if i != 3:
                act.wait_ge(sem("norm_xc"), i)
                nc.scalar.activation(sq[:, :], xc[:, :], ACT.Square).then_inc(sem("norm_sq"), 1)
            act.wait_ge(sem("norm_var"), i)
            nc.scalar.activation(rstd[:, :], ps[:, 6, :], ACT.Ln, bias=eps).then_inc(sem("norm_ln"), 1)
            act.wait_ge(sem("norm_ln"), i)
            nc.scalar.activation(rstd[:, :], rstd[:, :], ACT.Exp, scale=-0.5).then_inc(sem("norm_rstd"), 1)

        def deviations(dve, i):
            dve.wait_ge(sem("norm_mean"), i)
            nc.vector.tensor_tensor(xc[:, :], x[:, :], ps[:, 5, :], ALU.subtract).then_inc(sem("norm_xc"), 1)

        def norm_dve(dve, i):
            deviations(dve, i)
            dve.wait_ge(sem("norm_rstd"), i)

        def recurrent(eng, body):
            cur = eng.alloc_register("cur")
            op = eng.alloc_register("op")
            code = eng.alloc_register("code")
            at = eng.alloc_register("at")
            wi = eng.alloc_register("wi")
            has_att = eng.alloc_register("has_att")
            has_ffn = eng.alloc_register("has_ffn")
            eng.reg_mov(cur, 0)
            with eng.Fori(0, NEST[0]), eng.If_cmp(cur, STEPS + 1, "IS_LT"), \
                    eng.Fori(0, NEST[1]), eng.If_cmp(cur, STEPS + 1, "IS_LT"), eng.Fori(0, NEST[2]):
                for p in range(2):
                    with eng.If_cmp(cur, STEPS + 1, "IS_LT"):
                        body.start(eng)
                        eng.load(op, topi[0:1, 0:1])
                        eng.reg_mul(at, op, STEPS + 1)
                        eng.reg_add(at, at, cur)
                        ati = eng.snap(at, min_val=0, max_val=OPS * (STEPS + 1) - 1)
                        eng.load(code, nexts[0:1, bass.ds(ati, 1)])
                        eng.reg_alu(cur, code, 2, ALU.logical_shift_right)
                        eng.reg_mul(wi, cur, OPS)
                        eng.reg_add(wi, wi, op)
                        eng.reg_add(cur, cur, 1)
                        eng.reg_alu(has_ffn, code, 1, ALU.bitwise_and)
                        eng.reg_alu(has_att, code, 2, ALU.bitwise_and)
                        with eng.If_cmp(code, NONE, "IS_LT"):
                            body.begin(eng)
                            with eng.If_cmp(has_att, 0, "IS_NE"):
                                body.attention(eng, wi, p)
                            with eng.If_cmp(has_ffn, 0, "IS_NE"):
                                body.ffn(eng, wi, p)
                            with eng.If_cmp(has_ffn, 0, "IS_EQ"):
                                body.no_ffn(eng, p)
                        with eng.If_cmp(code, NONE, "IS_GE"):
                            body.finish(eng)

        def spread_w1(eng_copy, first, p, done):
            for g in (first, first + 2):
                rows = slice(C * g, C * g + C)
                eng_copy(w1z[rows, g % 2, :], w1[rows, p, :]).then_inc(sem(done), 1)

        class SPBody:
            def start(self, sp):
                sp.wait_ge(sem("go_sp"), 1)
                sp.sem_clear(sem("go_sp"))

            def begin(self, sp):
                pass

            def attention(self, sp, wi, p):
                i = sp.snap(wi, min_val=0, max_val=STEPS * OPS - 1)
                w4 = dr("L0_ffn_w4")[bass.ds(i, 1), :, :].rearrange("o c d -> (o c) d")
                sp.dma_start(rs4[:, :, :].rearrange("p a c -> p (a c)"), every_pair(w4)).then_inc(
                    sem("l_attn_w_%d" % p), 16)

            def ffn(self, sp, wi, p):
                i = sp.snap(wi, min_val=0, max_val=STEPS * OPS - 1)
                step = lambda name: dr("L0_ffn_ffn_" + name)[bass.ds(i, 1)]
                l_w2 = sem("l_w2_%d" % p)
                sp.dma_start(w1[:, p, :], every_pair(step("w1").rearrange("o c d -> (o c) d"))).then_inc(
                    sem("l_w1_%d" % p), 16)
                sp.dma_start(w2b1[:, p, :], step("w2b1").rearrange("o c d -> (o c) d")).then_inc(l_w2, 16)
                sp.dma_start(b2[:, p:p + 1], every_pair(step("b2").rearrange("o (c k) -> (o c) k", k=1))).then_inc(l_w2, 16)

            def no_ffn(self, sp, p):
                pass

            def finish(self, sp):
                pass

        class PEBody:
            def start(self, pe):
                keep_clock(2, 7)
                pe.wait_ge(sem("go_pe"), 1)
                pe.sem_clear(sem("go_pe"))

            def begin(self, pe):
                pe.wait_ge(sem("clear_pe"), 1)
                pe.sem_clear(sem("clear_pe"))

            def attention(self, pe, wi, p):
                keep_clock(4, 7)
                pe.wait_ge(sem("r_w"), 1)
                att_pe(pe, "r_", [r4[:, n, :] for n in range(4)])
                pe.wait_ge(sem("r_fin"), 1)

            def ffn(self, pe, wi, p):
                keep_clock(FILL[p], 7)
                w2 = w2b1[:, p, 0:C]
                pe.wait_ge(sem("l_z_act"), 2)
                pe.wait_ge(sem("l_z_dve"), 2)

                def hidden(g):
                    rows = slice(2 * C * (g // 2), 2 * C * (g // 2) + 2 * C)
                    nc.tensor.matmul(ps[:, g, :], w1z[rows, g % 2, :], u[rows, :],
                                     start=True, stop=True).then_inc(sem("l_hid"), 1)

                hidden(0)
                hidden(1)
                pe.wait_ge(sem("l_w2_%d" % p), 32)
                pe.wait_ge(sem("l_relu_act"), 1)
                nc.tensor.matmul(ps[0:C, 6, 0:1], w2, relu[:, 0, 0:1], start=True, stop=True).then_inc(sem("l_first"), 1)
                hidden(2)
                pe.wait_ge(sem("l_hcol"), 1)
                nc.tensor.matmul(ps[0:1, 5, 0:C], hcol[:, :], ident[0:C, 0:C],
                                 start=True, stop=True).then_inc(sem("l_col"), 1)
                hidden(3)
                for g in range(BP):
                    pe.wait_ge(sem("l_relu_dve" if g % 2 else "l_relu_act"), g // 2 + 1)
                    last = nc.tensor.matmul(ps[C * g:C * g + C, 4, :], w2, relu[:, g, :],
                                            start=True, stop=True)
                last.then_inc(sem("l_ffn"), 1)

            def no_ffn(self, pe, p):
                nc.tensor.matmul(ps[0:1, 5, 0:C], u[0:C, 0:1], ident[0:C, 0:C],
                                 start=True, stop=True).then_inc(sem("l_col"), 1)

            def finish(self, pe):
                pe.wait_ge(sem("b_x"), 1)
                norm_pe(pe, 3, 7, (2, 2))

        class ACTBody:
            def start(self, act):
                act.wait_ge(sem("go_act"), 1)
                act.sem_clear(sem("go_act"))

            def begin(self, act):
                pass

            def attention(self, act, wi, p):
                att_act(act, "r_", 0.0, 0.0)

            def ffn(self, act, wi, p):
                act.wait_ge(sem("zero_r4"), 2)
                act.wait_ge(sem("l_w1_%d" % p), 16)
                spread_w1(lambda o, i: nc.scalar.activation(o, i, ACT.Copy), 0, p, "l_z_act")
                act.wait_ge(sem("l_w2_%d" % p), 32)
                for g in (0, 2):
                    act.wait_ge(sem("l_hid"), g + 1)
                    nc.scalar.activation(relu[:, g, :], ps[:, g, :], ACT.Relu,
                                         bias=w2b1[:, p, C:C + 1]).then_inc(sem("l_relu_act"), 1)
                act.sem_inc(sem("l_done"), 1)

            def no_ffn(self, act, p):
                act.sem_inc(sem("l_done"), 1)

            def finish(self, act):
                pass

        class DVEBody:
            def start(self, dve):
                pass

            def begin(self, dve):
                pass

            def attention(self, dve, wi, p):
                dve.wait_ge(sem("l_attn_w_%d" % p), 16)
                dve.wait_ge(sem("zero_r4"), 1)
                for g in range(BP):
                    rows = slice(C * g, C * g + C)
                    last = nc.vector.tensor_copy(r4[rows, :, rows], rs4[rows, :, :])
                last.then_inc(sem("r_w"), 1)
                att_dve(dve, "r_", zero, None)
                nc.vector.tensor_copy(u[:, :], ps[:, 0, :]).then_inc(sem("r_fin"), 1)
                dve.wait_ge(sem("r_fin"), 1)

            def ffn(self, dve, wi, p):
                dve.wait_ge(sem("zero_r4"), 2)
                dve.wait_ge(sem("l_w1_%d" % p), 16)
                spread_w1(nc.vector.tensor_copy, 1, p, "l_z_dve")
                dve.wait_ge(sem("l_w2_%d" % p), 32)

                def hidden(g):
                    dve.wait_ge(sem("l_hid"), g + 1)
                    nc.vector.tensor_scalar(relu[:, g, :], ps[:, g, :], w2b1[:, p, C:C + 1], 0.0,
                                            ALU.add, ALU.max).then_inc(sem("l_relu_dve"), 1)

                hidden(1)
                dve.wait_ge(sem("l_first"), 1)
                nc.vector.tensor_scalar(hcol[:, :], ps[0:C, 6, 0:1], b2[0:C, p:p + 1], None,
                                        ALU.add).then_inc(sem("l_hcol"), 1)
                self.pick(dve)
                hidden(3)
                dve.wait_ge(sem("l_ffn"), 1)
                nc.vector.tensor_scalar(u[:, :], ps[:, 4, :], b2[:, p:p + 1], None, ALU.add).then_inc(sem("l_h"), 1)
                dve.wait_ge(sem("l_h"), 1)
                self.end(dve, p)

            def no_ffn(self, dve, p):
                self.pick(dve)
                self.end(dve, p)

            def pick(self, dve):
                dve.wait_ge(sem("l_col"), 1)
                pick_op(dve, "l_pick")
                dve.sem_clear(sem("l_pick"))

            def end(self, dve, p):
                dve.wait_ge(sem("l_done"), 1)
                dve.sem_clear(loop_sems)
                dve.sem_clear(load_sems[p])
                dve.sem_inc(sem("clear_pe"), 1)
                dve.sem_inc(sem("go_act"), 1)

            def finish(self, dve):
                nc.vector.tensor_tensor(x[:, :], x[:, :], u[:, :], ALU.add).then_inc(sem("b_x"), 1)
                deviations(dve, 3)
                dve.wait_ge(sem("norm_xc"), 3)
                nc.vector.tensor_tensor(sq[:, :], xc[:, :], xc[:, :], ALU.mult).then_inc(sem("norm_sq"), 1)

        def pick_op(dve, name):
            link = Chain(dve, sem(name))
            link(nc.vector.max(top[:, :], ps[0:1, 5, 0:OPS]))
            link(nc.vector.max_index(topi[:, :], top[:, :], ps[0:1, 5, 0:OPS]))
            dve.sem_inc(sem("go_pe"), 1)
            dve.sem_inc(sem("go_sp"), 1)

        def sample_steps(wins):
            return [(jh, k3, g, w) for jh in range(J * NH) for k3 in range(TAPS // K3)
                    for g in range(DG) for w in range(len(wins))]

        def by_act(bp, k):
            return (bp * K + k) % 2 == 0

        def copies(j, eng):
            return (j + 1) * sum(by_act(g, k) == (eng == 0) for g in range(BP) for k in range(K))

        def spread(eng_copy, j, eng, done):
            for bp in range(BP):
                for k in range(K):
                    if by_act(bp, k) == (eng == 0):
                        to, frm, n = max(0, 1 - k), max(0, k - 1), W - abs(k - 1)
                        eng_copy(xs[C * k:C * k + C, j, bp, 2:2 + H, to:to + n],
                                 xwin[C * bp:C * bp + C, j, 2:2 + H, frm:frm + n]).then_inc(sem(done), 1)

        def by_fit(eng, run):
            eng.wait_ge(sem("c_fit"), 1)
            fits = eng.alloc_register("fits")
            eng.load(fits, fiti[0:1, 0:1])
            with eng.If_cmp(fits, 0, "IS_NE"):
                run((None,))
            with eng.If_cmp(fits, 0, "IS_EQ"):
                run((0, 1))

        def on_pool(n):
            return n % 4 == 3

        def weigh(eng, wins, n, step):
            jh, k3, g, w = step
            if n >= 3:
                eng.wait_ge(sem("s_tr"), n - 2)
            ks = slice(g * TAPS + K3 * k3, g * TAPS + K3 * k3 + K3)
            rows = ty[:, w, jh, ks, :, :].rearrange("p k g r -> p (k g) r")
            colw = tx[:, jh, ks, :, :].rearrange("p k g r -> p (k g) r")
            shape = [P, K3 * BP, WROWS, W]
            return eng.tensor_tensor(smat[:, n % 3, :, :].rearrange("p u (r c) -> p u r c", c=W),
                                     rows.unsqueeze(3).broadcast_to(shape), colw.unsqueeze(2).broadcast_to(shape),
                                     ALU.mult)

        def sample_pool(pool, wins):
            nw = len(wins)
            for n, step in enumerate(sample_steps(wins)):
                if on_pool(n):
                    pool.wait_ge(sem("s_ty"), y_count(nw, step[0], nw - 1) + 1)
                    pool.wait_ge(sem("s_tx"), step[0] + 1)
                    weigh(nc.gpsimd, wins, n, step).then_inc(sem("s_wp"), 1)

        def y_count(nw, jh, w):
            return jh * nw + w + nw - 1

        def distance_y(jh, i, lo):
            shape = [P, BP, GK, WROWS]
            nc.vector.tensor_tensor(disty[:, i % 2, :, :, :],
                                    om[:, BP * jh:BP * jh + BP, 0:GK].unsqueeze(3).broadcast_to(shape),
                                    cst[:, lo:lo + WROWS].unsqueeze(1).unsqueeze(1).broadcast_to(shape),
                                    ALU.subtract).then_inc(sem("s_dy"), 1)

        def distance_x(dve, jh):
            if jh >= 2:
                dve.wait_ge(sem("s_tx"), jh - 1)
            shape = [P, BP, GK, W]
            nc.vector.tensor_tensor(distx[:, jh % 2, :, :, :],
                                    om[:, BP * jh:BP * jh + BP, GK:2 * GK].unsqueeze(3).broadcast_to(shape),
                                    const("grid").unsqueeze(1).unsqueeze(1).broadcast_to(shape),
                                    ALU.subtract).then_inc(sem("s_dx"), 1)

        def sigmoid_mask(dve, link, jh):
            dve.wait_ge(sem("c_me"), jh // NH + 1)
            m = msk[:, BP * jh:BP * jh + BP, :]
            link(nc.vector.tensor_scalar(m, m, 1.0, None, ALU.add))
            link(nc.vector.reciprocal(m, m))

        def row_weights(dve, nw, jh, w):
            i = y_count(nw, jh, w)
            dve.wait_ge(sem("s_ay"), i + 1)
            nc.vector.tensor_tensor(ty[:, w, jh, :, :, :].rearrange("p k g r -> p g k r"),
                                    disty[:, i % 2, :, :, :],
                                    msk[:, BP * jh:BP * jh + BP, :].unsqueeze(3).broadcast_to([P, BP, GK, WROWS]),
                                    ALU.mult).then_inc(sem("s_ty"), 1)

        def sample_dve(dve, wins, link):
            nw = len(wins)
            steps = sample_steps(wins)
            per_group = DG * nw
            per_jh = len(steps) // (J * NH)

            def keep(q):
                dve.wait_ge(sem("s_mm"), per_group * (q + 1))
                if q >= 2:
                    dve.wait_ge(sem("s_cv"), q - 1)
                nc.vector.tensor_copy(samp[:, q % 2, :, :], ps[:, 6, 0:K3 * P]).then_inc(sem("s_samp"), 1)

            for n, step in enumerate(steps):
                jh = step[0]
                at_ = n % per_jh
                if nw > 1 and at_ == 0:
                    if jh:
                        sigmoid_mask(dve, link, jh)
                    for w in range(nw):
                        distance_y(jh, y_count(nw, jh, w), CA["wide"][0] + ((jh % NH) * 2 + w) * WROWS)
                        row_weights(dve, nw, jh, w)
                    if jh:
                        distance_x(dve, jh)
                if not on_pool(n):
                    dve.wait_ge(sem("s_ty"), y_count(nw, jh, nw - 1) + 1)
                    dve.wait_ge(sem("s_tx"), jh + 1)
                    weigh(nc.vector, wins, n, step).then_inc(sem("s_wd"), 1)
                if nw == 1 and jh + 1 < J * NH:
                    if at_ == 1:
                        distance_y(jh + 1, y_count(nw, jh + 1, 0), CA["grid"][0])
                    elif at_ == 2:
                        distance_x(dve, jh + 1)
                    elif at_ == 3:
                        sigmoid_mask(dve, link, jh + 1)
                    elif at_ == 4:
                        row_weights(dve, nw, jh + 1, 0)
                if n >= 2 and (n - 1) % per_group == 0:
                    keep((n - 1) // per_group - 1)
            keep(len(steps) // per_group - 1)

        def tent_y(act, i):
            act.wait_ge(sem("s_dy"), i + 1)
            d = disty[:, i % 2, :, :, :]
            nc.scalar.activation(d, d, ACT.Abs).then_inc(sem("s_achain"), 1)
            act.wait_ge(sem("s_achain"), i + 1)
            nc.scalar.activation(d, d, ACT.Relu, bias=1.0, scale=-1.0).then_inc(sem("s_ay"), 1)

        def abs_x(act, jh):
            act.wait_ge(sem("s_dx"), jh + 1)
            d = distx[:, jh % 2, :, :, :]
            nc.scalar.activation(d, d, ACT.Abs).then_inc(sem("s_ax"), 1)

        def relu_x(act, jh):
            act.wait_ge(sem("s_ax"), jh + 1)
            nc.scalar.activation(tx[:, jh, :, :, :].rearrange("p k g r -> p g k r"), distx[:, jh % 2, :, :, :],
                                 ACT.Relu, bias=1.0, scale=-1.0).then_inc(sem("s_tx"), 1)

        def tent_x(act, jh):
            abs_x(act, jh)
            relu_x(act, jh)

        def sample_act(act, wins):
            nw = len(wins)
            steps = sample_steps(wins)
            per_jh = len(steps) // (J * NH)
            for n, step in enumerate(steps):
                jh = step[0]
                if nw > 1 and n % per_jh == 0:
                    for w in range(nw):
                        tent_y(act, y_count(nw, jh, w))
                    if jh:
                        tent_x(act, jh)
                act.wait_ge(sem("s_tr"), n + 1)
                if n >= 2:
                    act.wait_ge(sem("s_mm"), n - 1)
                nc.scalar.activation(smatT[:, n % 2, :, :, :].rearrange("p k g n -> p (k g n)"),
                                     ps[:, 3 * (n % 2):3 * (n % 2) + 3, :].rearrange("p b n -> p (b n)"),
                                     ACT.Copy).then_inc(sem("s_smt"), 1)
                if nw == 1 and jh + 1 < J * NH:
                    if n % per_jh == 1:
                        tent_y(act, y_count(nw, jh + 1, 0))
                    elif n % per_jh == 2:
                        abs_x(act, jh + 1)
                    elif n % per_jh == 3:
                        relu_x(act, jh + 1)

        def sample_pe(pe, wins):
            nw = len(wins)
            steps = sample_steps(wins)
            per_group = DG * nw
            pe.wait_ge(sem("c_xts"), J * DG)
            if nw > 1:
                for j in range(J):
                    for w in range(2):
                        last = nc.tensor.transpose(
                            ps[:, 2 + j, w * P:(w + 1) * P],
                            xwin[:, j, 2 + WROWS * w:2 + WROWS * w + WROWS, :].rearrange("p r c -> p (r c)"), ident)
                last.then_inc(sem("s_xt"), 1)
                pe.wait_ge(sem("s_xts"), J * DG)

            def transposes(n):
                if on_pool(n):
                    pe.wait_ge(sem("s_wp"), n // 4 + 1)
                else:
                    pe.wait_ge(sem("s_wd"), n - (n + 1) // 4 + 1)
                if n >= 2:
                    pe.wait_ge(sem("s_smt"), n - 1)
                for kk in range(K3):
                    for bp in range(BP):
                        last = nc.tensor.transpose(ps[:, 3 * (n % 2) + kk, bp * P:(bp + 1) * P],
                                                   smat[:, n % 3, kk * BP + bp, :], ident)
                last.then_inc(sem("s_tr"), 1)

            def products(n):
                jh, k3, g, w = steps[n]
                j, h = jh // NH, jh % NH
                pe.wait_ge(sem("s_smt"), n + 1)
                first, final = n % per_group == 0, n % per_group == per_group - 1
                if nw == 1:
                    for blk in range(2):
                        for bp in range(BP):
                            o = ps[C * bp:C * bp + C, 6, 0:K3 * P].rearrange("c (k n) -> c k n", k=K3)
                            last = nc.tensor.matmul(o[:, :, blk * BLK:(blk + 1) * BLK],
                                                    xt[:, j, g, 2 * h + blk, bp, :],
                                                    smatT[:, n % 2, :, bp, blk * BLK:(blk + 1) * BLK],
                                                    start=(first and blk == 0), stop=final, skip_group_check=True)
                else:
                    for bp in range(BP):
                        o = ps[C * bp:C * bp + C, 6, 0:K3 * P].rearrange("c (k n) -> c k n", k=K3)
                        last = nc.tensor.matmul(o, xt[:, j, g, w, bp, :], smatT[:, n % 2, :, bp, :],
                                                start=first, stop=final, skip_group_check=True)
                last.then_inc(sem("s_mm"), 1)

            def convolve(q):
                jh, k3 = q // (TAPS // K3), q % (TAPS // K3)
                pe.wait_ge(sem("s_samp"), q + 1)
                for kk in range(K3):
                    tap = K3 * k3 + kk
                    last = nc.tensor.matmul(ps[:, 7, jh * P:(jh + 1) * P], wc[:, tap, :, :].rearrange("p g o -> p (g o)"),
                                            samp[:, q % 2, kk, :], start=(tap == 0), stop=(tap == TAPS - 1))
                last.then_inc(sem("c_out" if q == len(steps) // per_group - 1 else "s_cv"), 1)

            keep_clock(2, 6)
            transposes(0)
            for n in range(len(steps)):
                if n + 1 < len(steps):
                    transposes(n + 1)
                if n and n % per_group == 0:
                    convolve(n // per_group - 1)
                products(n)
            convolve(len(steps) // per_group - 1)

        def windows(eng_copy, eng, name, nwin, done):
            eng.wait_ge(sem(name), 1)
            for j in range(J):
                for g in range(DG):
                    src_ = ps[:, 2 + j, 0:nwin * P].rearrange("p (w g c) -> p w g c", w=nwin, g=BP)
                    eng_copy(xt[:, j, g, 0:nwin, :, CG * g:CG * g + CG],
                             src_[:, :, :, CG * g:CG * g + CG]).then_inc(sem(done), 1)

        @block.sync
        def _(sp):
            sp.dma_start(x[:, :], dr("x")).then_inc(sem("ld_x"), 16)
            sp.dma_start(cst[:, :], dr("cst")).then_inc(sem("ld_cst"), 16)
            sp.dma_start(a4[:, :, :], every_pair(dr("L0_conv_w4"))).then_inc(sem("ld_a"), 16)
            sp.dma_start(acol[:, :], every_pair(dr("L0_conv_col"))).then_inc(sem("ld_a"), 16)
            sp.dma_start(bvrow[:, :], dr("L0_conv_bv").partition_broadcast(P)).then_inc(sem("ld_a"), 16)
            sp.dma_start(masks[:, 0, :], dr("L0_ffn_attn_mask")).then_inc(sem("ld_m"), 16)
            sp.dma_start(masks[:, 1, :], dr("L0_ffn_ffn_mask")).then_inc(sem("ld_m"), 16)
            sp.dma_start(codes[:, :], dr("codes")).then_inc(sem("ld_m"), 16)
            sp.wait_ge(sem("table_op"), 1)
            sp.dma_start(nexts[0:1, :].rearrange("a (o s) -> a o s", o=OPS), nexts_op[:, :]).then_inc(sem("table"), 16)
            sp.wait_ge(sem("table"), 16)
            recurrent(sp, SPBody())
            for j in range(J):
                half = slice(j * N, j * N + N)
                sp.wait_ge(sem("out_ready"), j + 1)
                sp.dma_start(out[:, half], fin[:, half]).then_inc(sem("stored"), 16)
            sp.wait_ge(sem("stored"), 16 * J)

        @block.gpsimd
        def _(pool):
            nc.gpsimd.memset(a4t[:, :, :], 0.0).then_inc(sem("zero_a4"), 1)
            nc.gpsimd.memset(q_sb[:, :, :], 0.0).then_inc(sem("zero_a4"), 1)
            nc.gpsimd.memset(r4[:, :, :], 0.0).then_inc(sem("zero_r4"), 1)
            nc.gpsimd.memset(w1z[:, :, :], 0.0).then_inc(sem("zero_r4"), 1)
            pool.dma_start(woff_n[:, :], dr("L1_conv_w_off").rearrange("o c a b -> o (c a b)")).then_inc(sem("ld_c"), 16)
            pool.dma_start(wc_n[:, :], dr("L1_conv_w").rearrange("o c a b -> o (c a b)")).then_inc(sem("ld_c"), 16)
            pool.dma_start(gw_n[:, :], dr("L1_ffn_gate_w")).then_inc(sem("ld_c"), 16)
            pool.dma_start(boff[:, :], dr("L1_conv_b_off").partition_broadcast(P)).then_inc(sem("ld_c"), 16)
            nc.gpsimd.memset(xwin[:, :, :, :], 0.0).then_inc(sem("zero_c"), 1)
            nc.gpsimd.memset(woff[:, :, :], 0.0).then_inc(sem("zero_c"), 1)
            nc.gpsimd.memset(wc[:, :, :, :], 0.0).then_inc(sem("zero_c"), 1)
            nc.gpsimd.memset(gwt[:, :, :, :, :], 0.0).then_inc(sem("zero_c"), 1)
            nc.gpsimd.memset(xs[:, :, :, :, :], 0.0).then_inc(sem("zero_c"), 1)
            nc.gpsimd.memset(xt[:, :, :, :, :, :], 0.0).then_inc(sem("zero_c"), 1)
            pool.wait_ge(sem("zero_c"), 6)
            nc.gpsimd.memset(pooled[C:C + 1, :, :], 1.0).then_inc(sem("zero_c"), 1)
            pool.dma_start(ccol[:, :], every_pair(dr("L1_conv_col"))).then_inc(sem("ld_d"), 16)
            pool.dma_start(gb[:, :], dr("L1_ffn_gate_b").rearrange("(e k) -> e k", k=1).unsqueeze(0).broadcast_to(
                [B, E, 1])).then_inc(sem("ld_d"), 16)
            pool.dma_start(ew1[:, :, :], dr("L1_ffn_weight1").rearrange("e d h -> d e h")).then_inc(sem("ld_d"), 16)
            w2_ = dr("L1_ffn_weight2").rearrange("e h o -> h e o")
            pool.dma_start(ew2[:, :, :], w2_[0:HID, :, :]).then_inc(sem("ld_d"), 16)
            pool.dma_start(eb2[:, :], dr("L1_ffn_weight2")[:, HID, :].unsqueeze(0).broadcast_to(
                [B, E, C])).then_inc(sem("ld_d"), 16)
            by_fit(pool, lambda wins: sample_pool(pool, wins))

        @block.scalar
        def _(act):
            nc.scalar.preload_act_table_set("natural_log_exp_and_others")
            act.wait_ge(sem("ld_cst"), 16)
            norm_act(act, 1, eps6)

            def weights_of_3(t):
                if t == BP:
                    act.wait_ge(sem("c_w"), 1)
                    act.wait_ge(sem("zero_c"), 7)
                if t >= BP:
                    g = t - BP
                    rows = slice(C * g, C * g + C)
                    if g < K:
                        taps = ps[0:C, 0, 0:TAPS * OCH].rearrange("c (i k o) -> c k i o", k=K, o=OCH)
                        nc.scalar.activation(woff[rows, :, 0:OCH], taps[:, g, :, :], ACT.Copy).then_inc(sem("c_wa"), 1)
                    nc.scalar.activation(wc[rows, :, g, :], ps[0:C, 1, 0:TAPS * C].rearrange("c (t o) -> c t o", o=C),
                                         ACT.Copy).then_inc(sem("c_wa"), 1)

            act.wait_ge(sem("a_bqs"), 1)
            att_act(act, "a_", bqs, acol[:, 2:3], weights_of_3)
            norm_act(act, 2, eps5)
            act.wait_ge(sem("table"), 16)
            recurrent(act, ACTBody())
            norm_act(act, 3, eps6)
            for j in range(J):
                act.wait_ge(sem("c_u"), j + 1)
                spread(lambda o, i: nc.scalar.activation(o, i, ACT.Copy), j, 0, "c_xsa")

            def channels_first(j):
                act.wait_ge(sem("c_omc"), j + 1)
                nc.scalar.activation(omc[:, j, :], ps[:, j, :], ACT.Copy).then_inc(sem("c_omcs"), 1)

            def exp_mask(j):
                act.wait_ge(sem("c_oms"), j + 1)
                i = slice(NH * BP * j, NH * BP * j + NH * BP)
                nc.scalar.activation(msk[:, i, :], om[:, i, 2 * GK:], ACT.Exp, scale=-1.0).then_inc(sem("c_me"), 1)

            channels_first(0)
            exp_mask(0)
            channels_first(1)
            tent_y(act, 0)
            tent_x(act, 0)
            exp_mask(1)
            windows(lambda o, i: nc.scalar.activation(o, i, ACT.Copy), act, "c_xt", NWIN, "c_xts")

            def run(wins):
                if len(wins) > 1:
                    windows(lambda o, i: nc.scalar.activation(o, i, ACT.Copy), act, "s_xt", 2, "s_xts")
                sample_act(act, wins)
            by_fit(act, run)
            act.wait_ge(sem("c_var"), 1)
            link = Chain(act, sem("a_main"))
            link(nc.scalar.activation(bn[:, 2:3], ps[:, 1, 0:1], ACT.Ln, bias=eps5))
            nc.scalar.activation(bn[:, 3:4], bn[:, 2:3], ACT.Exp, scale=-0.5).then_inc(sem("c_rs"), 1)
            norm_act(act, 4, eps5)
            act.wait_ge(sem("e_ut"), 1)
            nc.scalar.activation(ut[:, :, :].rearrange("p i c -> p (i c)"), ps[:, 1, :], ACT.Copy).then_inc(sem("e_uts"), 1)
            act.wait_ge(sem("e_max"), 1)
            nc.scalar.activation(pr[:, :], lg[:, :], ACT.Exp, bias=lnm[:, 0:1], accum_out=lnm[:, 1:2]).then_inc(sem("e_ex"), 1)
            act.wait_ge(sem("e_h"), 1)
            nc.scalar.activation(hid[:, :, :].rearrange("p e b -> p (e b)"), ps[:, 4, 0:E * B], ACT.Gelu).then_inc(sem("e_hid"), 1)

        @block.tensor
        def _(pe):
            pe.wait_ge(sem("zero_a4"), 1)
            keep_clock(3, 7, a4t[:, 0, :], a4t[:, 0:2, :].rearrange("p a n -> p (a n)"))
            pe.wait_ge(sem("ld_x"), 16)
            pe.wait_ge(sem("ld_cst"), 16)
            norm_pe(pe, 1, 7)
            pe.wait_ge(sem("a_u"), 1)
            pe.wait_ge(sem("a_w"), 1)

            def weights_of_3():
                pe.wait_ge(sem("ld_c"), 64)
                for tap in range(TAPS):
                    nc.tensor.transpose(ps[0:C, 0, tap * OCH:(tap + 1) * OCH], woff_n[:, tap::TAPS], ident[0:OCH, 0:OCH])
                for tap in range(TAPS):
                    nc.tensor.transpose(ps[0:C, 1, tap * C:(tap + 1) * C], wc_n[:, tap::TAPS], ident[0:C, 0:C])
                nc.tensor.transpose(ps[0:C, 1, TAPS * C:TAPS * C + E], gw_n[:, :], ident[0:E, 0:E]).then_inc(sem("c_w"), 1)

            att_pe(pe, "a_", [a4t[:, n, :] for n in range(4)], weights_of_3)
            pe.wait_ge(sem("a_x"), 1)
            norm_pe(pe, 2, 7)
            pe.wait_ge(sem("b_u"), 1)
            nc.tensor.matmul(ps[0:1, 5, 0:C], u[0:C, 0:1], ident[0:C, 0:C], start=True, stop=True).then_inc(sem("b_col"), 1)
            pe.wait_ge(sem("table"), 16)
            keep_clock(3, 7)
            recurrent(pe, PEBody())
            pe.wait_ge(sem("c_wd"), 1)

            def positions_first(j):
                pe.wait_ge(sem("c_omcs"), j + 1)
                for h in range(NH):
                    for i in range(2):
                        c0 = i * N + h * P
                        last = nc.tensor.transpose(ps[:, OMBANK[j], (2 * h + i) * P:(2 * h + i + 1) * P],
                                                   omc[:, j, c0:c0 + P], ident)
                last.then_inc(sem("c_om"), 1)

            keep_clock(5, 7)
            for j in range(J):
                pe.wait_ge(sem("c_xsa"), copies(j, 0))
                pe.wait_ge(sem("c_xsd"), copies(j, 1))
                for ki in range(K):
                    for s in range(2):
                        last = nc.tensor.matmul(ps[OPAD * s:OPAD * s + OPAD, j, :], woff[:, ki, :],
                                                xs[:, j, s::2, ki + 1:ki + 1 + H, :].rearrange("p g r c -> p g (r c)"),
                                                start=(ki == 0), stop=(ki == K - 1))
                    if j == 1 and ki == 0:
                        positions_first(0)
                last.then_inc(sem("c_omc"), 1)
            pe.wait_ge(sem("c_u"), J)
            for j in range(J):
                for w in range(NWIN):
                    last = nc.tensor.transpose(ps[:, 2 + j, w * P:(w + 1) * P],
                                               xwin[:, j, 4 * w:4 * w + WROWS, :].rearrange("p r c -> p (r c)"), ident)
            last.then_inc(sem("c_xt"), 1)
            positions_first(1)
            keep_clock(3, 6)
            pe.wait_ge(sem("c_fitp"), 1)
            nc.tensor.transpose(ps[0:1, 5, 0:P], fitm[:, 0:1], ident).then_inc(sem("c_fitt"), 1)
            keep_clock(5, 6)
            by_fit(pe, lambda wins: sample_pe(pe, wins))
            keep_clock(4, 4)
            pe.wait_ge(sem("c_agg"), 1)
            nc.tensor.matmul(ps[:, 0, 0:1], fold, agg[:, 0:1], start=True, stop=True).then_inc(sem("c_mu"), 1)
            pe.wait_ge(sem("c_dev"), 1)
            nc.tensor.matmul(ps[:, 1, 0:1], fold, bn[:, 1:2], start=True, stop=True).then_inc(sem("c_var"), 1)
            keep_clock(5, 4)
            pe.wait_ge(sem("c_xn"), 1)
            norm_pe(pe, 4, 4)
            pe.wait_ge(sem("e_u"), 1)
            for j in range(J):
                last = nc.tensor.matmul(ps[:, 0, 0:N], gwt[:, j, :, :, :].rearrange("p g j e -> p (g j e)"),
                                        u[:, j * N:(j + 1) * N], start=(j == 0), stop=(j == J - 1))
            last.then_inc(sem("e_lg"), 1)
            for i in range(J * NH):
                last = nc.tensor.transpose(ps[:, 1, i * P:(i + 1) * P], u[:, i * P:(i + 1) * P], ident)
            last.then_inc(sem("e_ut"), 1)
            keep_clock(6, 4)
            pe.wait_ge(sem("e_pm"), 1)
            for h in range(NH):
                last = nc.tensor.transpose(ps[:, 2, h * P:(h + 1) * P], pm[:, h * P:(h + 1) * P], ident)
            last.then_inc(sem("e_pmt"), 1)
            keep_clock(1, 4)
            pe.wait_ge(sem("e_uts"), 1)
            pe.wait_ge(sem("e_pmts"), 1)
            for j in range(J):
                for h in range(NH):
                    last = nc.tensor.matmul(ps[:, 3, j * P:(j + 1) * P], ut[:, j * NH + h, :], pmT[:, h, :],
                                            start=(h == 0), stop=(h == NH - 1))
            last.then_inc(sem("e_pool"), 1)
            pe.wait_ge(sem("ld_d"), 16 * 5)
            pe.wait_ge(sem("e_pools"), BP)
            for e in range(E):
                last = nc.tensor.matmul(ps[:, 4, e * B:(e + 1) * B], ew1[:, e, :], pooled[:, e, :], start=True, stop=True)
            last.then_inc(sem("e_h"), 1)
            pe.wait_ge(sem("e_hid"), 1)
            for e in range(E):
                last = nc.tensor.matmul(ps[0:C, 5, e * B:(e + 1) * B], ew2[:, e, :], hid[:, e, :], start=True, stop=True)
            last.then_inc(sem("e_o"), 1)
            pe.wait_ge(sem("e_os"), 1)
            nc.tensor.transpose(ps[:, 6, 0:C], eo[:, :, :].rearrange("o b e -> o (b e)"), ident[0:C, 0:C]).then_inc(sem("e_ot"), 1)
            pe.wait_ge(sem("e_ol"), 1)
            for j in range(J):
                last = nc.tensor.matmul(ps[:, 7 - j, 0:N], eol[:, j, :, :].rearrange("p g o -> p (g o)"),
                                        pm[:, :], start=True, stop=True)
                last.then_inc(sem("e_y"), 1)

        @block.vector
        def _(dve):
            dve.wait_ge(sem("ld_x"), 16)
            link = Chain(dve, sem("d_main"))

            def weights_of_1():
                dve.wait_ge(sem("ld_a"), 16 * 3)
                nc.vector.tensor_scalar(bqs[:, :], acol[:, 1:2], QSCALE, None, ALU.mult).then_inc(sem("a_bqs"), 1)
                link(nc.vector.transpose(a4s[:, :, :].rearrange("p a b -> p (a b)"),
                                         a4[:, :, :].rearrange("p a b -> p (a b)")))
                dve.wait_ge(sem("zero_a4"), 2)
                for g in range(BP):
                    rows = slice(C * g, C * g + C)
                    last = nc.vector.tensor_copy(a4t[rows, :, rows], a4s[rows, :, :])
                last.then_inc(sem("a_w"), 1)

            deviations(dve, 1)
            weights_of_1()
            dve.wait_ge(sem("norm_rstd"), 1)
            nc.vector.scalar_tensor_tensor(out=u[:, :], in0=xc[:, :], scalar=acol[:, 0:1], in1=rstd[:, :],
                                           op0=ALU.mult, op1=ALU.mult).then_inc(sem("a_u"), 1)
            att_dve(dve, "a_", acol[:, 1:2], bvrow[:, :], table_step)
            nc.vector.scalar_tensor_tensor(out=x[:, :], in0=ps[:, 0, :], scalar=acol[:, 3:4], in1=x[:, :],
                                           op0=ALU.add, op1=ALU.add).then_inc(sem("a_x"), 1)
            dve.wait_ge(sem("c_w"), 1)
            for g in range(BP):
                for j in range(J):
                    last = nc.vector.tensor_copy(gwt[C * g:C * g + C, j, g, j, :], ps[0:C, 1, TAPS * C:TAPS * C + E])
            last.then_inc(sem("c_wd"), 1)
            dve.wait_ge(sem("a_x"), 1)
            norm_dve(dve, 2)
            for cols in (FIRST, REST):
                nc.vector.tensor_tensor(u[:, cols], xc[:, cols], rstd[:, cols], ALU.mult).then_inc(sem("b_u"), 1)
            dve.wait_ge(sem("b_u"), 2)
            dve.wait_ge(sem("b_col"), 1)
            pick_op(dve, "d_pick")
            dve.sem_inc(sem("clear_pe"), 1)
            dve.sem_inc(sem("go_act"), 1)
            dve.wait_ge(sem("table"), 16)
            recurrent(dve, DVEBody())
            dve.wait_ge(sem("b_x"), 1)
            dve.wait_ge(sem("zero_c"), 7)
            dve.wait_ge(sem("ld_c"), 64)
            link(nc.vector.tensor_tensor(offb[:, :], boff[:, :], const("base"), ALU.add))
            dve.wait_ge(sem("norm_rstd"), 3)
            for j in range(J):
                half = slice(j * N, j * N + N)
                nc.vector.scalar_tensor_tensor(out=xwin[:, j, 2:2 + H, :],
                                               in0=xc[:, half].rearrange("p (r c) -> p r c", r=H), scalar=0.0,
                                               in1=rstd[:, half].rearrange("p (r c) -> p r c", r=H),
                                               op0=ALU.max, op1=ALU.mult).then_inc(sem("c_u"), 1)
                dve.wait_ge(sem("c_u"), j + 1)
                spread(nc.vector.tensor_copy, j, 1, "c_xsd")

            def offsets(j):
                dve.wait_ge(sem("c_om"), j + 1)
                nb = NH * BP
                nc.vector.tensor_tensor(om[:, nb * j:nb * j + nb, :],
                                        ps[:, OMBANK[j], :].rearrange("p (i o) -> p i o", o=OPAD)[:, :, 0:OCH],
                                        offb[:, :].unsqueeze(1).broadcast_to([P, nb, OCH]),
                                        ALU.add).then_inc(sem("c_oms"), 1)
                dve.wait_ge(sem("c_oms"), j + 1)

            offsets(0)
            distance_y(0, 0, CA["grid"][0])
            distance_x(dve, 0)
            sigmoid_mask(dve, link, 0)
            offsets(1)
            mid = (WROWS - 1) / 2
            link(nc.vector.tensor_scalar(fit[:, :, :], om[:, :, 0:GK], -mid, None, ALU.add))
            nc.vector.tensor_reduce(fitm[:, 0:1], fit[:, :, :], AX.XY, ALU.max,
                                    apply_absolute_value=True).then_inc(sem("c_fitp"), 1)
            row_weights(dve, 1, 0, 0)
            dve.wait_ge(sem("c_fitt"), 1)
            link(nc.vector.tensor_reduce(fitm[0:1, 1:2], ps[0:1, 5, 0:P], AX.X, ALU.max))
            nc.vector.tensor_scalar(fiti[:, :], fitm[0:1, 1:2], mid, None, ALU.is_le).then_inc(sem("c_fit"), 1)
            by_fit(dve, lambda wins: sample_dve(dve, wins, Chain(dve, sem("s_dchain"))))
            dve.wait_ge(sem("ld_d"), 16 * 5)
            dve.wait_ge(sem("c_out"), 1)
            link(nc.vector.tensor_scalar(y[:, :], ps[:, 7, :], ccol[:, 0:1], None, ALU.add))
            link(nc.vector.bn_stats(stats[:, :], y[:, :]))
            nc.vector.bn_aggr(agg[:, :], stats[:, :]).then_inc(sem("c_agg"), 1)
            dve.wait_ge(sem("c_mu"), 1)
            link(nc.vector.tensor_tensor(bn[:, 0:1], agg[:, 0:1], ps[:, 0, 0:1], ALU.subtract))
            nc.vector.scalar_tensor_tensor(out=bn[:, 1:2], in0=bn[:, 0:1], scalar=bn[:, 0:1], in1=agg[:, 1:2],
                                           op0=ALU.mult, op1=ALU.add).then_inc(sem("c_dev"), 1)
            link(nc.vector.tensor_copy(bn[:, 5:6], ps[:, 0, 0:1]))
            dve.wait_ge(sem("c_rs"), 1)
            link(nc.vector.tensor_tensor(bn[:, 4:5], bn[:, 3:4], ccol[:, 1:2], ALU.mult))
            link(nc.vector.tensor_scalar(y[:, :], y[:, :], bn[:, 5:6], bn[:, 4:5], ALU.subtract, ALU.mult))
            nc.vector.scalar_tensor_tensor(out=x[:, :], in0=y[:, :], scalar=ccol[:, 2:3], in1=x[:, :],
                                           op0=ALU.add, op1=ALU.add).then_inc(sem("c_xn"), 1)
            dve.wait_ge(sem("c_xn"), 1)
            norm_dve(dve, 4)
            nc.vector.tensor_tensor(u[:, :], xc[:, :], rstd[:, :], ALU.mult).then_inc(sem("e_u"), 1)
            dve.wait_ge(sem("e_lg"), 1)
            link(nc.vector.tensor_scalar(lg[:, :], ps[:, 0, 0:N], gb[:, 0:1], None, ALU.add))
            link(nc.vector.reduce_max(lnm[:, 2:3], lg[:, :], AX.X))
            nc.vector.tensor_scalar(lnm[:, 0:1], lnm[:, 2:3], -1.0, None, ALU.mult).then_inc(sem("e_max"), 1)
            dve.wait_ge(sem("e_ex"), 1)
            link(nc.vector.reciprocal(lnm[:, 3:4], lnm[:, 1:2]))
            link(nc.vector.tensor_scalar(pr[:, :], pr[:, :], lnm[:, 3:4], None, ALU.mult))
            link(nc.vector.max(ptop[:, :], pr[:, :]))
            link(nc.vector.match_replace(rest[:, :], ptop[:, :], pr[:, :], -1.0))
            nc.vector.scalar_tensor_tensor(out=pm[:, :], in0=rest[:, :], scalar=0.0, in1=pr[:, :],
                                           op0=ALU.is_lt, op1=ALU.mult).then_inc(sem("e_pm"), 1)
            dve.wait_ge(sem("e_pmt"), 1)
            nc.vector.tensor_copy(pmT[:, :, :].rearrange("p h n -> p (h n)"), ps[:, 2, 0:NH * P]).then_inc(sem("e_pmts"), 1)
            dve.wait_ge(sem("e_pool"), 1)
            for g in range(BP):
                span = J * (P + E)
                own = ps[C * g:C * g + C, 3, J * E * g:J * E * g + span].rearrange("c (j n) -> c j n", j=J)[:, :, 0:E]
                nc.vector.tensor_copy(pooled[0:C, :, J * g:J * g + J].rearrange("c e j -> c j e"),
                                      own).then_inc(sem("e_pools"), 1)
            dve.wait_ge(sem("e_o"), 1)
            nc.vector.tensor_copy(eo[:, :, :], ps[0:C, 5, 0:E * B].rearrange("o (e b) -> o b e", b=B)).then_inc(sem("e_os"), 1)
            dve.wait_ge(sem("e_ot"), 1)
            link(nc.vector.tensor_tensor(eoT[:, :], ps[:, 6, 0:C], eb2[:, :], ALU.add))
            nc.vector.tensor_tensor(eol[:, :, :, :].rearrange("p j g o -> p (j g) o"),
                                    eoT[:, :].unsqueeze(1).broadcast_to([P, J * BP, C]),
                                    const("own").unsqueeze(2).broadcast_to([P, J * BP, C]),
                                    ALU.mult).then_inc(sem("e_ol"), 1)
            for j in range(J):
                half = slice(j * N, j * N + N)
                dve.wait_ge(sem("e_y"), j + 1)
                nc.vector.tensor_tensor(fin[:, half], ps[:, 7 - j, 0:N], x[:, half], ALU.add).then_inc(sem("out_ready"), 1)


def pair_major(v):
    return np.asarray(v).reshape(BP, J, C, N).transpose(0, 2, 1, 3).reshape(P, F)


def kernel(**inputs):
    import concourse.bacc as _bacc
    from concourse.bass_utils import run_bass_kernel_spmd as _run

    nc = _bacc.Bacc("TRN2", target_bir_lowering=False, num_devices=1)
    inputs = dict(inputs)
    cst, _ = constants()
    arrays, aps = {}, {}
    inputs["cst"], inputs["codes"] = cst, step_codes()
    inputs["x"] = pair_major(inputs["x"])
    inputs["L0_conv_w4"] = np.stack([inputs.pop("L0_conv_" + n) for n in ("wq", "wk", "wv", "wo")], 1)
    inputs["L0_conv_col"] = np.stack([inputs.pop("L0_conv_" + n) for n in ("freq_weights", "bq", "bk", "bo")], 1)
    inputs["L1_conv_col"] = np.stack([inputs.pop("L1_conv_" + n) for n in ("b", "gamma", "beta")], 1)
    inputs["L0_ffn_w4"] = np.concatenate([inputs.pop("L0_ffn_" + n) for n in ("wq", "wk", "wv", "wo")], -1)
    b1 = np.asarray(inputs.pop("L0_ffn_ffn_b1"))
    inputs["L0_ffn_ffn_w2b1"] = np.concatenate([inputs.pop("L0_ffn_ffn_w2"), b1[..., None]], -1)
    for name, v in inputs.items():
        v = np.ascontiguousarray(v)
        if v.dtype == np.bool_:
            v = np.ascontiguousarray(v.T).astype(np.int32)
        elif name in ("L0_ffn_w4", "L0_ffn_ffn_w1", "L0_ffn_ffn_w2b1", "L0_ffn_ffn_b2"):
            v = v.reshape((-1,) + v.shape[2:])
        arrays[f"in_{name}"] = v
        aps[name] = nc.dram_tensor(f"in_{name}", v.shape, mybir.dt.from_np(v.dtype), kind="ExternalInput").ap()
    out = nc.dram_tensor("out", (P, F), f32, kind="ExternalOutput").ap()
    metaformer_kernel(nc, aps, out)
    res = _run(nc, [arrays], core_ids=[0]).results[0]["out"]
    return np.ascontiguousarray(res.reshape(BP, C, J, H, W).transpose(0, 2, 1, 3, 4)).reshape(B, C, H, W)
```
